# Optimizing a Trainium2 kernel written in Bass

```python
import numpy as np
import jax
import jax.numpy as jnp

def _softmax(x, axis=-1):
    return jax.nn.softmax(x, axis=axis)

def _gelu(x):
    return jax.nn.gelu(x, approximate=True)

def _silu(x):
    return jax.nn.silu(x)

def _sigmoid(x):
    return jax.nn.sigmoid(x)

def _layernorm(x, axis=-1, eps=1e-05):
    m = jnp.mean(x, axis=axis, keepdims=True)
    v = jnp.var(x, axis=axis, keepdims=True)
    return (x - m) / jnp.sqrt(v + eps)

def _scatter_add(tgt, idx, src, axis=0):
    return tgt.at[idx].add(src)

def _segment_sum(src, seg, n):
    return jax.ops.segment_sum(src, seg, n)
kernel_name = 'mk_adaln_d2_jaxref_r8_cfdf11'

def setup_inputs(seed: int=0):
    np.random.seed(seed)
    _w = jnp.asarray

    def _L0_attn_setup():
        import jax, jax.numpy as jnp
        import numpy as np
        EPS = 1e-06
        DECAY = 0.9
        THR = 0.5
        SBETA = 10.0
        KW = 4

        def _rms(x, w):
            return x * jax.lax.rsqrt(jnp.mean(x * x, axis=-1, keepdims=True) + EPS) * w
        B, T, D, H, dk, dv, r, dff = (2, 256, 128, 8, 64, 64, 64, 512)
        keys = iter(jax.random.split(jax.random.key(seed), 24))

        def g(shape, s=0.02):
            return jax.random.normal(next(keys), shape, jnp.float32) * s
        return {'x': jax.random.normal(next(keys), (B, T, D), jnp.float32), 'norm_in_w': jnp.ones((D,), jnp.float32), 'conv_w': g((D, 1, KW), 0.3), 'conv_b': jnp.zeros((D,), jnp.float32), 'Wq': g((D, H * dk)), 'Wk': g((D, H * dk)), 'Wv': g((D, H * dv)), 'Wo': g((H * dv, D)), 'Wspike': g((D, H * dk), 0.1), 'Wau': g((D, r)), 'bau': jnp.zeros((r,), jnp.float32), 'Wad': g((r, H * dk)), 'bad': jnp.zeros((H * dk,), jnp.float32), 'alpha_spike': jnp.zeros((1, H, dk), jnp.float32), 'Wbeta': g((D, H)), 'bbeta': jnp.zeros((H,), jnp.float32), 'beta_spike': jnp.zeros((1, H, dk), jnp.float32), 'head_norm_w': jnp.ones((H, dv), jnp.float32), 'Wu1': g((D, r)), 'bu1': jnp.zeros((r,), jnp.float32), 'Wu2': g((r, D)), 'bu2': jnp.zeros((D,), jnp.float32), 'ff_norm_w': jnp.ones((D,), jnp.float32), 'Wff1': g((D, dff)), 'Wff3': g((D, dff)), 'Wff2': g((dff, D))}
    _L0_attn_in = _L0_attn_setup()

    def _L0_ffn_setup():
        import jax, jax.numpy as jnp
        import numpy as np
        N_EMBD = 128
        N_STATE = 512
        key = jax.random.key(seed)
        k_x, k_w1, k_b1, k_w2, k_b2 = jax.random.split(key, 5)
        x = jax.random.normal(k_x, (4, 256, N_EMBD), dtype=jnp.float32)
        w1 = jax.random.normal(k_w1, (N_EMBD, N_STATE), dtype=jnp.float32) * (1.0 / np.sqrt(N_EMBD))
        b1 = jax.random.normal(k_b1, (N_STATE,), dtype=jnp.float32) * 0.02
        w2 = jax.random.normal(k_w2, (N_STATE, N_EMBD), dtype=jnp.float32) * (1.0 / np.sqrt(N_STATE))
        b2 = jax.random.normal(k_b2, (N_EMBD,), dtype=jnp.float32) * 0.02
        return {'x': x, 'w1': w1, 'b1': b1, 'w2': w2, 'b2': b2}
    _L0_ffn_in = _L0_ffn_setup()
    _L0_c = _w((lambda *s: np.random.randn(*s).astype(np.float32) * 0.05)(1, 128))
    _L0_wmod = _w((lambda *s: np.random.randn(*s).astype(np.float32) * 0.05)(128, 6 * 128) * 128 ** (-0.5))

    def _L1_attn_setup():
        import jax, jax.numpy as jnp
        import numpy as np
        NUM_HEADS = 16
        WINDOW = 32

        def _sliding_window_attn(x, wq, wk, wv, wo):
            B, S, D = x.shape
            H, W = (NUM_HEADS, WINDOW)
            Dh = D // H
            nb = S // W

            def proj(w):
                y = (x @ w.T).reshape(B, nb, W, H, Dh)
                return y.transpose(0, 3, 1, 2, 4)
            q = proj(wq)
            k = proj(wk)
            v = proj(wv)
            zpad = jnp.zeros((B, H, 1, W, Dh), dtype=x.dtype)
            kpad = jnp.concatenate([zpad, k], axis=2)
            vpad = jnp.concatenate([zpad, v], axis=2)
            k2 = jnp.concatenate([kpad[:, :, :-1], kpad[:, :, 1:]], axis=3)
            v2 = jnp.concatenate([vpad[:, :, :-1], vpad[:, :, 1:]], axis=3)
            scores = jnp.einsum('bhjqd,bhjkd->bhjqk', q, k2) / jnp.sqrt(jnp.asarray(Dh, dtype=x.dtype))
            qi = jnp.arange(W)[:, None]
            ki = jnp.arange(2 * W)[None, :]
            band = (ki >= qi + 1) & (ki <= qi + W)
            kpos_ok = (jnp.arange(nb)[:, None, None] - 1) * W + ki[None] >= 0
            mask = band[None] & kpos_ok
            neg = jnp.finfo(scores.dtype).min
            scores = jnp.where(mask[None, None], scores, neg)
            attn = jax.nn.softmax(scores, axis=-1)
            out = jnp.einsum('bhjqk,bhjkd->bhjqd', attn, v2)
            out = out.transpose(0, 2, 3, 1, 4).reshape(B, S, D)
            return out @ wo.T
        key = jax.random.key(seed)
        k1, k2, k3, k4, k5 = jax.random.split(key, 5)
        B, S, D = (2, 512, 128)
        scale = 0.02
        return {'x': jax.random.normal(k1, (B, S, D), dtype=jnp.float32), 'wq': jax.random.normal(k2, (D, D), dtype=jnp.float32) * scale, 'wk': jax.random.normal(k3, (D, D), dtype=jnp.float32) * scale, 'wv': jax.random.normal(k4, (D, D), dtype=jnp.float32) * scale, 'wo': jax.random.normal(k5, (D, D), dtype=jnp.float32) * scale}
    _L1_attn_in = _L1_attn_setup()

    def _L1_ffn_setup():
        import jax, jax.numpy as jnp
        import numpy as np
        B, S, H, F, G = (8, 256, 128, 512, 128)
        EPS = 1e-05

        def _dequant(q, scales, g):
            K, N = q.shape
            w = (q.astype(jnp.float32) - 128.0).reshape(K // g, g, N) * scales[:, None, :]
            return w.reshape(K, N)
        key = jax.random.key(seed)
        ks = jax.random.split(key, 8)
        x = jax.random.normal(ks[0], (B, S, H), dtype=jnp.float32)
        ln_gamma = jnp.ones((H,), jnp.float32)
        ln_beta = jnp.zeros((H,), jnp.float32)
        fc1_q = jax.random.randint(ks[1], (H, F), 0, 32, dtype=jnp.int32)
        fc2_q = jax.random.randint(ks[2], (F, H), 0, 32, dtype=jnp.int32)
        fc1_scales = jax.random.uniform(ks[3], (H // G, F), jnp.float32) * 0.02 + 0.001
        fc2_scales = jax.random.uniform(ks[4], (F // G, H), jnp.float32) * 0.02 + 0.001
        fc1_bias = jax.random.normal(ks[5], (F,), jnp.float32) * 0.02
        fc2_bias = jax.random.normal(ks[6], (H,), jnp.float32) * 0.02
        return {'x': x, 'ln_gamma': ln_gamma, 'ln_beta': ln_beta, 'fc1_q': fc1_q, 'fc1_scales': fc1_scales, 'fc1_bias': fc1_bias, 'fc2_q': fc2_q, 'fc2_scales': fc2_scales, 'fc2_bias': fc2_bias}
    _L1_ffn_in = _L1_ffn_setup()
    _L1_c = _w((lambda *s: np.random.randn(*s).astype(np.float32) * 0.05)(1, 128))
    _L1_wmod = _w((lambda *s: np.random.randn(*s).astype(np.float32) * 0.05)(128, 6 * 128) * 128 ** (-0.5))
    _d = {'L0_attn_x': _L0_attn_in['x'], 'L0_attn_norm_in_w': _L0_attn_in['norm_in_w'], 'L0_attn_conv_w': _L0_attn_in['conv_w'], 'L0_attn_conv_b': _L0_attn_in['conv_b'], 'L0_attn_Wq': _L0_attn_in['Wq'], 'L0_attn_Wk': _L0_attn_in['Wk'], 'L0_attn_Wv': _L0_attn_in['Wv'], 'L0_attn_Wo': _L0_attn_in['Wo'], 'L0_attn_Wspike': _L0_attn_in['Wspike'], 'L0_attn_Wau': _L0_attn_in['Wau'], 'L0_attn_bau': _L0_attn_in['bau'], 'L0_attn_Wad': _L0_attn_in['Wad'], 'L0_attn_bad': _L0_attn_in['bad'], 'L0_attn_alpha_spike': _L0_attn_in['alpha_spike'], 'L0_attn_Wbeta': _L0_attn_in['Wbeta'], 'L0_attn_bbeta': _L0_attn_in['bbeta'], 'L0_attn_beta_spike': _L0_attn_in['beta_spike'], 'L0_attn_head_norm_w': _L0_attn_in['head_norm_w'], 'L0_attn_Wu1': _L0_attn_in['Wu1'], 'L0_attn_bu1': _L0_attn_in['bu1'], 'L0_attn_Wu2': _L0_attn_in['Wu2'], 'L0_attn_bu2': _L0_attn_in['bu2'], 'L0_attn_ff_norm_w': _L0_attn_in['ff_norm_w'], 'L0_attn_Wff1': _L0_attn_in['Wff1'], 'L0_attn_Wff3': _L0_attn_in['Wff3'], 'L0_attn_Wff2': _L0_attn_in['Wff2'], 'L0_ffn_w1': _L0_ffn_in['w1'], 'L0_ffn_b1': _L0_ffn_in['b1'], 'L0_ffn_w2': _L0_ffn_in['w2'], 'L0_ffn_b2': _L0_ffn_in['b2'], 'L0_c': _L0_c, 'L0_wmod': _L0_wmod, 'L1_attn_wq': _L1_attn_in['wq'], 'L1_attn_wk': _L1_attn_in['wk'], 'L1_attn_wv': _L1_attn_in['wv'], 'L1_attn_wo': _L1_attn_in['wo'], 'L1_ffn_ln_gamma': _L1_ffn_in['ln_gamma'], 'L1_ffn_ln_beta': _L1_ffn_in['ln_beta'], 'L1_ffn_fc1_q': _L1_ffn_in['fc1_q'], 'L1_ffn_fc1_scales': _L1_ffn_in['fc1_scales'], 'L1_ffn_fc1_bias': _L1_ffn_in['fc1_bias'], 'L1_ffn_fc2_q': _L1_ffn_in['fc2_q'], 'L1_ffn_fc2_scales': _L1_ffn_in['fc2_scales'], 'L1_ffn_fc2_bias': _L1_ffn_in['fc2_bias'], 'L1_c': _L1_c, 'L1_wmod': _L1_wmod}
    _x0 = _d['L0_attn_x']
    _d['L0_attn_x'] = jax.random.normal(jax.random.fold_in(jax.random.key(seed), 1), (1, 2048, 128), dtype=_x0.dtype)
    del _x0
    return _d

def reference(L0_attn_x, L0_attn_norm_in_w, L0_attn_conv_w, L0_attn_conv_b, L0_attn_Wq, L0_attn_Wk, L0_attn_Wv, L0_attn_Wo, L0_attn_Wspike, L0_attn_Wau, L0_attn_bau, L0_attn_Wad, L0_attn_bad, L0_attn_alpha_spike, L0_attn_Wbeta, L0_attn_bbeta, L0_attn_beta_spike, L0_attn_head_norm_w, L0_attn_Wu1, L0_attn_bu1, L0_attn_Wu2, L0_attn_bu2, L0_attn_ff_norm_w, L0_attn_Wff1, L0_attn_Wff3, L0_attn_Wff2, L0_ffn_w1, L0_ffn_b1, L0_ffn_w2, L0_ffn_b2, L0_c, L0_wmod, L1_attn_wq, L1_attn_wk, L1_attn_wv, L1_attn_wo, L1_ffn_ln_gamma, L1_ffn_ln_beta, L1_ffn_fc1_q, L1_ffn_fc1_scales, L1_ffn_fc1_bias, L1_ffn_fc2_q, L1_ffn_fc2_scales, L1_ffn_fc2_bias, L1_c, L1_wmod):

    def _L0_attn_ref(x, norm_in_w, conv_w, conv_b, Wq, Wk, Wv, Wo, Wspike, Wau, bau, Wad, bad, alpha_spike, Wbeta, bbeta, beta_spike, head_norm_w, Wu1, bu1, Wu2, bu2, ff_norm_w, Wff1, Wff3, Wff2):
        import jax, jax.numpy as jnp
        import numpy as np
        EPS = 1e-06
        DECAY = 0.9
        THR = 0.5
        SBETA = 10.0
        KW = 4

        def _rms(x, w):
            return x * jax.lax.rsqrt(jnp.mean(x * x, axis=-1, keepdims=True) + EPS) * w
        B, T, D = x.shape
        H, dk = (alpha_spike.shape[1], alpha_spike.shape[2])
        dv = head_norm_w.shape[1]
        h = _rms(x, norm_in_w)
        hc = jnp.transpose(h, (0, 2, 1))
        conv = jax.lax.conv_general_dilated(hc, conv_w, window_strides=(1,), padding=[(KW - 1, 0)], dimension_numbers=('NCH', 'OIH', 'NCH'), feature_group_count=D)
        conv = conv + conv_b[None, :, None]
        h = jax.nn.silu(jnp.transpose(conv, (0, 2, 1)))

        def heads(z, d):
            return z.reshape(B, T, H, d)
        q = heads(h @ Wq, dk)
        k = heads(h @ Wk, dk)
        v = heads(h @ Wv, dv)
        q = q / (jnp.linalg.norm(q, axis=-1, keepdims=True) + 1e-06)
        k = k / (jnp.linalg.norm(k, axis=-1, keepdims=True) + 1e-06)
        drive = heads(h @ Wspike, dk)
        alpha_base = heads(jax.nn.silu(h @ Wau + bau) @ Wad + bad, dk)
        beta_base = h @ Wbeta + bbeta
        asp = alpha_spike[0]
        bsp = beta_spike[0]

        def step(carry, ins):
            s, mem = carry
            qt, kt, vt, dt, at, bt = ins
            mem = DECAY * mem + dt
            sg = jax.nn.sigmoid(SBETA * (mem - THR))
            hard = (mem > THR).astype(mem.dtype)
            spike = sg + jax.lax.stop_gradient(hard - sg)
            mem = mem - spike * THR
            alpha = jax.nn.sigmoid(at + asp * spike)
            beta = jax.nn.sigmoid(bt[..., None] + jnp.sum(spike * bsp, -1, keepdims=True))
            active = (jnp.sum(jnp.abs(spike), -1, keepdims=True) > 0).astype(qt.dtype)
            alpha = jnp.where(active > 0, alpha, jnp.ones_like(alpha))
            beta = beta * active
            s = s * alpha[..., None]
            pred = jnp.einsum('bhk,bhkv->bhv', kt, s)
            s = s + (beta * kt)[..., None] * (vt - pred)[:, :, None, :]
            out = jnp.einsum('bhk,bhkv->bhv', qt, s)
            return ((s, mem), out)
        s0 = jnp.zeros((B, H, dk, dv), x.dtype)
        m0 = jnp.zeros((B, H, dk), x.dtype)
        xs = (jnp.moveaxis(q, 1, 0), jnp.moveaxis(k, 1, 0), jnp.moveaxis(v, 1, 0), jnp.moveaxis(drive, 1, 0), jnp.moveaxis(alpha_base, 1, 0), jnp.moveaxis(beta_base, 1, 0))
        _, y = jax.lax.scan(step, (s0, m0), xs)
        y = jnp.moveaxis(y, 0, 1)
        y = y * jax.lax.rsqrt(jnp.mean(y * y, axis=-1, keepdims=True) + EPS) * head_norm_w
        y = y.reshape(B, T, H * dv)
        gate = jax.nn.sigmoid(jax.nn.silu(x @ Wu1 + bu1) @ Wu2 + bu2)
        y = x + y @ Wo * gate
        z = _rms(y, ff_norm_w)
        y = y + jax.nn.silu(z @ Wff1) * (z @ Wff3) @ Wff2
        return y

    def _L0_ffn_ref(x, w1, b1, w2, b2):
        import jax, jax.numpy as jnp
        import numpy as np
        N_EMBD = 128
        N_STATE = 512
        h = jax.nn.gelu(jnp.einsum('bse,eh->bsh', x, w1) + b1, approximate=False)
        return jnp.einsum('bsh,he->bse', h, w2) + b2

    def _L1_attn_ref(x, wq, wk, wv, wo):
        import jax, jax.numpy as jnp
        import numpy as np
        NUM_HEADS = 16
        WINDOW = 32

        def _sliding_window_attn(x, wq, wk, wv, wo):
            B, S, D = x.shape
            H, W = (NUM_HEADS, WINDOW)
            Dh = D // H
            nb = S // W

            def proj(w):
                y = (x @ w.T).reshape(B, nb, W, H, Dh)
                return y.transpose(0, 3, 1, 2, 4)
            q = proj(wq)
            k = proj(wk)
            v = proj(wv)
            zpad = jnp.zeros((B, H, 1, W, Dh), dtype=x.dtype)
            kpad = jnp.concatenate([zpad, k], axis=2)
            vpad = jnp.concatenate([zpad, v], axis=2)
            k2 = jnp.concatenate([kpad[:, :, :-1], kpad[:, :, 1:]], axis=3)
            v2 = jnp.concatenate([vpad[:, :, :-1], vpad[:, :, 1:]], axis=3)
            scores = jnp.einsum('bhjqd,bhjkd->bhjqk', q, k2) / jnp.sqrt(jnp.asarray(Dh, dtype=x.dtype))
            qi = jnp.arange(W)[:, None]
            ki = jnp.arange(2 * W)[None, :]
            band = (ki >= qi + 1) & (ki <= qi + W)
            kpos_ok = (jnp.arange(nb)[:, None, None] - 1) * W + ki[None] >= 0
            mask = band[None] & kpos_ok
            neg = jnp.finfo(scores.dtype).min
            scores = jnp.where(mask[None, None], scores, neg)
            attn = jax.nn.softmax(scores, axis=-1)
            out = jnp.einsum('bhjqk,bhjkd->bhjqd', attn, v2)
            out = out.transpose(0, 2, 3, 1, 4).reshape(B, S, D)
            return out @ wo.T
        return _sliding_window_attn(x, wq, wk, wv, wo)

    def _L1_ffn_ref(x, ln_gamma, ln_beta, fc1_q, fc1_scales, fc1_bias, fc2_q, fc2_scales, fc2_bias):
        import jax, jax.numpy as jnp
        import numpy as np
        B, S, H, F, G = (8, 256, 128, 512, 128)
        EPS = 1e-05

        def _dequant(q, scales, g):
            K, N = q.shape
            w = (q.astype(jnp.float32) - 128.0).reshape(K // g, g, N) * scales[:, None, :]
            return w.reshape(K, N)
        residual = x
        mu = jnp.mean(x, axis=-1, keepdims=True)
        var = jnp.mean(jnp.square(x - mu), axis=-1, keepdims=True)
        h = (x - mu) * jax.lax.rsqrt(var + EPS) * ln_gamma + ln_beta
        hf = h.reshape(-1, H)
        w1 = _dequant(fc1_q, fc1_scales, G)
        y = hf @ w1 + fc1_bias
        y = jax.nn.silu(y)
        w2 = _dequant(fc2_q, fc2_scales, G)
        z = y @ w2 + fc2_bias
        return residual + 0.5 * z.reshape(residual.shape)
    x = L0_attn_x
    mod = (_silu(L0_c) @ L0_wmod).reshape(L0_c.shape[0], 6, 1, -1)
    sa, ca, ga, sb, cb, gb = (mod[:, 0], mod[:, 1], mod[:, 2], mod[:, 3], mod[:, 4], mod[:, 5])
    ga = (2 * (ga >= 0) - 1) * jnp.maximum(jnp.abs(ga), 0.25)
    gb = (2 * (gb >= 0) - 1) * jnp.maximum(jnp.abs(gb), 0.25)
    h = _layernorm(x, axis=-1) * (1 + ca) + sa
    x = x + ga * _L0_attn_ref(h, L0_attn_norm_in_w, L0_attn_conv_w, L0_attn_conv_b, L0_attn_Wq, L0_attn_Wk, L0_attn_Wv, L0_attn_Wo, L0_attn_Wspike, L0_attn_Wau, L0_attn_bau, L0_attn_Wad, L0_attn_bad, L0_attn_alpha_spike, L0_attn_Wbeta, L0_attn_bbeta, L0_attn_beta_spike, L0_attn_head_norm_w, L0_attn_Wu1, L0_attn_bu1, L0_attn_Wu2, L0_attn_bu2, L0_attn_ff_norm_w, L0_attn_Wff1, L0_attn_Wff3, L0_attn_Wff2)
    h = _layernorm(x, axis=-1) * (1 + cb) + sb
    x = x + gb * _L0_ffn_ref(h, L0_ffn_w1, L0_ffn_b1, L0_ffn_w2, L0_ffn_b2)
    mod = (_silu(L1_c) @ L1_wmod).reshape(L1_c.shape[0], 6, 1, -1)
    sa, ca, ga, sb, cb, gb = (mod[:, 0], mod[:, 1], mod[:, 2], mod[:, 3], mod[:, 4], mod[:, 5])
    ga = (2 * (ga >= 0) - 1) * jnp.maximum(jnp.abs(ga), 0.25)
    gb = (2 * (gb >= 0) - 1) * jnp.maximum(jnp.abs(gb), 0.25)
    h = _layernorm(x, axis=-1) * (1 + ca) + sa
    x = x + ga * _L1_attn_ref(h, L1_attn_wq, L1_attn_wk, L1_attn_wv, L1_attn_wo)
    h = _layernorm(x, axis=-1) * (1 + cb) + sb
    x = x + gb * _L1_ffn_ref(h, L1_ffn_ln_gamma, L1_ffn_ln_beta, L1_ffn_fc1_q, L1_ffn_fc1_scales, L1_ffn_fc1_bias, L1_ffn_fc2_q, L1_ffn_fc2_scales, L1_ffn_fc2_bias)
    return x

_drawn_inputs = setup_inputs


def setup_inputs(seed=0):
    import zlib

    import numpy as np

    out = dict(_drawn_inputs(seed))
    spreads = {'L0_attn_norm_in_w': (1.0, 0.6),
     'L0_attn_conv_b': (0.0, 0.48),
     'L0_attn_bau': (0.0, 0.8),
     'L0_attn_bad': (0.0, 0.8),
     'L0_attn_alpha_spike': (0.0, 0.8),
     'L0_attn_bbeta': (0.0, 0.8),
     'L0_attn_beta_spike': (0.0, 0.8),
     'L0_attn_head_norm_w': (1.0, 0.6),
     'L0_attn_bu1': (0.0, 0.8),
     'L0_attn_bu2': (0.0, 0.8),
     'L0_attn_ff_norm_w': (1.0, 0.6),
     'L1_ffn_ln_gamma': (1.0, 0.2),
     'L1_ffn_ln_beta': (0.0, 0.1)}
    factors = {'L0_attn_Wspike': 8.0,
     'L0_attn_Wau': 8.0,
     'L0_attn_Wad': 8.0,
     'L0_attn_Wbeta': 8.0,
     'L0_attn_Wu1': 8.0,
     'L0_attn_Wu2': 8.0,
     'L0_attn_Wff1': 8.0,
     'L0_attn_Wff3': 8.0,
     'L0_attn_Wff2': 8.0,
     'L0_ffn_b1': 64.0,
     'L0_ffn_b2': 46.355,
     'L1_attn_wq': 8.0,
     'L1_attn_wk': 8.0,
     'L1_attn_wv': 8.0,
     'L1_attn_wo': 8.0,
     'L1_ffn_fc1_scales': 17.417,
     'L1_ffn_fc1_bias': 64.0,
     'L1_ffn_fc2_bias': 64.0}
    for name, (base, spread) in spreads.items():
        noise = np.random.default_rng([zlib.crc32(name.encode()), seed]).standard_normal(out[name].shape)
        drawn = base * np.exp(spread * noise) if base else spread * noise
        out[name] = jnp.asarray(drawn.astype(out[name].dtype))
    for name, factor in factors.items():
        out[name] = (out[name] * factor).astype(out[name].dtype)
    return out
```

```python
from contextlib import ExitStack

import concourse.bass as bass
from concourse import mybir

F32 = mybir.dt.float32
I32 = mybir.dt.int32
U8 = mybir.dt.uint8
ALU = mybir.AluOpType
ACT = mybir.ActivationFunctionType
AX = mybir.AxisListType.X

P = 128
T, D = 2048, 128
NT = T // P
H, HD = 8, 64
NP = H // 2
R = 64
FF = 512
NF = FF // P
KW = 4
DECAY = 0.9
MIN_LOG_GATE = -20.0
FLOOR = -80.0
BASE = 8
UPPER = [8, 16, 32, 64]
LEVELS = [1, 2, 4] + UPPER


class Tensors:
    pass


class Steps:

    def __init__(self, names, rounds_ahead=0):
        self.names, self.done = names, 0
        self.index = {n: k + 1 for k, n in enumerate(names)}
        assert len(self.index) == len(names)
        self.credit = rounds_ahead * len(names)

    def at(self, name, i=0):
        return i * len(self.names) + self.index[name] + self.credit

    def before(self, name, i):
        return self.at(name, i) - len(self.names)

    def one(self, name):
        assert self.names[self.done % len(self.names)] == name, (name, self.done)
        self.done += 1
        return 1


def bc(ap, shape):
    return ap.to_broadcast(shape)


def setup_phase(nc, m, a):
    with ExitStack() as ctx:
        setup_tensors(nc, ctx, m)
        a.x, a.mods, a.weights = sources(m, a.ins)

        def steps(names):
            return Steps(names.split())

        x_in = ctx.enter_context(nc.semaphore("x_in"))
        mod_in = ctx.enter_context(nc.semaphore("mod_in"))
        weights_in = ctx.enter_context(nc.semaphore("weights_in"))
        pool_done = ctx.enter_context(nc.semaphore("setup_pool_done"))
        pool = steps("zero one select ident "
                     + " ".join(f"from{k} upto{k}" for k in range(1 + len(LEVELS)))
                     + " causal bd0 bd1 bd2 scan scan0 beta_w fills")
        vector_done = ctx.enter_context(nc.semaphore("setup_vector_done"))
        vec = steps("""
            eps c0 sum mean center var_sum norm c1 c2 c3
            ones_c g_neg g_max g_sign g_sign2 g_fin rows_c1 cols_c1
            h1 h hvar rms_in conv_w tap0 tap1 tap2 tap3 floor s1 s2 silu
            spike_beta masks first_neg flags states""" + " drive1 drive3 drive5 drive7 drive9 drive11 drive13 drive15")
        scalar_done = ctx.enter_context(nc.semaphore("setup_scalar_done"))
        act = steps("""c_exp sq1 ln1 r1 rows0 rows1 rows2 rows3 cols
            sq2 ln2 r2 hT0 hT1 hT2 hT3 s_exp""" + " drive0 drive2 drive4 drive6 drive8 drive10 drive12 drive14")
        tensor_done = ctx.enter_context(nc.semaphore("setup_tensor_done"))
        pe = steps("""rows0 rows1 rows2 rows3 cols hT0 hT1 hT2 hT3 """ + " ".join(f"drive{n}" for n in range(16)))

        x, xc, sq = m.x, m.arena[:, 0:2048], m.arena[:, 2048:4096]
        xc3, sq3 = (v.rearrange("p (n d) -> p n d", d=D) for v in (xc, sq))
        hr = m.arena[:, 4096:6144]
        hr3 = hr.rearrange("p (n d) -> p n d", d=D)
        st = m.stats
        block = ctx.enter_context(nc.Block())

        n_weights = len(a.weights)

        @block.sync
        def _(eng):
            eng.dma_start(m.x[:, :, :], a.x).then_inc(x_in, 16)
            for dst, src in a.weights[::2]:
                eng.dma_start(dst, src).then_inc(weights_in, 16)

        @block.gpsimd
        def _(eng):
            eng.memset(m.ident[:, :], 0.0).then_inc(pool_done, pool.one("zero"))
            eng.wait_ge(pool_done, pool.at("zero"))
            eng.memset(m.ones[:, :], 1.0).then_inc(pool_done, pool.one("one"))
            eng.wait_ge(pool_done, pool.at("one"))
            eng.memset(m.maskf[:, :], 1.0).then_inc(pool_done, pool.one("select"))
            eng.wait_ge(pool_done, pool.at("select"))
            eng.affine_select(out=m.ident[:, :], in_=m.ident[:, :], compare_op=ALU.not_equal, fill=1.0,
                                   base=0, pattern=[[-1, P]], channel_multiplier=1).then_inc(pool_done, pool.one("ident"))
            eng.wait_ge(pool_done, pool.at("ident"))
            own = m.maskf[:, 0:P].rearrange("p (b s) -> p b s", s=BASE)
            tables = [(own, BASE, BASE)]
            for n, s in enumerate(LEVELS):
                at = P + HD * n
                tables.append((m.maskf[:, at:at + HD].rearrange("p (b s) -> p b s", s=s), 2 * s, s))
            for k, (v, step, s) in enumerate(tables):
                nb = v.shape[1]
                eng.affine_select(out=v, in_=v, compare_op=ALU.is_ge, fill=0.0, base=0,
                                       pattern=[[-step, nb], [0, s]], channel_multiplier=1).then_inc(pool_done, pool.one(f"from{k}"))
                eng.wait_ge(pool_done, pool.at(f"from{k}"))
                eng.affine_select(out=v, in_=v, compare_op=ALU.is_ge, fill=0.0, base=s - 1,
                                       pattern=[[step, nb], [0, s]], channel_multiplier=-1).then_inc(pool_done, pool.one(f"upto{k}"))
                eng.wait_ge(pool_done, pool.at(f"upto{k}"))
            eng.affine_select(out=own, in_=own, compare_op=ALU.is_ge, fill=0.0, base=0,
                                   pattern=[[BASE, P // BASE], [1, BASE]], channel_multiplier=-1).then_inc(pool_done, pool.one("causal"))
            eng.wait_ge(pool_done, pool.at("causal"))
            eng.memset(m.bd[:, :], 0.0).then_inc(pool_done, pool.one("bd0"))
            eng.wait_ge(pool_done, pool.at("bd0"))
            eng.memset(m.bd[0:HD, 0:HD], 1.0).then_inc(pool_done, pool.one("bd1"))
            eng.wait_ge(pool_done, pool.at("bd1"))
            eng.memset(m.bd[HD:P, HD:P], 1.0).then_inc(pool_done, pool.one("bd2"))
            eng.wait_ge(pool_done, pool.at("bd2"))
            eng.memset(m.scan_keep[:, :, :], 1.0).then_inc(pool_done, pool.one("scan"))
            eng.wait_ge(pool_done, pool.at("scan"))
            eng.memset(m.scan_keep[:, :, 0:1], 0.0).then_inc(pool_done, pool.one("scan0"))
            eng.wait_ge(pool_done, pool.at("scan0"))
            eng.wait_ge(weights_in, 16 * n_weights)
            eng.tensor_copy(m.beta_w[:, :, :], bc(m.wbeta[:, :].unsqueeze(2), [P, H, HD])).then_inc(pool_done, pool.one("beta_w"))
            eng.wait_ge(pool_done, pool.at("beta_w"))
            eng.tensor_copy(m.beta_b[:, :, :], bc(m.bbeta[:, :].unsqueeze(2), [1, H, HD])).then_inc(pool_done, pool.one("fills"))
            eng.wait_ge(pool_done, pool.at("fills"))

        @block.scalar
        def _(eng):
            for dst, src in a.mods:
                eng.dma_start(dst, src).then_inc(mod_in, 16)
            for dst, src in a.weights[1::2]:
                eng.dma_start(dst, src).then_inc(weights_in, 16)
            eng.wait_ge(vector_done, vec.at("c0"))
            eng.activation(st[:, 0:2], m.c[:, :], ACT.Exp, scale=-1.0).then_inc(scalar_done, act.one("c_exp"))
            eng.wait_ge(vector_done, vec.at("center"))
            eng.activation(sq, xc, ACT.Square).then_inc(scalar_done, act.one("sq1"))
            eng.wait_ge(vector_done, vec.at("var_sum"))
            eng.wait_ge(vector_done, vec.at("eps"))
            eng.activation(st[:, 48:64], st[:, 48:64], ACT.Ln, scale=1.0 / D, bias=m.eps[:, 0:1]).then_inc(scalar_done, act.one("ln1"))
            eng.wait_ge(scalar_done, act.at("ln1"))
            eng.activation(st[:, 48:64], st[:, 48:64], ACT.Exp, scale=-0.5).then_inc(scalar_done, act.one("r1"))
            for l in range(2):
                for b in range(2):
                    n = 2 * l + b
                    eng.wait_ge(tensor_done, pe.at(f"rows{n}"))
                    eng.activation(m.mod_rows[:, l, 384 * b:384 * b + 384], m.ps[:, n, 0:384], ACT.Copy).then_inc(scalar_done, act.one(f"rows{n}"))
            eng.wait_ge(tensor_done, pe.at("cols"))
            eng.activation(m.mod_cols[:, :, :].rearrange("p l k -> p (l k)"), m.ps[:, 4, 0:12], ACT.Copy).then_inc(scalar_done, act.one("cols"))
            eng.wait_ge(vector_done, vec.at("h"))
            eng.activation(sq, m.h[:, :, :].rearrange("p n d -> p (n d)"), ACT.Square).then_inc(scalar_done, act.one("sq2"))
            eng.wait_ge(vector_done, vec.at("hvar"))
            eng.activation(st[:, 64:80], st[:, 64:80], ACT.Ln, scale=1.0 / D, bias=m.eps[:, 1:2]).then_inc(scalar_done, act.one("ln2"))
            eng.wait_ge(scalar_done, act.at("ln2"))
            eng.activation(st[:, 64:80], st[:, 64:80], ACT.Exp, scale=-0.5).then_inc(scalar_done, act.one("r2"))
            eng.wait_ge(vector_done, vec.at("c3"))
            for n in range(4):
                eng.wait_ge(tensor_done, pe.at(f"hT{n}"))
                eng.activation(m.hist[:, KW - 1 + 512 * n:KW - 1 + 512 * n + 512], m.ps[:, n, :], ACT.Copy).then_inc(scalar_done, act.one(f"hT{n}"))
            eng.wait_ge(vector_done, vec.at("floor"))
            eng.activation(sq, xc, ACT.Exp, scale=-1.0).then_inc(scalar_done, act.one("s_exp"))
            for n in range(0, 16, 2):
                eng.wait_ge(tensor_done, pe.at(f"drive{n}"))
                eng.activation(m.drive[:, n // 4, 512 * (n % 4):512 * (n % 4) + 512], m.ps[:, n % 8, :],
                                       ACT.Copy, scale=2.0).then_inc(scalar_done, act.one(f"drive{n}"))

        @block.tensor
        def _(eng):
            eng.wait_ge(vector_done, vec.at("ones_c"))
            for l in range(2):
                for b in range(2):
                    eng.matmul(m.ps[:, 2 * l + b, 0:384], m.c_wide[:, l, :], m.wmod[:, l, 384 * b:384 * b + 384],
                                      start=True, stop=True).then_inc(tensor_done, pe.one(f"rows{2 * l + b}"))
            for l in range(2):
                for k in range(6):
                    ins = eng.matmul(m.ps[:, 4, 6 * l + k:6 * l + k + 1], m.wmod[:, l, k * D:(k + 1) * D],
                                     st[:, 4 + l:5 + l], start=True, stop=True)
            ins.then_inc(tensor_done, pe.one("cols"))
            eng.wait_ge(pool_done, pool.at("ident"))
            eng.wait_ge(vector_done, vec.at("rms_in"))
            for n in range(4):
                eng.wait_ge(scalar_done, act.at(f"rows{n}"))
                for k in range(4):
                    ins = eng.transpose(m.ps[:, n, k * D:(k + 1) * D], hr3[:, 4 * n + k, :], m.ident[:, :])
                ins.then_inc(tensor_done, pe.one(f"hT{n}"))
            eng.wait_ge(vector_done, vec.at("silu"))
            eng.wait_ge(scalar_done, act.at("cols"))
            for n in range(16):
                if n < 4:
                    eng.wait_ge(scalar_done, act.at(f"hT{n}"))
                if n >= 8:
                    if n % 2 == 0:
                        eng.wait_ge(scalar_done, act.at(f"drive{n - 8}"))
                    else:
                        eng.wait_ge(vector_done, vec.at(f"drive{n - 8}"))
                eng.matmul(m.ps[:, n % 8, :], m.wspike[:, n // 4 * P:n // 4 * P + P],
                                  m.hh[:, 512 * (n % 4):512 * (n % 4) + 512], start=True, stop=True).then_inc(tensor_done, pe.one(f"drive{n}"))

        @block.vector
        def _(eng):
            eng.memset(m.eps[:, 0:1], 1e-5)
            eng.memset(m.eps[:, 1:2], 1e-6).then_inc(vector_done, vec.one("eps"))
            eng.wait_ge(mod_in, 16 * len(a.mods))
            eng.tensor_scalar(m.c[:, :], m.c[:, :], FLOOR, None, ALU.max).then_inc(vector_done, vec.one("c0"))
            eng.wait_ge(x_in, 16)
            eng.tensor_reduce(st[:, 16:32], x[:, :, :], AX, ALU.add).then_inc(vector_done, vec.one("sum"))
            eng.wait_ge(vector_done, vec.at("sum"))
            eng.tensor_scalar(st[:, 32:48], st[:, 16:32], -1.0 / D, None, ALU.mult).then_inc(vector_done, vec.one("mean"))
            eng.wait_ge(vector_done, vec.at("mean"))
            eng.tensor_tensor(xc3, x[:, :, :], bc(st[:, 32:48].unsqueeze(2), [P, NT, D]), ALU.add).then_inc(vector_done, vec.one("center"))
            eng.wait_ge(scalar_done, act.at("sq1"))
            eng.tensor_reduce(st[:, 48:64], sq3, AX, ALU.add).then_inc(vector_done, vec.one("var_sum"))
            eng.wait_ge(scalar_done, act.at("r1"))
            eng.tensor_tensor(xc3, xc3, bc(st[:, 48:64].unsqueeze(2), [P, NT, D]), ALU.mult).then_inc(vector_done, vec.one("norm"))
            eng.wait_ge(scalar_done, act.at("c_exp"))
            eng.tensor_scalar(st[:, 2:4], st[:, 0:2], 1.0, None, ALU.add).then_inc(vector_done, vec.one("c1"))
            eng.wait_ge(vector_done, vec.at("c1"))
            eng.reciprocal(st[:, 6:8], st[:, 2:4]).then_inc(vector_done, vec.one("c2"))
            eng.wait_ge(vector_done, vec.at("c2"))
            eng.wait_ge(mod_in, 16 * len(a.mods))
            eng.memset(m.hist[:, 0:KW - 1], 0.0)
            eng.tensor_tensor(st[:, 4:6], st[:, 6:8], m.c[:, :], ALU.mult).then_inc(vector_done, vec.one("c3"))
            eng.wait_ge(vector_done, vec.at("c3"))
            eng.tensor_copy(m.c_wide[:, :, :], bc(st[:, 4:6].unsqueeze(2), [P, 2, P])).then_inc(vector_done, vec.one("ones_c"))
            eng.wait_ge(scalar_done, act.at("rows3"))
            g = m.mod_rows[:, :, :].rearrange("p l (u k d) -> p (l u) k d", u=2, k=3)[:, :, 2, :]
            s1 = m.scratch[:, 0:512].rearrange("p (u d) -> p u d", u=4)
            eng.tensor_scalar(s1, g, -1.0, None, ALU.mult).then_inc(vector_done, vec.one("g_neg"))
            eng.wait_ge(vector_done, vec.at("g_neg"))
            eng.tensor_tensor(s1, s1, g, ALU.max).then_inc(vector_done, vec.one("g_max"))
            s2 = m.scratch[:, 512:1024].rearrange("p (u d) -> p u d", u=4)
            eng.tensor_scalar(s2, g, 0.0, 2.0, ALU.is_ge, ALU.mult).then_inc(vector_done, vec.one("g_sign"))
            eng.wait_ge(vector_done, vec.at("g_sign"))
            eng.tensor_scalar(s2, s2, -1.0, None, ALU.add).then_inc(vector_done, vec.one("g_sign2"))
            eng.wait_ge(vector_done, vec.at("g_sign2"))
            eng.scalar_tensor_tensor(g, s1, 0.25, s2, ALU.max, ALU.mult).then_inc(vector_done, vec.one("g_fin"))
            one_row = m.mod_rows[:, :, :].rearrange("p l (u k d) -> p (l u) k d", u=2, k=3)[:, :, 1, :]
            eng.tensor_scalar(one_row, one_row, 1.0, None, ALU.add).then_inc(vector_done, vec.one("rows_c1"))
            eng.wait_ge(scalar_done, act.at("cols"))
            one_col = m.mod_cols[:, :, :].rearrange("p l (u k) -> p (l u) k", u=2)[:, :, 1]
            eng.tensor_scalar(one_col, one_col, 1.0, None, ALU.add).then_inc(vector_done, vec.one("cols_c1"))
            eng.wait_ge(vector_done, vec.at("norm"))
            eng.wait_ge(vector_done, vec.at("rows_c1"))
            eng.tensor_tensor(m.h[:, :, :], xc3, bc(m.mod_rows[:, 0:1, D:2 * D], [P, NT, D]), ALU.mult).then_inc(vector_done, vec.one("h1"))
            eng.wait_ge(vector_done, vec.at("h1"))
            eng.tensor_tensor(m.h[:, :, :], m.h[:, :, :], bc(m.mod_rows[:, 0:1, 0:D], [P, NT, D]), ALU.add).then_inc(vector_done, vec.one("h"))
            eng.wait_ge(scalar_done, act.at("sq2"))
            eng.tensor_reduce(st[:, 64:80], sq3, AX, ALU.add).then_inc(vector_done, vec.one("hvar"))
            eng.wait_ge(scalar_done, act.at("r2"))
            eng.tensor_tensor(hr3, m.h[:, :, :], bc(st[:, 64:80].unsqueeze(2), [P, NT, D]), ALU.mult).then_inc(vector_done, vec.one("rms_in"))
            eng.wait_ge(weights_in, 16 * n_weights)
            eng.tensor_scalar(m.conv_w[:, :], m.conv_w[:, :], m.norm_in[:, 0:1], None, ALU.mult).then_inc(vector_done, vec.one("conv_w"))
            eng.wait_ge(vector_done, vec.at("conv_w"))
            eng.wait_ge(scalar_done, act.at("hT3"))
            eng.tensor_scalar(xc, m.hist[:, 0:T], m.conv_w[:, 0:1], m.conv_b[:, 0:1], ALU.mult, ALU.add).then_inc(vector_done, vec.one("tap0"))
            for k in range(1, KW):
                eng.wait_ge(vector_done, vec.at(f"tap{k - 1}"))
                eng.scalar_tensor_tensor(xc, m.hist[:, k:k + T], m.conv_w[:, k:k + 1], xc, ALU.mult, ALU.add).then_inc(vector_done, vec.one(f"tap{k}"))
            eng.wait_ge(vector_done, vec.at(f"tap{KW - 1}"))
            eng.tensor_scalar(xc, xc, FLOOR, None, ALU.max).then_inc(vector_done, vec.one("floor"))
            eng.wait_ge(scalar_done, act.at("s_exp"))
            eng.tensor_scalar(sq, sq, 1.0, None, ALU.add).then_inc(vector_done, vec.one("s1"))
            eng.wait_ge(vector_done, vec.at("s1"))
            eng.reciprocal(hr, sq).then_inc(vector_done, vec.one("s2"))
            eng.wait_ge(vector_done, vec.at("s2"))
            eng.tensor_tensor(m.hh[:, :], hr, xc, ALU.mult).then_inc(vector_done, vec.one("silu"))
            eng.wait_ge(pool_done, pool.at("fills"))
            eng.tensor_tensor(m.beta_s[:, :, :], bc(m.bd[:, :].unsqueeze(1), [P, NP, P]),
                                      bc(m.bspike[:, :].unsqueeze(2), [P, NP, P]), ALU.mult).then_inc(vector_done, vec.one("spike_beta"))
            eng.tensor_scalar(m.mask[:, :], m.maskf[:, :], 0.5, None, ALU.is_gt).then_inc(vector_done, vec.one("masks"))
            for n in range(len(LEVELS)):
                ins = eng.tensor_reduce(m.first_neg[:, n:n + 1], m.maskf[:, P + HD * n:P + HD * n + HD], AX, ALU.max, negate=True)
            ins.then_inc(vector_done, vec.one("first_neg"))
            eng.memset(m.diff[:, :, :], 0.0)
            eng.memset(m.wide[:, :], 0.0).then_inc(vector_done, vec.one("flags"))
            eng.memset(m.mem[:, :, 0:1], 0.0).then_inc(vector_done, vec.one("states"))
            for n in range(1, 16, 2):
                eng.wait_ge(tensor_done, pe.at(f"drive{n}"))
                eng.tensor_scalar(m.drive[:, n // 4, 512 * (n % 4):512 * (n % 4) + 512], m.ps[:, n % 8, :],
                                          2.0, None, ALU.mult).then_inc(vector_done, vec.one(f"drive{n}"))


def spike_phase(nc, m):
    with ExitStack() as ctx:
        step = ctx.enter_context(nc.semaphore("membrane_step"))
        block = ctx.enter_context(nc.Block())
        u, d = m.mem, m.drive[:, :, :].rearrange("p c (n t) -> p (c n) t", t=P)
        start = u[:, :, 0:1].rearrange("p (c n) o -> p c (n o)", c=NP)
        end = u[:, :, P:P + 1].rearrange("p (c n) o -> p c (n o)", c=NP)

        @block.vector
        def _(eng):
            eng.sem_clear(step)
            eng.memset(m.flag[:, 0:32], 0).then_inc(step, 1)
            eng.wait_ge(step, 1)
            eng.memset(m.flag[:, 0:1], 1).then_inc(step, 1)
            eng.wait_ge(step, 2)
            with eng.Fori(0, NT) as _:
                changed = eng.value_load(m.flag[0:1, 0:1])
                for q in range(1, 4):
                    changed = changed + eng.value_load(m.flag[32 * q:32 * q + 1, 0:1])
                with eng.If(changed > 0):
                    eng.sem_clear(step)
                    for t in range(P):
                        if t:
                            eng.wait_ge(step, 2 * t)
                        eng.scalar_tensor_tensor(m.kept[:, :], u[:, :, t], 1.0, u[:, :, t], ALU.is_gt, ALU.subtract).then_inc(step, 1)
                        eng.wait_ge(step, 2 * t + 1)
                        eng.scalar_tensor_tensor(u[:, :, t + 1], m.kept[:, :], -DECAY, d[:, :, t], ALU.mult, ALU.add).then_inc(step, 1)
                    n = 2 * P
                    eng.wait_ge(step, n)
                    eng.tensor_tensor(m.diff[:, :, 0:NT - 1], start[:, :, 1:NT], end[:, :, 0:NT - 1], ALU.not_equal).then_inc(step, 1)
                    eng.wait_ge(step, n + 1)
                    eng.tensor_reduce(m.wide[:, 0:1], m.diff[:, :, :].rearrange("p c n -> p (c n)"), AX, ALU.max).then_inc(step, 1)
                    eng.tensor_copy(start[:, :, 1:NT], end[:, :, 0:NT - 1]).then_inc(step, 1)
                    eng.wait_ge(step, n + 3)
                    eng.transpose(m.wide_t[:, 0:32], m.wide[:, 0:32]).then_inc(step, 1)
                    eng.wait_ge(step, n + 4)
                    eng.tensor_reduce(m.flag[:, 0:1], m.wide_t[:, 0:32], AX, ALU.max).then_inc(step, 1)
                    eng.wait_ge(step, n + 5)


def delta_phase(nc, m):
    with ExitStack() as ctx:
        delta_tensors(nc, ctx, m)

        def steps(names):
            return Steps(names.split(), rounds_ahead=1)

        HALVES = "ab"
        join = "".join(f" TXa{s} XTa{s} TXb{s} XTb{s}" if s < 64 else f" XTa{s} XTb{s}" for s in LEVELS[1:])
        tensor_done = ctx.enter_context(nc.semaphore("delta_tensor_done"))
        pe = steps("k q v au ksum qsum drive_a count beta"
                   + "".join(f" base{n}" for n in range(4))
                   + "".join(f" up{s}{x}" for s in UPPER for x in HALVES) + " tra trb"
                   + "".join(f" X{s}a X{s}b" + (f" TXa{s} XTa{s} TXb{s} XTb{s}" if s < 64 else f" XTa{s} XTb{s}")
                             for s in LEVELS[1:])
                   + " kend seen solved out update")
        scalar_done = ctx.enter_context(nc.semaphore("delta_scalar_done"))
        act = steps("hh k q v au_e ln_n rt_n z_e z_ln beta_e"
                    + " lift_up lift_p lift_n lift_all last"
                    + " tra trb" + "".join(f" X{s}a X{s}b" for s in LEVELS[1:])
                    + " kend solved out")
        vector_done = ctx.enter_context(nc.semaphore("delta_vector_done"))
        vec = steps("spikes guard au0 au1 au2 au active z zfloor b0 log_a G b1 b2 b3 n1 n2 unit beta_k mid"
                    + "".join(f" lo{s} hi{s}" for s in UPPER) + " toend kq_base"
                    + "".join(f" kq{s}" for s in UPPER) + " kq_all k_end"
                    + "".join(f" base{n}" for n in range(4)) + " up8a up8b tt"
                    + "".join(f" up{s}{x}" for s in UPPER[1:] for x in HALVES) + join
                    + " rest keep update")
        pool_done = ctx.enter_context(nc.semaphore("delta_pool_done"))
        pool = steps("square push km_base" + "".join(f" km{s}" for s in UPPER))

        kq = m.kq
        kqf = kq[:, :, :].rearrange("p a c -> p (a c)")
        EX = m.arena[:, 0:3072].rearrange("p (n c) -> p n c", c=512)
        up_lift = {s: EX[:, n] for n, s in enumerate(UPPER)}
        end_lift, mid = EX[:, 4], EX[:, 5]
        base_p, base_n, all_lift = (m.arena[:, 3072 + 512 * n:3584 + 512 * n] for n in range(3))
        square = m.arena[:, 4608:5632]
        g3 = m.G[:, :, :]
        gf = m.G[:, :, :].rearrange("p c t -> p (c t)")
        bt = {s: m.drive[:, :, :].rearrange("p c t -> p (c t)")[:, 1024 * n:1024 * n + 1024].rearrange("p (h t) -> p h t", t=P)
              for n, s in enumerate(LEVELS)}

        def halves(ap, s):
            return ap.rearrange("p (b two s) -> p b two s", two=2, s=s)

        def head_halves(ap, s, hs, which):
            return ap[:, hs, :].rearrange("p h (b two s) -> p h b two s", two=2, s=s)[:, :, :, which, :]

        def mask_of(s, n, table=m.mask):
            c = P + HD * LEVELS.index(s)
            v = table[:, c:c + HD].rearrange("p (b s) -> p b s", s=s).unsqueeze(1)
            return bc(v, [P, n, HD // s, s])

        def base_heads(n):
            return range(4 * (n // 2) + n % 2, 4 * (n // 2) + 4, 2)

        def tok(i):
            return bass.ds(i * P, P)

        block = ctx.enter_context(nc.Block())

        @block.gpsimd
        def _(eng):
            eng.sem_inc(pool_done, pool.credit)
            with eng.Fori(0, NT) as i:
                eng.wait_ge(scalar_done, act.at("k", i))
                eng.wait_ge(scalar_done, act.at("q", i))
                eng.wait_ge(tensor_done, pe.before("qsum", i))
                eng.tensor_tensor(square, kq[:, :, :].rearrange("p a c -> p (a c)"),
                                           kq[:, :, :].rearrange("p a c -> p (a c)"), ALU.mult).then_inc(pool_done, pool.one("square"))
                eng.wait_ge(vector_done, vec.at("spikes", i))
                eng.tensor_tensor(m.push[:, :, :], m.spk[:, :, :], bc(m.aspike[:, :].unsqueeze(2), [P, NP, P]), ALU.mult).then_inc(pool_done, pool.one("push"))
                eng.wait_ge(vector_done, vec.at("beta_k", i))
                eng.wait_ge(scalar_done, act.at("lift_n", i))
                eng.wait_ge(tensor_done, pe.before("base3", i))
                eng.tensor_tensor(m.km[:, :], m.beta_k[:, :], base_n, ALU.mult).then_inc(pool_done, pool.one("km_base"))
                for s in UPPER:
                    eng.wait_ge(vector_done, vec.at(f"kq{s}", i))
                    eng.tensor_tensor(up_lift[s], m.beta_k[:, :], up_lift[s], ALU.mult).then_inc(pool_done, pool.one(f"km{s}"))

        @block.scalar
        def _(eng):
            eng.sem_inc(scalar_done, act.credit)
            with eng.Fori(0, NT) as i:
                eng.wait_ge(tensor_done, pe.before("beta", i))
                eng.activation(m.hh_tile[:, :], m.hh[:, tok(i)], ACT.Copy).then_inc(scalar_done, act.one("hh"))
                eng.wait_ge(tensor_done, pe.at("k", i))
                eng.wait_ge(vector_done, vec.before("kq_all", i))
                eng.wait_ge(pool_done, pool.before("square", i))
                eng.activation(kq[:, 0, :], m.ps[:, 0, :], ACT.Copy).then_inc(scalar_done, act.one("k"))
                eng.wait_ge(tensor_done, pe.at("q", i))
                eng.activation(kq[:, 1, :], m.ps[:, 1, :], ACT.Copy).then_inc(scalar_done, act.one("q"))
                eng.wait_ge(tensor_done, pe.at("v", i))
                eng.wait_ge(vector_done, vec.before("rest", i))
                eng.activation(m.v[:, :], m.ps[:, 2, :], ACT.Copy).then_inc(scalar_done, act.one("v"))
                eng.wait_ge(vector_done, vec.at("au0", i))
                eng.activation(m.au_e[:, :], m.au_x[:, :], ACT.Exp, scale=-1.0).then_inc(scalar_done, act.one("au_e"))
                eng.activation(m.norm[:, :], m.norm[:, :], ACT.Ln).then_inc(scalar_done, act.one("ln_n"))
                eng.wait_ge(scalar_done, act.at("ln_n", i))
                eng.activation(m.norm[:, :], m.norm[:, :], ACT.Exp, scale=0.5).then_inc(scalar_done, act.one("rt_n"))
                eng.wait_ge(vector_done, vec.at("zfloor", i))
                eng.activation(m.z[:, :], m.z[:, :], ACT.Exp, scale=-1.0).then_inc(scalar_done, act.one("z_e"))
                eng.wait_ge(scalar_done, act.at("z_e", i))
                eng.activation(m.z[:, :], m.z[:, :], ACT.Ln, bias=1.0).then_inc(scalar_done, act.one("z_ln"))
                eng.wait_ge(vector_done, vec.at("b0", i))
                eng.activation(m.beta[:, :], m.beta[:, :], ACT.Exp, scale=-1.0).then_inc(scalar_done, act.one("beta_e"))
                eng.wait_ge(vector_done, vec.at("toend", i))
                eng.activation(EX[:, 0:5, :], EX[:, 0:5, :], ACT.Exp).then_inc(scalar_done, act.one("lift_up"))
                eng.wait_ge(vector_done, vec.before("kq_base", i))
                eng.activation(base_p, mid, ACT.Exp).then_inc(scalar_done, act.one("lift_p"))
                eng.wait_ge(pool_done, pool.before("km_base", i))
                eng.activation(base_n, mid, ACT.Exp, scale=-1.0).then_inc(scalar_done, act.one("lift_n"))
                eng.wait_ge(vector_done, vec.before("kq_all", i))
                eng.activation(all_lift, gf, ACT.Exp).then_inc(scalar_done, act.one("lift_all"))
                eng.wait_ge(vector_done, vec.before("keep", i))
                eng.activation(m.last[:, :].unsqueeze(2), g3[:, :, P - 1:P], ACT.Exp).then_inc(scalar_done, act.one("last"))
                for n, x in enumerate(HALVES):
                    eng.wait_ge(tensor_done, pe.at(f"tr{x}", i))
                    eng.activation(m.tm[:, 4 * n:4 * n + 4, :], m.ps[:, 4 + n, :].rearrange("p (h t) -> p h t", t=P), ACT.Copy).then_inc(scalar_done, act.one(f"tr{x}"))
                for s in LEVELS[1:]:
                    for n, x in enumerate(HALVES):
                        hs = slice(4 * n, 4 * n + 4)
                        eng.wait_ge(tensor_done, pe.at(f"X{s}{x}", i))
                        src = m.ps[:, 6 + n, 0:256].rearrange("p (h b s) -> p h b s", h=4, s=s)
                        dst = head_halves(m.xf, s, hs, 0)
                        if HD // s == 1:
                            src, dst = src[:, :, 0, :], dst[:, :, 0, :]
                        eng.activation(dst, src, ACT.Copy).then_inc(scalar_done, act.one(f"X{s}{x}"))
                eng.wait_ge(tensor_done, pe.at("kend", i))
                eng.activation(m.k_end_rows[:, :], m.ps[:, 4, :], ACT.Copy).then_inc(scalar_done, act.one("kend"))
                eng.wait_ge(tensor_done, pe.at("solved", i))
                eng.activation(m.u_rows[:, :], m.ps[:, 5, :], ACT.Copy).then_inc(scalar_done, act.one("solved"))
                eng.wait_ge(tensor_done, pe.at("out", i))
                eng.wait_ge(vector_done, vec.at("spikes", i))
                y = m.mem[:, :, 0:P].rearrange("p (c n) t -> p c n t", c=NP)[:, :, bass.ds(i, 1), :]
                for e in range(2):
                    ins = eng.activation(y[:, :, :, HD * e:HD * e + HD],
                                         m.ps[:, e, 0:256].rearrange("p (c v) -> p c v", c=NP).unsqueeze(2), ACT.Copy)
                ins.then_inc(scalar_done, act.one("out"))

        @block.tensor
        def _(eng):
            eng.sem_inc(tensor_done, pe.credit)

            def head(h):
                return slice(HD * (h % 2), HD * (h % 2) + HD), slice(P * (h // 2), P * (h // 2) + P)

            with eng.Fori(0, NT) as i:
                eng.wait_ge(scalar_done, act.at("hh", i))
                for c in range(NP):
                    ins = eng.matmul(m.ps[:, 0, c * P:c * P + P], m.wk[:, c * P:c * P + P], m.hh_tile[:, :], start=True, stop=True)
                ins.then_inc(tensor_done, pe.one("k"))
                for c in range(NP):
                    ins = eng.matmul(m.ps[:, 1, c * P:c * P + P], m.wq[:, c * P:c * P + P], m.hh_tile[:, :], start=True, stop=True)
                ins.then_inc(tensor_done, pe.one("q"))
                eng.wait_ge(vector_done, vec.before("rest", i))
                eng.matmul(m.ps[:, 2, :], m.hh_tile[:, :], m.wv[:, :], start=True, stop=True).then_inc(tensor_done, pe.one("v"))
                eng.wait_ge(vector_done, vec.before("update", i))
                eng.matmul(m.ps[0:R, 3, 0:P], m.wau[:, :], m.hh_tile[:, :], start=True, stop=True).then_inc(tensor_done, pe.one("au"))
                eng.wait_ge(pool_done, pool.at("square", i))
                eng.matmul(m.ps[:, 4, :], m.bd[:, :], square[:, 0:512], start=True, stop=True).then_inc(tensor_done, pe.one("ksum"))
                eng.matmul(m.ps[:, 5, :], m.bd[:, :], square[:, 512:1024], start=True, stop=True).then_inc(tensor_done, pe.one("qsum"))
                eng.wait_ge(vector_done, vec.at("au", i))
                for c in range(NP):
                    ins = eng.matmul(m.ps[:, 3, c * P:c * P + P], m.wad[:, c * P:c * P + P], m.au[:, :], start=True, stop=True)
                ins.then_inc(tensor_done, pe.one("drive_a"))
                eng.wait_ge(vector_done, vec.at("spikes", i))
                eng.matmul(m.ps[:, 7, :], m.bd[:, :], m.spk[:, :, :].rearrange("p c t -> p (c t)"), start=True, stop=True).then_inc(tensor_done, pe.one("count"))
                for c in range(NP):
                    o = m.ps[:, 6, c * P:c * P + P]
                    eng.matmul(o, m.beta_w[:, :, :].rearrange("p h k -> p (h k)")[:, c * P:c * P + P], m.hh_tile[:, :], start=True, stop=False)
                    eng.matmul(o, m.beta_s[:, c, :], m.spk[:, c, :], start=False, stop=False)
                    ins = eng.matmul(o, m.beta_b[:, :, :].rearrange("p h k -> p (h k)")[:, c * P:c * P + P], m.ones[0:1, :], start=False, stop=True)
                ins.then_inc(tensor_done, pe.one("beta"))
                eng.wait_ge(vector_done, vec.at("kq_base", i))
                eng.wait_ge(scalar_done, act.at("v", i))
                eng.wait_ge(pool_done, pool.at("km_base", i))
                for n in range(4):
                    for j, h in enumerate(base_heads(n)):
                        ks, cs = head(h)
                        ins = eng.matmul(m.ps[:, n, 256 * j:256 * j + 256], m.km[ks, cs], m.kq_base[ks, :, cs], start=True, stop=True)
                    ins.then_inc(tensor_done, pe.one(f"base{n}"))
                for s in UPPER:
                    eng.wait_ge(vector_done, vec.at(f"kq{s}", i))
                    eng.wait_ge(pool_done, pool.at(f"km{s}", i))
                    at = {8: 4, 16: 6, 32: 0, 64: 2}[s]
                    for n, x in enumerate(HALVES):
                        if s == 16:
                            eng.wait_ge(scalar_done, act.at("beta_e", i))
                        if s == 32:
                            eng.wait_ge(vector_done, vec.at(f"base{n}", i))
                        if s == 64:
                            eng.wait_ge(vector_done, vec.at(f"base{2 + n}", i))
                        for h in range(n, H, 2):
                            ks, cs = head(h)
                            half = slice(HD * (h // 2), HD * (h // 2) + HD)
                            ins = eng.matmul(m.ps[:, at + n, P * (h // 2):P * (h // 2) + P], up_lift[s][ks, cs], m.kq_up[s][ks, :, half], start=True, stop=True)
                        ins.then_inc(tensor_done, pe.one(f"up{s}{x}"))
                eng.wait_ge(vector_done, vec.at("tt", i))
                for n, x in enumerate(HALVES):
                    for h in range(4 * n, 4 * n + 4):
                        ins = eng.transpose(m.ps[:, 4 + n, P * (h % 4):P * (h % 4) + P], m.tt[:, h, :], m.ident[:, :])
                    ins.then_inc(tensor_done, pe.one(f"tr{x}"))
                eng.wait_ge(vector_done, vec.at("up64b", i))
                prev = None
                for s in LEVELS[1:]:
                    for n, x in enumerate(HALVES):
                        if prev is None:
                            eng.wait_ge(scalar_done, act.at(f"tr{x}", i))
                        else:
                            eng.wait_ge(vector_done, vec.at(f"TX{x}{prev}", i))
                            eng.wait_ge(scalar_done, act.at(f"X{prev}{x}", i))
                        for h in range(4 * n, 4 * n + 4):
                            ins = eng.matmul(m.ps[:, 6 + n, HD * (h % 4):HD * (h % 4) + HD], bt[s][:, h, :],
                                             m.tm[:, h, :].rearrange("p (b two s) -> p b two s", two=2, s=s)[:, :, 0, :], start=True, stop=True)
                        ins.then_inc(tensor_done, pe.one(f"X{s}{x}"))
                    for n, x in enumerate(HALVES):
                        eng.wait_ge(scalar_done, act.at(f"X{s}{x}", i))
                        if prev is not None:
                            eng.wait_ge(vector_done, vec.at(f"XT{x}{prev}", i))
                        if s < 64:
                            for h in range(4 * n, 4 * n + 4):
                                ins = eng.matmul(m.ps[:, 2 + n, HD * (h % 4):HD * (h % 4) + HD], m.tt[:, h, :],
                                                 m.xf[:, h, :].rearrange("p (b two s) -> p b two s", two=2, s=s)[:, :, 0, :], start=True, stop=True)
                            ins.then_inc(tensor_done, pe.one(f"TX{x}{s}"))
                        for h in range(4 * n, 4 * n + 4):
                            ins = eng.matmul(m.ps[:, 0 + n, HD * (h % 4):HD * (h % 4) + HD], m.xf[:, h, :],
                                             m.tt[:, h, :].rearrange("p (b two s) -> p b two s", two=2, s=s)[:, :, 1, :], start=True, stop=True)
                        ins.then_inc(tensor_done, pe.one(f"XT{x}{s}"))
                    prev = s
                eng.wait_ge(vector_done, vec.at("k_end", i))
                for c in range(NP):
                    ins = eng.transpose(m.ps[:, 4, c * P:c * P + P], m.k_end[:, c * P:c * P + P], m.ident[:, :])
                ins.then_inc(tensor_done, pe.one("kend"))
                eng.wait_ge(vector_done, vec.at("TXb32", i))
                for h in range(H):
                    ks, cs = head(h)
                    ins = eng.matmul(m.ps[:, 2 + h % 2, HD * (h // 2):HD * (h // 2) + HD], m.kq_all[ks, 0, cs], m.state[ks, h // 2, :], start=True, stop=True)
                ins.then_inc(tensor_done, pe.one("seen"))
                eng.wait_ge(vector_done, vec.at("rest", i))
                for h in range(H):
                    ins = eng.matmul(m.ps[:, 5, HD * h:HD * h + HD], m.tt[:, h, :], m.rest[:, HD * h:HD * h + HD], start=True, stop=True)
                ins.then_inc(tensor_done, pe.one("solved"))
                eng.wait_ge(scalar_done, act.at("solved", i))
                for h in range(H):
                    ks, cs = head(h)
                    o = m.ps[:, h % 2, HD * (h // 2):HD * (h // 2) + HD]
                    eng.matmul(o, m.kq_all[ks, 1, cs], m.state[ks, h // 2, :], start=True, stop=False)
                    ins = eng.matmul(o, m.a_qk[:, h, :], m.u_rows[:, HD * h:HD * h + HD], start=False, stop=True)
                ins.then_inc(tensor_done, pe.one("out"))
                eng.wait_ge(scalar_done, act.at("kend", i))
                for h in range(H):
                    e = HD * (h % 2)
                    ins = eng.matmul(m.ps[e:e + HD, 6, HD * (h // 2):HD * (h // 2) + HD], m.k_end_rows[:, HD * h:HD * h + HD],
                                     m.u_rows[:, HD * h:HD * h + HD], start=True, stop=True)
                ins.then_inc(tensor_done, pe.one("update"))

        @block.vector
        def _(eng):
            eng.sem_inc(vector_done, vec.credit)
            eng.memset(m.state[:, :, :], 0.0)
            eng.memset(m.xf[:, :, :], 0.0)
            eng.memset(m.a_qk[:, :, :], 0.0)
            eng.memset(m.au[R:R + 1, :], 1.0)
            eng.memset(m.drive[:, :, :], 0.0).then_inc(m.chain_v, 1)
            eng.wait_ge(m.chain_v, 1)
            with eng.Fori(0, NT) as i:
                u = m.mem[:, :, 1:P + 1].rearrange("p (c n) t -> p c n t", c=NP)[:, :, bass.ds(i, 1), :]
                eng.wait_ge(tensor_done, pe.before("beta", i))
                eng.wait_ge(pool_done, pool.before("push", i))
                eng.tensor_scalar(m.spk[:, :, :].unsqueeze(2), u, 1.0, None, ALU.is_gt).then_inc(vector_done, vec.one("spikes"))
                eng.wait_ge(tensor_done, pe.at("qsum", i))
                eng.tensor_scalar(m.norm[:, :], m.ps[:, 4:6, :].rearrange("p b c -> p (b c)"), 1e-19, None, ALU.max).then_inc(vector_done, vec.one("guard"))
                eng.wait_ge(tensor_done, pe.at("au", i))
                eng.tensor_scalar(m.au_x[:, :], m.ps[0:R, 3, 0:P], m.bau[:, 0:1], FLOOR, ALU.add, ALU.max).then_inc(vector_done, vec.one("au0"))
                eng.wait_ge(scalar_done, act.at("au_e", i))
                eng.tensor_scalar(m.au_e[:, :], m.au_e[:, :], 1.0, None, ALU.add).then_inc(vector_done, vec.one("au1"))
                eng.wait_ge(vector_done, vec.at("au1", i))
                eng.reciprocal(m.au_r[:, :], m.au_e[:, :]).then_inc(vector_done, vec.one("au2"))
                eng.wait_ge(vector_done, vec.at("au2", i))
                eng.tensor_tensor(m.au[0:R, :], m.au_x[:, :], m.au_r[:, :], ALU.mult).then_inc(vector_done, vec.one("au"))
                eng.wait_ge(tensor_done, pe.at("count", i))
                eng.tensor_scalar(m.active[:, :], m.ps[:, 7, :], 0.5, None, ALU.is_gt).then_inc(vector_done, vec.one("active"))
                eng.wait_ge(tensor_done, pe.at("drive_a", i))
                eng.wait_ge(pool_done, pool.at("push", i))
                eng.tensor_tensor(m.z[:, :], m.ps[:, 3, :], m.push[:, :, :].rearrange("p c t -> p (c t)"), ALU.add).then_inc(vector_done, vec.one("z"))
                eng.wait_ge(vector_done, vec.at("z", i))
                eng.tensor_scalar(m.z[:, :], m.z[:, :], MIN_LOG_GATE, None, ALU.max).then_inc(vector_done, vec.one("zfloor"))
                eng.wait_ge(tensor_done, pe.at("beta", i))
                eng.tensor_scalar(m.beta[:, :], m.ps[:, 6, :], FLOOR, None, ALU.max).then_inc(vector_done, vec.one("b0"))
                eng.wait_ge(scalar_done, act.at("z_ln", i))
                eng.wait_ge(vector_done, vec.at("active", i))
                eng.scalar_tensor_tensor(m.z[:, :], m.z[:, :], -1.0, m.active[:, :], ALU.mult, ALU.mult).then_inc(vector_done, vec.one("log_a"))
                eng.wait_ge(vector_done, vec.at("log_a", i))
                eng.tensor_tensor_scan(gf, m.scan_keep[:, :, :].rearrange("p c t -> p (c t)"), m.z[:, :], 0.0, ALU.mult, ALU.add).then_inc(vector_done, vec.one("G"))
                eng.wait_ge(scalar_done, act.at("beta_e", i))
                eng.tensor_scalar(m.beta[:, :], m.beta[:, :], 1.0, None, ALU.add).then_inc(vector_done, vec.one("b1"))
                eng.wait_ge(vector_done, vec.at("b1", i))
                eng.reciprocal(m.beta[:, :], m.beta[:, :]).then_inc(vector_done, vec.one("b2"))
                eng.wait_ge(vector_done, vec.at("b2", i))
                eng.tensor_tensor(m.beta[:, :], m.beta[:, :], m.active[:, :], ALU.mult).then_inc(vector_done, vec.one("b3"))
                eng.wait_ge(scalar_done, act.at("rt_n", i))
                eng.tensor_scalar(m.norm[:, :], m.norm[:, :], 1e-6, None, ALU.add).then_inc(vector_done, vec.one("n1"))
                eng.wait_ge(vector_done, vec.at("n1", i))
                eng.reciprocal(m.norm[:, :], m.norm[:, :]).then_inc(vector_done, vec.one("n2"))
                eng.wait_ge(vector_done, vec.at("n2", i))
                eng.tensor_tensor(kqf, kqf, m.norm[:, :], ALU.mult).then_inc(vector_done, vec.one("unit"))
                eng.wait_ge(vector_done, vec.at("unit", i))
                eng.wait_ge(pool_done, pool.before("km64", i))
                eng.tensor_tensor(m.beta_k[:, :], kq[:, 0, :], m.beta[:, :], ALU.mult).then_inc(vector_done, vec.one("beta_k"))
                eng.wait_ge(vector_done, vec.at("G", i))
                eng.wait_ge(scalar_done, act.before("lift_n", i))
                gb = gf.rearrange("p (b s) -> p b s", s=BASE)
                eng.tensor_tensor(mid.rearrange("p (b s) -> p b s", s=BASE), gb,
                                          bc(gb[:, :, BASE // 2 - 1:BASE // 2], [P, 512 // BASE, BASE]), ALU.subtract).then_inc(vector_done, vec.one("mid"))
                eng.wait_ge(tensor_done, pe.before("up64b", i))
                for s in UPPER:
                    gs, xs = halves(gf, s), halves(up_lift[s], s)
                    split = bc(gs[:, :, 0, s - 1:s], [P, 256 // s, s])
                    eng.tensor_tensor(xs[:, :, 0, :], split, gs[:, :, 0, :], ALU.subtract).then_inc(vector_done, vec.one(f"lo{s}"))
                    eng.tensor_tensor(xs[:, :, 1, :], gs[:, :, 1, :], split, ALU.subtract).then_inc(vector_done, vec.one(f"hi{s}"))
                eng.tensor_tensor(end_lift.rearrange("p (c t) -> p c t", t=P), bc(g3[:, :, P - 1:P], [P, NP, P]), g3, ALU.subtract).then_inc(vector_done, vec.one("toend"))
                eng.wait_ge(scalar_done, act.at("lift_p", i))
                eng.wait_ge(tensor_done, pe.before("base3", i))
                eng.tensor_tensor(m.kq_base[:, :, :], kq[:, :, :], bc(base_p.unsqueeze(1), [P, 2, 512]), ALU.mult).then_inc(vector_done, vec.one("kq_base"))
                eng.wait_ge(scalar_done, act.at("lift_up", i))
                for s in UPPER:
                    for n in range(2):
                        ins = eng.tensor_tensor(m.kq_up[s][:, n, :].rearrange("p (b s) -> p b s", s=s), halves(kq[:, n, :], s)[:, :, 1, :],
                                                halves(up_lift[s], s)[:, :, 1, :], ALU.mult)
                    ins.then_inc(vector_done, vec.one(f"kq{s}"))
                eng.wait_ge(scalar_done, act.at("lift_all", i))
                eng.wait_ge(tensor_done, pe.before("out", i))
                eng.tensor_tensor(m.kq_all[:, :, :], kq[:, :, :], bc(all_lift.unsqueeze(1), [P, 2, 512]), ALU.mult).then_inc(vector_done, vec.one("kq_all"))
                eng.wait_ge(tensor_done, pe.before("kend", i))
                eng.tensor_tensor(m.k_end[:, :], m.beta_k[:, :], end_lift, ALU.mult).then_inc(vector_done, vec.one("k_end"))
                for n in range(4):
                    eng.wait_ge(tensor_done, pe.at(f"base{n}", i))
                    eng.memset(m.wait_word[:, n:n + 1], 0.0)
                    ps = m.ps[:, n, :].rearrange("p (h a t) -> p h a t", h=2, a=2)
                    hs = slice(4 * (n // 2) + n % 2, 4 * (n // 2) + 4, 2)
                    for s in LEVELS[:3]:
                        eng.copy_predicated(head_halves(bt[s], s, hs, 1), mask_of(s, 2),
                                            ps[:, :, 0, :].rearrange("p h (b two s) -> p h b two s", two=2, s=s)[:, :, :, 1, :])
                    eng.copy_predicated(m.a_qk[:, hs, :], bc(m.mask[:, 0:P].unsqueeze(1), [P, 2, P]), ps[:, :, 1, :]).then_inc(vector_done, vec.one(f"base{n}"))
                for s in UPPER:
                    at = {8: 4, 16: 6, 32: 0, 64: 2}[s]
                    for n, x in enumerate(HALVES):
                        eng.wait_ge(tensor_done, pe.at(f"up{s}{x}", i))
                        ps = m.ps[:, at + n, :].rearrange("p (h a b s) -> p h a b s", h=4, a=2, s=s)
                        hs = slice(n, H, 2)
                        eng.wait_ge(vector_done, vec.at("base3" if s == 8 else f"up{s // 2}{x}", i))
                        if s == 64:
                            q = slice(0, HD)
                            eng.tensor_copy(bt[s][q, hs, HD:P], ps[q, :, 0, 0, :])
                            ins = eng.tensor_copy(m.a_qk[q, hs, HD:P], ps[q, :, 1, 0, :])
                        else:
                            eng.tensor_tensor(head_halves(bt[s], s, hs, 1), ps[:, :, 0, :, :], mask_of(s, 4, m.maskf), ALU.mult)
                            ins = eng.copy_predicated(head_halves(m.a_qk, s, hs, 1), mask_of(s, 4), ps[:, :, 1, :, :])
                        ins.then_inc(vector_done, vec.one(f"up{s}{x}"))
                    if s == 8:
                        eng.wait_ge(tensor_done, pe.before("solved", i))
                        eng.scalar_tensor_tensor(m.tt[:, :, :], bt[1][:, :, :], -1.0, bc(m.ident[:, :].unsqueeze(1), [P, H, P]),
                                                         ALU.mult, ALU.add).then_inc(vector_done, vec.one("tt"))
                for s in LEVELS[1:]:
                    for n, x in enumerate(HALVES):
                        hs = slice(4 * n, 4 * n + 4)
                        if s < 64:
                            eng.wait_ge(tensor_done, pe.at(f"TX{x}{s}", i))
                            v = halves(m.tm[:, hs, :].rearrange("p h t -> p (h t)"), s)[:, :, 0, :]
                            if s > 2:
                                eng.wait_ge(vector_done, vec.at(f"TX{x}{s // 2}", i))
                            eng.tensor_tensor(v, v, m.ps[:, 2 + n, 0:256].rearrange("p (b s) -> p b s", s=s), ALU.subtract).then_inc(vector_done, vec.one(f"TX{x}{s}"))
                        eng.wait_ge(tensor_done, pe.at(f"XT{x}{s}", i))
                        v = halves(m.tt[:, hs, :].rearrange("p h t -> p (h t)"), s)[:, :, 1, :]
                        eng.wait_ge(vector_done, vec.at(f"XT{x}{s // 2}" if s > 2 else "tt", i))
                        eng.scalar_tensor_tensor(v, m.ps[:, n, 0:256].rearrange("p (b s) -> p b s", s=s),
                                                         m.first_neg[:, LEVELS.index(s):LEVELS.index(s) + 1], v, ALU.mult, ALU.add).then_inc(vector_done, vec.one(f"XT{x}{s}"))
                eng.wait_ge(tensor_done, pe.at("seen", i))
                eng.wait_ge(scalar_done, act.at("v", i))
                for e in range(2):
                    parity = [t.rearrange("p (c e v) -> p c e v", c=NP, e=2)[:, :, e, :] for t in (m.rest, m.v[:, :])]
                    ins = eng.tensor_tensor(parity[0], parity[1], m.ps[:, 2 + e, 0:256].rearrange("p (c v) -> p c v", c=NP), ALU.subtract)
                ins.then_inc(vector_done, vec.one("rest"))
                eng.wait_ge(tensor_done, pe.at("out", i))
                eng.wait_ge(scalar_done, act.at("last", i))
                eng.tensor_tensor(m.state[:, :, :], m.state[:, :, :], bc(m.last[:, :].unsqueeze(2), [P, NP, HD]), ALU.mult).then_inc(vector_done, vec.one("keep"))
                eng.wait_ge(tensor_done, pe.at("update", i))
                eng.wait_ge(vector_done, vec.at("keep", i))
                eng.tensor_tensor(m.state[:, :, :], m.state[:, :, :], m.ps[:, 6, 0:256].rearrange("p (c v) -> p c v", c=NP), ALU.add).then_inc(vector_done, vec.one("update"))


def allocate(nc, ctx, m):
    def sb(name, shape, dt=F32):
        return ctx.enter_context(nc.sbuf_tensor(name, shape, dt))

    m.ps = ctx.enter_context(nc.psum_tensor("ps", [P, 8, 512], F32))
    m.chain_v = ctx.enter_context(nc.semaphore("blocks_cleared"))
    m.x = sb("x", [P, NT, D])
    m.h = sb("h", [P, NT, D])
    m.hh = sb("hh", [P, T])
    m.drive = sb("drive", [P, NP, T])
    m.mem = sb("mem", [P, NP * NT, P + 1])
    m.stats = sb("stats", [P, 96])
    m.c = sb("c", [P, 2]);
    m.mod_rows = sb("mod_rows", [P, 2, 6 * D]); m.mod_cols = sb("mod_cols", [P, 2, 6]); m.eps = sb("eps", [P, 2])
    m.conv_w = sb("conv_w", [P, KW]); m.conv_b = sb("conv_b", [P, 1]); m.norm_in = sb("norm_in", [P, 1])
    m.wq = sb("wq", [P, 512]); m.wk = sb("wk", [P, 512]); m.wv = sb("wv", [P, 512]);
    m.wau = sb("wau", [P, R]); m.bau = sb("bau", [R, 1]); m.wad = sb("wad", [R + 1, 512])
    m.aspike = sb("aspike", [P, NP]); m.bspike = sb("bspike", [P, NP]); m.wbeta = sb("wbeta", [P, H]); m.bbeta = sb("bbeta", [1, H])
    m.beta_w = sb("beta_w", [P, H, HD]); m.beta_b = sb("beta_b", [1, H, HD]); m.beta_s = sb("beta_s", [P, NP, P])
    m.ident = sb("ident", [P, P]); m.ones = sb("ones", [P, P]); m.bd = sb("bd", [P, P])
    n = P + HD * len(LEVELS)
    m.maskf = sb("maskf", [P, n]); m.mask = sb("mask", [P, n], U8); m.first_neg = sb("first_neg", [P, len(LEVELS)])
    m.scan_keep = sb("scan_keep", [P, NP, P])
    m.kept = sb("kept", [P, NP * NT]); m.diff = sb("diff", [P, NP, NT]); m.wide = sb("wide", [P, 32]); m.wide_t = sb("wide_t", [P, 32]); m.flag = sb("flag", [P, 32], I32)


def setup_tensors(nc, ctx, m):
    def sb(name, shape, dt=F32):
        return ctx.enter_context(nc.sbuf_tensor("setup_" + name, shape, dt))

    m.arena = sb("arena", [P, 6144])
    m.hist = sb("hist", [P, KW - 1 + T])
    m.c_wide = sb("c_wide", [P, 2, P])
    m.wmod = sb("wmod", [P, 2, 6 * D])
    m.scratch = sb("scratch", [P, 1024])
    m.wspike = sb("wspike", [P, 512])


def delta_tensors(nc, ctx, m):
    def sb(name, shape, dt=F32):
        return ctx.enter_context(nc.sbuf_tensor("delta_" + name, shape, dt))

    m.arena = sb("arena", [P, 5632])
    m.state = sb("state", [P, NP, HD]); m.wait_word = sb("wait_word", [P, 4]); m.last = sb("last", [P, NP])
    m.hh_tile = sb("hh_tile", [P, P]); m.kq = sb("kq", [P, 2, 512]); m.v = sb("v", [P, 512]); m.norm = sb("norm", [P, 1024])
    m.au_e = sb("au_e", [R, P]); m.au_x = sb("au_x", [R, P]); m.au_r = sb("au_r", [R, P]); m.au = sb("au", [R + 1, P])
    m.spk = sb("spk", [P, NP, P]); m.push = sb("push", [P, NP, P]); m.active = sb("active", [P, 512]); m.z = sb("z", [P, 512]); m.G = sb("G", [P, NP, P])
    m.beta = sb("beta", [P, 512]); m.beta_k = sb("beta_k", [P, 512])
    m.km = sb("km", [P, 512]); m.kq_base = sb("kq_base", [P, 2, 512]); m.kq_all = sb("kq_all", [P, 2, 512]); m.k_end = sb("k_end", [P, 512])
    m.kq_up = {s: sb(f"kq_up{s}", [P, 2, 256]) for s in UPPER}
    m.a_qk = sb("a_qk", [P, H, P]); m.tt = sb("tt", [P, H, P]); m.tm = sb("tm", [P, H, P]); m.xf = sb("xf", [P, H, P])
    spare = m.drive[:, :, :].rearrange("p c t -> p (c t)")[:, len(LEVELS) * H * P:]
    m.k_end_rows, m.rest = spare[:, 0:512], spare[:, 512:1024]
    m.u_rows = sb("u_rows", [P, 512])


def sources(m, ins):
    def col(v, n):
        return v.rearrange("(c p) -> p c", p=n)

    g = {k[8:]: v for k, v in ins.items() if k.startswith("L0_attn_")}
    x = g["x"].rearrange("a (n p) d -> p (a n) d", p=P)
    mods = [(m.wmod[:, l, :], ins[f"L{l}_wmod"]) for l in range(2)] + \
           [(m.c[:, l:l + 1], ins[f"L{l}_c"].rearrange("a p -> p a")) for l in range(2)]
    weights = [
        (m.conv_w[:, :], g["conv_w"].rearrange("p a k -> p (a k)")), (m.conv_b[:, :], col(g["conv_b"], P)),
        (m.norm_in[:, :], col(g["norm_in_w"], P)), (m.wspike[:, :], g["Wspike"]),
        (m.wk[:, :], g["Wk"]), (m.wq[:, :], g["Wq"]), (m.wv[:, :], g["Wv"]),
        (m.wau[:, :], g["Wau"]), (m.bau[:, :], col(g["bau"], R)), (m.wad[0:R, :], g["Wad"]),
        (m.wad[R:R + 1, :], g["bad"].rearrange("(a n) -> a n", a=1)),
        (m.aspike[:, :], g["alpha_spike"]),
        (m.bspike[:, :], g["beta_spike"]),
        (m.wbeta[:, :], g["Wbeta"]), (m.bbeta[:, :], g["bbeta"].rearrange("(a n) -> a n", a=1)),
    ]
    return x, mods, weights


GROUP = 4
GT = GROUP * P
NH1, D1, WIN = 16, 8, 32
NW = P // WIN
NG = 4
QS = float(D1) ** -0.5
NEG = -1e30


def post_tensors(nc, ctx, m):
    def sb(name, shape, dt=F32):
        return ctx.enter_context(nc.sbuf_tensor("post_" + name, shape, dt))

    m.wo = sb("wo", [P, NP, D]); m.head_norm = sb("head_norm", [P, NP]); m.wu1 = sb("wu1", [P, R]); m.bu1 = sb("bu1", [R, 1])
    m.wu2 = sb("wu2", [R + 1, D]); m.ff_norm = sb("ff_norm", [P, 1]); m.wff1 = sb("wff1", [P, FF]); m.wff3 = sb("wff3", [P, FF]); m.wff2 = sb("wff2", [P, NF, D])
    m.w1 = sb("w1", [P, FF]); m.b1 = sb("b1", [P, NF]); m.w2 = sb("w2", [P, NF, D]); m.b2 = sb("b2", [1, D])
    m.wq1 = sb("wq1", [P, D]); m.wk1 = sb("wk1", [P, D]); m.wv1 = sb("wv1", [P, D]); m.wo1 = sb("wo1", [P, D])
    m.gamma = sb("gamma", [P, 1]); m.beta1 = sb("beta1", [P, 1])
    m.fc1_q = sb("fc1_q", [P, FF], I32); m.fc1 = sb("fc1", [P, FF]); m.fc1_s = sb("fc1_s", [1, FF]); m.fc1_b = sb("fc1_b", [P, NF])
    m.fc2_q = sb("fc2_q", [P, NF, D], I32); m.fc2 = sb("fc2", [P, NF, D]); m.fc2_s = sb("fc2_s", [1, FF]); m.fc2_b = sb("fc2_b", [1, D])
    m.st = sb("st", [P, 160])
    free = m.drive[:, :, :]
    m.work, m.work2 = free[:, 0, :], free[:, 1, :]
    m.yt = free[:, 2, :].rearrange("p (c t) -> p c t", t=GT)
    m.hid = free[:, 3, :].rearrange("p (c t) -> p c t", t=GT)
    m.xc = sb("xc", [P, GROUP, D]); m.y1 = sb("y1", [P, GROUP, D]); m.h_in = sb("h_in", [P, GROUP, D]); m.xs = sb("xs", [P, GROUP, D]); m.gate = sb("gate", [P, GT]); m.hT = sb("hT", [P, GT]); m.gu = sb("gu", [R + 1, GT]); m.gu_e = sb("gu_e", [R, GT]); m.gu_x = sb("gu_x", [R, GT])
    m.hid_e = sb("hid_e", [P, 2, GT])
    m.hc = sb("hc", [P, WIN + GT]); m.qc = sb("qc", [P, GT]); m.kc = sb("kc", [P, WIN + GT]); m.v2 = sb("v2", [P, GT // 64, D])
    m.head_of = sb("head_of", [P, NH1]); m.head_scaled = sb("head_scaled", [P, NH1]); m.band = sb("band", [P, NW, 2 * WIN])
    m.sc = sb("sc", [P, 16, 64]); m.pt = sb("pt", [P, 8, P]); m.ao = sb("ao", [P, GT]); m.mx = sb("mx", [P, 16]); m.sm = sb("sm", [P, 16])


def post_sources(m, ins):
    def col(v):
        return v.rearrange("(c p) -> p c", p=P)

    def row(v):
        return v.rearrange("(a n) -> a n", a=1)

    g = {k[8:]: v for k, v in ins.items() if k.startswith("L0_attn_")}
    f = {k[7:]: v for k, v in ins.items() if k.startswith("L0_ffn_")}
    l = {k[3:]: v for k, v in ins.items() if k.startswith("L1_")}
    return [
        (m.wo[:, :, :], g["Wo"].rearrange("(c p) d -> p c d", p=P)), (m.head_norm[:, :], g["head_norm_w"]),
        (m.wu1[:, :], g["Wu1"]), (m.bu1[:, :], g["bu1"].rearrange("(p a) -> p a", a=1)),
        (m.wu2[0:R, :], g["Wu2"]), (m.wu2[R:R + 1, :], row(g["bu2"])),
        (m.ff_norm[:, :], col(g["ff_norm_w"])), (m.wff1[:, :], g["Wff1"]), (m.wff3[:, :], g["Wff3"]),
        (m.wff2[:, :, :], g["Wff2"].rearrange("(c p) d -> p c d", p=P)),
        (m.w1[:, :], f["w1"]), (m.b1[:, :], f["b1"]), (m.w2[:, :, :], f["w2"].rearrange("(c p) d -> p c d", p=P)),
        (m.b2[:, :], row(f["b2"])),
        (m.wq1[:, :], l["attn_wq"]), (m.wk1[:, :], l["attn_wk"]), (m.wv1[:, :], l["attn_wv"]), (m.wo1[:, :], l["attn_wo"]),
        (m.gamma[:, :], col(l["ffn_ln_gamma"])), (m.beta1[:, :], col(l["ffn_ln_beta"])),
        (m.fc1_q[:, :], l["ffn_fc1_q"]), (m.fc1_s[:, :], l["ffn_fc1_scales"]), (m.fc1_b[:, :], l["ffn_fc1_bias"]),
        (m.fc2_q[:, :, :], l["ffn_fc2_q"].rearrange("(c p) d -> p c d", p=P)),
        (m.fc2_s[:, :], l["ffn_fc2_scales"].rearrange("(a c) d -> a (c d)", a=1)), (m.fc2_b[:, :], row(l["ffn_fc2_bias"])),
    ]


def post_phase(nc, m, ins, out):
    with ExitStack() as ctx:
        post_tensors(nc, ctx, m)
        loads = post_sources(m, ins)

        def steps(names, ahead=0):
            return Steps(names.split(), rounds_ahead=ahead)

        loaded = ctx.enter_context(nc.semaphore("post_weights_in"))
        stored = ctx.enter_context(nc.semaphore("stored"))

        def each(fmt, n):
            return " ".join(fmt.format(k) for k in range(n))

        def norm_vec(p):
            return f" {p}_sum {p}_mean {p}_cen {p}_var {p}_nrm"

        def norm_act(p):
            return f" {p}_sq {p}_ln {p}_r"

        pre_pool_done = ctx.enter_context(nc.semaphore("post_pool_setup_done"))
        pre_pool = steps("head band0 head_from head_upto band_lo band_hi")
        pre_vector_done = ctx.enter_context(nc.semaphore("post_vector_setup_done"))
        pre_vec = steps("scaled fc1_f fc2_f fc1_m fc2_m fc1_w fc2_w first")
        pre_tensor_done = ctx.enter_context(nc.semaphore("post_tensor_setup_done"))
        pre_pe = steps("scales1 scales2")
        vector_done = ctx.enter_context(nc.semaphore("post_vector_done"))
        vec = steps("x_in h_in y_var yn g0 g1 g2 gu s0 s1 s2 gated y1 zvar z " + each("a{0}", 4)
                    + " y2 y2g x1" + norm_vec("n1") + " x2m x2" + norm_vec("n2")
                    + " " + each("sc{0} mx{0} sub{0} sum{0} rec{0} prob{0} pick{0} fold{0} band{0}", GROUP)
                    + " hist x3m x3" + norm_vec("n3") + " h3m h3" + norm_vec("n4") + " "
                    + "zh zg x4", 1)
        scalar_done = ctx.enter_context(nc.semaphore("post_scalar_done"))
        act = steps("hT y_sq y_ln y_r g_e yt0 yt1 yt2 yt3 s_e z_sq z_ln z_r zT " + each("a{0}_e", 4)
                    + norm_act("n1") + " n1T " + each("gelu{0}", 4) + norm_act("n2")
                    + " n2T qc kc v2a v2b " + each("exp{0} pt{0}", GROUP)
                    + norm_act("n3") + norm_act("n4") + " n4T " + each("b{0}_e", 4), 1)
        tensor_done = ctx.enter_context(nc.semaphore("post_tensor_done"))
        pe = steps("hT g1 yT0 yT1 yT2 yT3 gate proj zT " + each("a{0}", 4) + " ff2 n1T "
                   + each("c{0}", 4) + " w2 n2T q k va vb " + each("sc{0} pt{0} pv{0}", GROUP)
                   + " wo n4T " + each("b{0}", 4) + " fc2", 1)
        pool_done = ctx.enter_context(nc.semaphore("post_pool_done"))
        pool = steps(each("qm{0}", GROUP), 1)
        st = m.st
        block = ctx.enter_context(nc.Block())
        flat = "p n d -> p (n d)"

        @block.sync
        def _(eng):
            for dst, src in loads:
                eng.dma_start(dst, src).then_inc(loaded, 16)
            o = out.rearrange("a (n p) d -> p (a n) d", p=P)
            with eng.Fori(0, NT // GROUP) as i:
                eng.wait_ge(vector_done, vec.at("x4", i))
                eng.dma_start(o[:, bass.ds(i * GROUP, GROUP), :], m.x[:, bass.ds(i * GROUP, GROUP), :]).then_inc(stored, 16)
            eng.wait_ge(stored, 16 * (NT // GROUP))

        @block.gpsimd
        def _(eng):
            eng.memset(m.head_of[:, :], 1.0).then_inc(pre_pool_done, pre_pool.one("head"))
            eng.wait_ge(pre_pool_done, pre_pool.at("head"))
            eng.memset(m.band[:, :, :], 0.0).then_inc(pre_pool_done, pre_pool.one("band0"))
            eng.wait_ge(pre_pool_done, pre_pool.at("band0"))
            eng.affine_select(out=m.head_of[:, :], in_=m.head_of[:, :], compare_op=ALU.is_ge, fill=0.0, base=0,
                                   pattern=[[-D1, NH1]], channel_multiplier=1).then_inc(pre_pool_done, pre_pool.one("head_from"))
            eng.wait_ge(pre_pool_done, pre_pool.at("head_from"))
            eng.affine_select(out=m.head_of[:, :], in_=m.head_of[:, :], compare_op=ALU.is_ge, fill=0.0, base=D1 - 1,
                                   pattern=[[D1, NH1]], channel_multiplier=-1).then_inc(pre_pool_done, pre_pool.one("head_upto"))
            eng.wait_ge(pre_pool_done, pre_pool.at("head_upto"))
            for a in range(4):
                v = m.band[WIN * a:WIN * a + WIN, :, :]
                ins_ = eng.affine_select(out=v, in_=v, compare_op=ALU.is_gt, fill=NEG, base=0,
                                         pattern=[[0, NW], [1, 2 * WIN]], channel_multiplier=-1)
            ins_.then_inc(pre_pool_done, pre_pool.one("band_lo"))
            eng.wait_ge(pre_pool_done, pre_pool.at("band_lo"))
            for a in range(4):
                v = m.band[WIN * a:WIN * a + WIN, :, :]
                ins_ = eng.affine_select(out=v, in_=v, compare_op=ALU.is_ge, fill=NEG, base=WIN,
                                         pattern=[[0, NW], [-1, 2 * WIN]], channel_multiplier=1)
            ins_.then_inc(pre_pool_done, pre_pool.one("band_hi"))
            eng.wait_ge(pre_pool_done, pre_pool.at("band_hi"))
            eng.wait_ge(pre_vector_done, pre_vec.at("first"))
            eng.sem_inc(pool_done, pool.credit)
            with eng.Fori(0, NT // GROUP) as i:
                for n in range(GROUP):
                    if n:
                        eng.wait_ge(tensor_done, pe.at(f"sc{n - 1}", i))
                    else:
                        eng.wait_ge(scalar_done, act.at("qc", i))
                    q = m.qc[:, P * n:P * n + P].rearrange("p (j q) -> p j q", q=WIN).unsqueeze(2)
                    eng.tensor_tensor(m.work2[:, :].rearrange("p (j h q) -> p j h q", h=NH1, q=WIN), bc(q, [P, NW, NH1, WIN]),
                                               bc(m.head_scaled[:, :].unsqueeze(1).unsqueeze(3), [P, NW, NH1, WIN]), ALU.mult).then_inc(pool_done, pool.one(f"qm{n}"))

        def group(t, i):
            return t[:, bass.ds(i * GROUP, GROUP), :]

        def y_group(i):
            return m.mem[:, :, 0:P].rearrange("p (c n) t -> p c n t", c=NP)[:, :, bass.ds(i * GROUP, GROUP), :]

        @block.scalar
        def _(eng):
            eng.sem_inc(scalar_done, act.credit)

            def norm(p, c, i, eps, width=D):
                eng.wait_ge(scalar_done, act.at(f"{p}_sq", i))
                eng.wait_ge(vector_done, vec.at({"y": "y_var", "z": "zvar"}.get(p, f"{p}_var"), i))
                eng.activation(c, c, ACT.Ln, scale=1.0 / width, bias=m.eps[:, eps:eps + 1]).then_inc(scalar_done, act.one(f"{p}_ln"))
                eng.wait_ge(scalar_done, act.at(f"{p}_ln", i))
                eng.activation(c, c, ACT.Exp, scale=-0.5).then_inc(scalar_done, act.one(f"{p}_r"))

            w512 = m.work[:, 0:GT]
            with eng.Fori(0, NT // GROUP) as i:
                eng.wait_ge(tensor_done, pe.at("hT", i))
                eng.activation(m.hT[:, :], m.ps[:, 4, :], ACT.Copy).then_inc(scalar_done, act.one("hT"))
                eng.activation(m.work[:, :].rearrange("p (c n t) -> p c n t", c=NP, n=GROUP), y_group(i), ACT.Square).then_inc(scalar_done, act.one("y_sq"))
                norm("y", st[:, 0:32], i, 1, HD)
                eng.wait_ge(vector_done, vec.at("g0", i))
                eng.activation(m.gu_e[:, :], m.gu_x[:, :], ACT.Exp, scale=-1.0).then_inc(scalar_done, act.one("g_e"))
                for c in range(NP):
                    eng.wait_ge(tensor_done, pe.at(f"yT{c}", i))
                    eng.activation(m.yt[:, c, :], m.ps[:, c, :], ACT.Copy, scale=m.head_norm[:, c:c + 1]).then_inc(scalar_done, act.one(f"yt{c}"))
                eng.wait_ge(vector_done, vec.at("s0", i))
                eng.activation(m.gate[:, :], m.gate[:, :], ACT.Exp, scale=-1.0).then_inc(scalar_done, act.one("s_e"))
                eng.wait_ge(vector_done, vec.at("y1", i))
                eng.activation(w512, m.y1[:, :, :].rearrange(flat), ACT.Square).then_inc(scalar_done, act.one("z_sq"))
                norm("z", st[:, 32:36], i, 1)
                eng.wait_ge(tensor_done, pe.at("zT", i))
                eng.activation(m.hT[:, :], m.ps[:, 4, :], ACT.Copy, scale=m.ff_norm[:, 0:1]).then_inc(scalar_done, act.one("zT"))
                for f in range(NF):
                    eng.wait_ge(tensor_done, pe.at(f"a{f}", i))
                    if f > 1:
                        eng.wait_ge(vector_done, vec.at(f"a{f - 2}", i))
                    eng.activation(m.hid_e[:, f % 2, :], m.ps[:, 2 * (f % 2), :], ACT.Silu).then_inc(scalar_done, act.one(f"a{f}_e"))

                def square(p):
                    eng.wait_ge(vector_done, vec.at(f"{p}_cen", i))
                    eng.activation(w512, m.xc[:, :, :].rearrange(flat), ACT.Square).then_inc(scalar_done, act.one(f"{p}_sq"))

                square("n1")
                norm("n1", st[:, 48:52], i, 0)
                eng.wait_ge(tensor_done, pe.at("n1T", i))
                eng.activation(m.hT[:, :], m.ps[:, 5, :], ACT.Identity, scale=m.mod_cols[:, 0, 4:5], bias=m.mod_cols[:, 0, 3:4]).then_inc(scalar_done, act.one("n1T"))
                for f in range(NF):
                    eng.wait_ge(tensor_done, pe.at(f"c{f}", i))
                    eng.activation(m.hid[:, f, :], m.ps[:, f, :], ACT.Gelu, bias=m.b1[:, f:f + 1]).then_inc(scalar_done, act.one(f"gelu{f}"))
                square("n2")
                norm("n2", st[:, 56:60], i, 0)
                eng.wait_ge(tensor_done, pe.at("n2T", i))
                eng.activation(m.hc[:, WIN:WIN + GT], m.ps[:, 6, :], ACT.Identity, scale=m.mod_cols[:, 1, 1:2], bias=m.mod_cols[:, 1, 0:1]).then_inc(scalar_done, act.one("n2T"))
                eng.wait_ge(tensor_done, pe.at("q", i))
                eng.activation(m.qc[:, :], m.ps[:, 0, :], ACT.Copy).then_inc(scalar_done, act.one("qc"))
                eng.wait_ge(tensor_done, pe.at("k", i))
                eng.activation(m.kc[:, WIN:WIN + GT], m.ps[:, 1, :], ACT.Copy).then_inc(scalar_done, act.one("kc"))
                for b, x in enumerate("ab"):
                    eng.wait_ge(tensor_done, pe.at(f"v{x}", i))
                    eng.activation(m.v2[:, 4 * b:4 * b + 4, :], m.ps[:, 2 + b, :].rearrange("p (w d) -> p w d", d=D), ACT.Copy).then_inc(scalar_done, act.one(f"v2{x}"))
                for n in range(GROUP):
                    eng.wait_ge(vector_done, vec.at(f"sub{n}", i))
                    eng.activation(m.sc[:, :, :], m.sc[:, :, :], ACT.Exp).then_inc(scalar_done, act.one(f"exp{n}"))
                    eng.wait_ge(tensor_done, pe.at(f"pt{n}", i))
                    eng.activation(m.pt[:, :, :].rearrange("p g t -> p (g t)"), m.ps[:, 2:4, :].rearrange("p b t -> p (b t)"), ACT.Copy).then_inc(scalar_done, act.one(f"pt{n}"))
                square("n3")
                norm("n3", st[:, 64:68], i, 0)
                square("n4")
                norm("n4", st[:, 72:76], i, 0)
                eng.wait_ge(tensor_done, pe.at("n4T", i))
                eng.activation(m.hT[:, :], m.ps[:, 5, :], ACT.Identity, scale=m.gamma[:, 0:1], bias=m.beta1[:, 0:1]).then_inc(scalar_done, act.one("n4T"))
                for f in range(NF):
                    eng.wait_ge(tensor_done, pe.at(f"b{f}", i))
                    eng.activation(m.hid[:, f, :], m.ps[:, f, :], ACT.Silu, bias=m.fc1_b[:, f:f + 1]).then_inc(scalar_done, act.one(f"b{f}_e"))

        @block.tensor
        def _(eng):
            eng.wait_ge(loaded, 16 * len(loads))
            eng.matmul(m.ps[:, 0, :], m.ones[0:1, :], m.fc1_s[:, :], start=True, stop=True).then_inc(pre_tensor_done, pre_pe.one("scales1"))
            eng.matmul(m.ps[:, 1, :], m.ones[0:1, :], m.fc2_s[:, :], start=True, stop=True).then_inc(pre_tensor_done, pre_pe.one("scales2"))
            eng.wait_ge(pre_vector_done, pre_vec.at("first"))
            eng.sem_inc(tensor_done, pe.credit)

            def rows_to_columns(bank, src3, name):
                for n in range(GROUP):
                    ins_ = eng.transpose(m.ps[:, bank, P * n:P * n + P], src3[:, n, :], m.ident[:, :])
                ins_.then_inc(tensor_done, pe.one(name))

            def hidden(bank, w, src, name):
                eng.matmul(m.ps[:, bank, :], w, src, start=True, stop=True).then_inc(tensor_done, pe.one(name))

            def back_to_rows(bank, src, w, name, bias=None):
                for n in range(GROUP):
                    o = m.ps[:, bank, P * n:P * n + P]
                    for f in range(NF):
                        ins_ = eng.matmul(o, src[:, f, P * n:P * n + P], w[:, f, :], start=(f == 0), stop=(f == NF - 1 and bias is None))
                    if bias is not None:
                        ins_ = eng.matmul(o, m.ones[0:1, :], bias, start=False, stop=True)
                ins_.then_inc(tensor_done, pe.one(name))

            with eng.Fori(0, NT // GROUP) as i:
                eng.wait_ge(vector_done, vec.at("h_in", i))
                rows_to_columns(4, m.h_in, "hT")
                eng.wait_ge(scalar_done, act.at("hT", i))
                eng.matmul(m.ps[0:R, 5, :], m.wu1[:, :], m.hT[:, :], start=True, stop=True).then_inc(tensor_done, pe.one("g1"))
                eng.wait_ge(vector_done, vec.at("yn", i))
                for c in range(NP):
                    rows_to_columns(c, m.work2[:, :].rearrange("p (c n t) -> p c n t", c=NP, n=GROUP)[:, c, :, :], f"yT{c}")
                eng.wait_ge(vector_done, vec.at("gu", i))
                for n in range(GROUP):
                    ins_ = eng.matmul(m.ps[:, 6, P * n:P * n + P], m.gu[:, P * n:P * n + P], m.wu2[:, :], start=True, stop=True)
                ins_.then_inc(tensor_done, pe.one("gate"))
                eng.wait_ge(scalar_done, act.at("yt3", i))
                back_to_rows(7, m.yt, m.wo, "proj")
                eng.wait_ge(vector_done, vec.at("z", i))
                rows_to_columns(4, m.xc, "zT")
                eng.wait_ge(scalar_done, act.at("zT", i))
                for f in range(NF):
                    if f >= 2:
                        eng.wait_ge(vector_done, vec.at(f"a{f - 2}", i))
                    eng.matmul(m.ps[:, 2 * (f % 2), :], m.wff1[:, P * f:P * f + P], m.hT[:, :], start=True, stop=True)
                    hidden(2 * (f % 2) + 1, m.wff3[:, P * f:P * f + P], m.hT[:, :], f"a{f}")
                eng.wait_ge(vector_done, vec.at("a3", i))
                back_to_rows(4, m.hid, m.wff2, "ff2")
                eng.wait_ge(vector_done, vec.at("n1_nrm", i))
                rows_to_columns(5, m.xc, "n1T")
                eng.wait_ge(scalar_done, act.at("n1T", i))
                for f in range(NF):
                    hidden(f, m.w1[:, P * f:P * f + P], m.hT[:, :], f"c{f}")
                eng.wait_ge(scalar_done, act.at("gelu3", i))
                back_to_rows(4, m.hid, m.w2, "w2", m.b2[:, :])
                eng.wait_ge(vector_done, vec.at("n2_nrm", i))
                rows_to_columns(6, m.xc, "n2T")
                eng.wait_ge(scalar_done, act.at("n2T", i))
                hidden(0, m.wq1[:, :], m.hc[:, WIN:WIN + GT], "q")
                hidden(1, m.wk1[:, :], m.hc[:, WIN:WIN + GT], "k")
                for b, x in enumerate("ab"):
                    for w in range(8):
                        win = 8 * b + w
                        e = 64 * (w % 2)
                        ins_ = eng.matmul(m.ps[e:e + 64, 2 + b, P * (w // 2):P * (w // 2) + P], m.hc[:, WIN * win:WIN * win + 64], m.wv1[:, :], start=True, stop=True)
                    ins_.then_inc(tensor_done, pe.one(f"v{x}"))
                eng.wait_ge(scalar_done, act.at("v2b", i))
                for n in range(GROUP):
                    eng.wait_ge(pool_done, pool.at(f"qm{n}", i))
                    if n:
                        eng.wait_ge(vector_done, vec.at(f"fold{n - 1}", i))
                    for j in range(NW):
                        for g in range(NG):
                            k0 = P * n + WIN * j
                            ins_ = eng.matmul(m.ps[:, j // 2, P * g + 64 * (j % 2):P * g + 64 * (j % 2) + 64],
                                              m.work2[:, 512 * j + P * g:512 * j + P * g + P], m.kc[:, k0:k0 + 64], start=True, stop=True)
                    ins_.then_inc(tensor_done, pe.one(f"sc{n}"))
                    eng.wait_ge(vector_done, vec.at(f"prob{n}", i))
                    s4 = m.sc[:, :, :].rearrange("p (a g j) k -> p a g (j k)", a=2, j=2)
                    for a in range(2):
                        for g in range(NG):
                            ins_ = eng.transpose(m.ps[:, 2 + a, P * g:P * g + P], s4[:, a, g, :], m.ident[:, :])
                    ins_.then_inc(tensor_done, pe.one(f"pt{n}"))
                    eng.wait_ge(scalar_done, act.at(f"pt{n}", i))
                    for j in range(NW):
                        e = 64 * (j % 2)
                        ins_ = eng.matmul(m.ps[:, 4 + j, :], m.v2[e:e + 64, 2 * n + j // 2, :],
                                          m.pt[e:e + 64, 4 * (j // 2):4 * (j // 2) + 4, :].rearrange("p g t -> p (g t)"), start=True, stop=True)
                    ins_.then_inc(tensor_done, pe.one(f"pv{n}"))
                eng.wait_ge(vector_done, vec.at(f"fold{GROUP - 1}", i))
                for n in range(GROUP):
                    ins_ = eng.matmul(m.ps[:, 4, P * n:P * n + P], m.ao[:, P * n:P * n + P], m.wo1[:, :], start=True, stop=True)
                ins_.then_inc(tensor_done, pe.one("wo"))
                eng.wait_ge(vector_done, vec.at("n4_nrm", i))
                rows_to_columns(5, m.xc, "n4T")
                eng.wait_ge(scalar_done, act.at("n4T", i))
                for f in range(NF):
                    hidden(f, m.fc1[:, P * f:P * f + P], m.hT[:, :], f"b{f}")
                eng.wait_ge(scalar_done, act.at("b3_e", i))
                back_to_rows(4, m.hid, m.fc2, "fc2", m.fc2_b[:, :])

        @block.vector
        def _(eng):
            eng.wait_ge(loaded, 16 * len(loads))
            eng.wait_ge(pre_pool_done, pre_pool.at("band_hi"))
            eng.tensor_scalar(m.head_scaled[:, :], m.head_of[:, :], QS, None, ALU.mult).then_inc(pre_vector_done, pre_vec.one("scaled"))
            fc2, fc2q = (t[:, :, :].rearrange("p c d -> p (c d)") for t in (m.fc2, m.fc2_q))
            eng.tensor_copy(m.fc1[:, :], m.fc1_q[:, :]).then_inc(pre_vector_done, pre_vec.one("fc1_f"))
            eng.tensor_copy(fc2, fc2q).then_inc(pre_vector_done, pre_vec.one("fc2_f"))
            eng.wait_ge(pre_vector_done, pre_vec.at("fc2_f"))
            eng.tensor_scalar(m.fc1[:, :], m.fc1[:, :], -128.0, None, ALU.add).then_inc(pre_vector_done, pre_vec.one("fc1_m"))
            eng.tensor_scalar(fc2, fc2, -128.0, None, ALU.add).then_inc(pre_vector_done, pre_vec.one("fc2_m"))
            eng.wait_ge(pre_vector_done, pre_vec.at("fc2_m"))
            eng.wait_ge(pre_tensor_done, pre_pe.at("scales2"))
            eng.tensor_tensor(m.fc1[:, :], m.fc1[:, :], m.ps[:, 0, :], ALU.mult).then_inc(pre_vector_done, pre_vec.one("fc1_w"))
            eng.tensor_tensor(fc2, fc2, m.ps[:, 1, :], ALU.mult).then_inc(pre_vector_done, pre_vec.one("fc2_w"))
            eng.memset(m.gu[R:R + 1, :], 1.0)
            eng.memset(m.hc[:, 0:WIN], 0.0)
            eng.memset(m.kc[:, 0:WIN], 0.0)
            eng.memset(m.band[:, 0, 0:WIN], NEG).then_inc(pre_vector_done, pre_vec.one("first"))
            eng.wait_ge(pre_vector_done, pre_vec.at("first"))
            eng.sem_inc(vector_done, vec.credit)
            w3 = m.work[:, 0:GT].rearrange("p (n d) -> p n d", d=D)

            with eng.Fori(0, NT // GROUP) as i:
                xs = m.xs[:, :, :]

                def bank3(b):
                    return m.ps[:, b, :].rearrange("p (n d) -> p n d", d=D)

                def mod_row(l, k):
                    return bc(m.mod_rows[:, l:l + 1, D * k:D * k + D], [P, GROUP, D])

                def norm(p, src, c):
                    mean, r = st[:, c + 4:c + 8], st[:, c:c + 4]
                    eng.tensor_reduce(mean, src, AX, ALU.add).then_inc(vector_done, vec.one(f"{p}_sum"))
                    eng.wait_ge(vector_done, vec.at(f"{p}_sum", i))
                    eng.tensor_scalar(mean, mean, -1.0 / D, None, ALU.mult).then_inc(vector_done, vec.one(f"{p}_mean"))
                    eng.wait_ge(vector_done, vec.at(f"{p}_mean", i))
                    eng.tensor_tensor(m.xc[:, :, :], src, bc(mean.unsqueeze(2), [P, GROUP, D]), ALU.add).then_inc(vector_done, vec.one(f"{p}_cen"))
                    eng.wait_ge(scalar_done, act.at(f"{p}_sq", i))
                    eng.tensor_reduce(r, w3, AX, ALU.add).then_inc(vector_done, vec.one(f"{p}_var"))
                    eng.wait_ge(scalar_done, act.at(f"{p}_r", i))
                    eng.tensor_tensor(m.xc[:, :, :], m.xc[:, :, :], bc(r.unsqueeze(2), [P, GROUP, D]), ALU.mult).then_inc(vector_done, vec.one(f"{p}_nrm"))

                eng.wait_ge(vector_done, vec.before("x4", i))
                eng.tensor_copy(xs, group(m.x, i)).then_inc(vector_done, vec.one("x_in"))
                eng.tensor_copy(m.h_in[:, :, :], group(m.h, i)).then_inc(vector_done, vec.one("h_in"))
                eng.wait_ge(scalar_done, act.at("y_sq", i))
                eng.tensor_reduce(st[:, 0:32], m.work[:, :].rearrange("p (g v) -> p g v", v=HD), AX, ALU.add).then_inc(vector_done, vec.one("y_var"))
                eng.wait_ge(scalar_done, act.at("y_r", i))
                for c in range(NP):
                    yc = m.mem[:, :, 0:P].rearrange("p (c n) t -> p c n t", c=NP)[:, c, bass.ds(i * GROUP, GROUP), :]
                    ins_ = eng.tensor_tensor(m.work2[:, 512 * c:512 * c + 512].rearrange("p (n e v) -> p n e v", n=GROUP, e=2),
                                             yc.rearrange("p n (e v) -> p n e v", e=2),
                                             bc(st[:, 8 * c:8 * c + 8].rearrange("p (n e) -> p n e", e=2).unsqueeze(3), [P, GROUP, 2, HD]), ALU.mult)
                ins_.then_inc(vector_done, vec.one("yn"))
                eng.wait_ge(tensor_done, pe.at("g1", i))
                eng.tensor_scalar(m.gu_x[:, :], m.ps[0:R, 5, :], m.bu1[:, 0:1], FLOOR, ALU.add, ALU.max).then_inc(vector_done, vec.one("g0"))
                eng.wait_ge(scalar_done, act.at("g_e", i))
                eng.tensor_scalar(m.gu_e[:, :], m.gu_e[:, :], 1.0, None, ALU.add).then_inc(vector_done, vec.one("g1"))
                eng.wait_ge(vector_done, vec.at("g1", i))
                eng.reciprocal(m.gu_e[:, :], m.gu_e[:, :]).then_inc(vector_done, vec.one("g2"))
                eng.wait_ge(vector_done, vec.at("g2", i))
                eng.tensor_tensor(m.gu[0:R, :], m.gu_x[:, :], m.gu_e[:, :], ALU.mult).then_inc(vector_done, vec.one("gu"))
                eng.wait_ge(tensor_done, pe.at("gate", i))
                eng.tensor_scalar(m.gate[:, :], m.ps[:, 6, :], FLOOR, None, ALU.max).then_inc(vector_done, vec.one("s0"))
                eng.wait_ge(scalar_done, act.at("s_e", i))
                eng.tensor_scalar(m.gate[:, :], m.gate[:, :], 1.0, None, ALU.add).then_inc(vector_done, vec.one("s1"))
                eng.wait_ge(vector_done, vec.at("s1", i))
                eng.reciprocal(m.gate[:, :], m.gate[:, :]).then_inc(vector_done, vec.one("s2"))
                eng.wait_ge(vector_done, vec.at("s2", i))
                eng.wait_ge(tensor_done, pe.at("proj", i))
                eng.tensor_tensor(m.gate[:, :], m.gate[:, :], m.ps[:, 7, :], ALU.mult).then_inc(vector_done, vec.one("gated"))
                eng.wait_ge(vector_done, vec.at("gated", i))
                eng.tensor_tensor(m.y1[:, :, :], m.gate[:, :].rearrange("p (n d) -> p n d", d=D), m.h_in[:, :, :], ALU.add).then_inc(vector_done, vec.one("y1"))
                eng.wait_ge(scalar_done, act.at("z_sq", i))
                eng.tensor_reduce(st[:, 32:36], w3, AX, ALU.add).then_inc(vector_done, vec.one("zvar"))
                eng.wait_ge(scalar_done, act.at("z_r", i))
                eng.tensor_tensor(m.xc[:, :, :], m.y1[:, :, :], bc(st[:, 32:36].unsqueeze(2), [P, GROUP, D]), ALU.mult).then_inc(vector_done, vec.one("z"))
                for f in range(NF):
                    eng.wait_ge(scalar_done, act.at(f"a{f}_e", i))
                    eng.tensor_tensor(m.hid[:, f, :], m.hid_e[:, f % 2, :], m.ps[:, 2 * (f % 2) + 1, :], ALU.mult).then_inc(vector_done, vec.one(f"a{f}"))
                eng.wait_ge(tensor_done, pe.at("ff2", i))
                eng.tensor_tensor(m.y1[:, :, :], m.y1[:, :, :], bank3(4), ALU.add).then_inc(vector_done, vec.one("y2"))
                eng.wait_ge(vector_done, vec.at("y2", i))
                eng.tensor_tensor(m.y1[:, :, :], m.y1[:, :, :], mod_row(0, 2), ALU.mult).then_inc(vector_done, vec.one("y2g"))
                eng.wait_ge(vector_done, vec.at("y2g", i))
                eng.tensor_tensor(xs, xs, m.y1[:, :, :], ALU.add).then_inc(vector_done, vec.one("x1"))
                eng.wait_ge(vector_done, vec.at("x1", i))
                norm("n1", xs, 48)
                eng.wait_ge(tensor_done, pe.at("w2", i))
                eng.tensor_tensor(m.y1[:, :, :], bank3(4), mod_row(0, 5), ALU.mult).then_inc(vector_done, vec.one("x2m"))
                eng.wait_ge(vector_done, vec.at("x2m", i))
                eng.tensor_tensor(xs, xs, m.y1[:, :, :], ALU.add).then_inc(vector_done, vec.one("x2"))
                eng.wait_ge(vector_done, vec.at("x2", i))
                norm("n2", xs, 56)
                for n in range(GROUP):
                    eng.wait_ge(tensor_done, pe.at(f"sc{n}", i))
                    band = bc(m.band[:, :, :].rearrange("p (a j) k -> p a (j k)", a=2).unsqueeze(2), [P, 2, NG, 4 * WIN])
                    eng.tensor_tensor(m.sc[:, :, :].rearrange("p (a g j) k -> p a g (j k)", a=2, j=2),
                                              m.ps[:, 0:2, :].rearrange("p a (g k) -> p a g k", g=NG), band, ALU.add).then_inc(vector_done, vec.one(f"sc{n}"))
                    eng.wait_ge(vector_done, vec.at(f"sc{n}", i))
                    eng.tensor_reduce(m.mx[:, :], m.sc[:, :, :], AX, ALU.max).then_inc(vector_done, vec.one(f"mx{n}"))
                    eng.wait_ge(vector_done, vec.at(f"mx{n}", i))
                    eng.tensor_tensor(m.sc[:, :, :], m.sc[:, :, :], bc(m.mx[:, :].unsqueeze(2), [P, 16, 64]), ALU.subtract).then_inc(vector_done, vec.one(f"sub{n}"))
                    eng.wait_ge(scalar_done, act.at(f"exp{n}", i))
                    eng.tensor_reduce(m.sm[:, :], m.sc[:, :, :], AX, ALU.add).then_inc(vector_done, vec.one(f"sum{n}"))
                    eng.wait_ge(vector_done, vec.at(f"sum{n}", i))
                    eng.reciprocal(m.sm[:, :], m.sm[:, :]).then_inc(vector_done, vec.one(f"rec{n}"))
                    eng.wait_ge(vector_done, vec.at(f"rec{n}", i))
                    eng.tensor_tensor(m.sc[:, :, :], m.sc[:, :, :], bc(m.sm[:, :].unsqueeze(2), [P, 16, 64]), ALU.mult).then_inc(vector_done, vec.one(f"prob{n}"))
                    eng.wait_ge(tensor_done, pe.at(f"pv{n}", i))
                    own = bc(m.head_of[:, :].unsqueeze(1).unsqueeze(3), [P, NW, NH1, WIN])
                    w4 = m.work[:, :].rearrange("p (j h q) -> p j h q", h=NH1, q=WIN)
                    eng.tensor_tensor(w4, m.ps[:, 4:8, :].rearrange("p j (h q) -> p j h q", q=WIN), own, ALU.mult).then_inc(vector_done, vec.one(f"pick{n}"))
                    eng.wait_ge(vector_done, vec.at(f"pick{n}", i))
                    eng.tensor_reduce(m.ao[:, P * n:P * n + P].rearrange("p (j q) -> p j q", q=WIN),
                                              m.work[:, :].rearrange("p (j h q) -> p j q h", h=NH1, q=WIN), AX, ALU.add).then_inc(vector_done, vec.one(f"fold{n}"))
                    eng.tensor_copy(m.band[:, 0, :], m.band[:, 1, :]).then_inc(vector_done, vec.one(f"band{n}"))
                    eng.wait_ge(vector_done, vec.at(f"band{n}", i))
                eng.tensor_copy(m.hc[:, 0:WIN], m.hc[:, GT:GT + WIN])
                eng.tensor_copy(m.kc[:, 0:WIN], m.kc[:, GT:GT + WIN]).then_inc(vector_done, vec.one("hist"))
                eng.wait_ge(tensor_done, pe.at("wo", i))
                eng.tensor_tensor(m.y1[:, :, :], bank3(4), mod_row(1, 2), ALU.mult).then_inc(vector_done, vec.one("x3m"))
                eng.wait_ge(vector_done, vec.at("x3m", i))
                eng.tensor_tensor(xs, xs, m.y1[:, :, :], ALU.add).then_inc(vector_done, vec.one("x3"))
                eng.wait_ge(vector_done, vec.at("x3", i))
                norm("n3", xs, 64)
                eng.wait_ge(vector_done, vec.at("n3_nrm", i))
                eng.tensor_tensor(m.y1[:, :, :], m.xc[:, :, :], mod_row(1, 4), ALU.mult).then_inc(vector_done, vec.one("h3m"))
                eng.wait_ge(vector_done, vec.at("h3m", i))
                eng.tensor_tensor(m.y1[:, :, :], m.y1[:, :, :], mod_row(1, 3), ALU.add).then_inc(vector_done, vec.one("h3"))
                eng.wait_ge(vector_done, vec.at("h3", i))
                norm("n4", m.y1[:, :, :], 72)
                eng.wait_ge(tensor_done, pe.at("fc2", i))
                eng.scalar_tensor_tensor(m.y1[:, :, :].rearrange(flat), m.ps[:, 4, :], 0.5, m.y1[:, :, :].rearrange(flat), ALU.mult, ALU.add).then_inc(vector_done, vec.one("zh"))
                eng.wait_ge(vector_done, vec.at("zh", i))
                eng.tensor_tensor(m.y1[:, :, :], m.y1[:, :, :], mod_row(1, 5), ALU.mult).then_inc(vector_done, vec.one("zg"))
                eng.wait_ge(vector_done, vec.at("zg", i))
                eng.tensor_tensor(group(m.x, i), xs, m.y1[:, :, :], ALU.add).then_inc(vector_done, vec.one("x4"))


def program(nc, ins, out):
    with ExitStack() as ctx:
        m, a = Tensors(), Tensors()
        allocate(nc, ctx, m)
        a.ins = ins
        setup_phase(nc, m, a)
        spike_phase(nc, m)
        delta_phase(nc, m)
        post_phase(nc, m, ins, out)


_COLUMNS = {"L0_attn_alpha_spike", "L0_attn_beta_spike", "L0_attn_head_norm_w", "L0_ffn_b1", "L1_ffn_fc1_bias"}
_TRANSPOSED = {"L1_attn_wq", "L1_attn_wk", "L1_attn_wv", "L1_attn_wo"}


def kernel(**inputs):
    import numpy as np
    import concourse.bacc as bacc
    from concourse import mybir as mb
    from concourse.bass_utils import run_bass_kernel_spmd as run

    nc = bacc.Bacc("TRN2", target_bir_lowering=False, num_devices=1)
    arrays, ins = {}, {}
    for name in inputs:
        v = np.asarray(inputs[name])
        if name in _COLUMNS:
            v = v.reshape(-1, 128).T
        elif name in _TRANSPOSED:
            v = v.T
        v = np.ascontiguousarray(v)
        arrays[f"in_{name}"] = v
        ins[name] = nc.dram_tensor(f"in_{name}", v.shape, mb.dt.from_np(v.dtype), kind="ExternalInput").ap()
    out = nc.dram_tensor("out", (1, 2048, 128), mb.dt.float32, kind="ExternalOutput").ap()
    program(nc, ins, out)
    r = run(nc, [arrays], core_ids=[0])
    return r.results[0]["out"]
```

```python
from contextlib import ExitStack

import concourse.bass as bass
from concourse import mybir

F32 = mybir.dt.float32
I32 = mybir.dt.int32
U8 = mybir.dt.uint8
ALU = mybir.AluOpType
ACT = mybir.ActivationFunctionType
AX = mybir.AxisListType.X

P = 128
T, D = 2048, 128
NT = T // P
H, HD = 8, 64
NP = H // 2
R = 64
FF = 512
NF = FF // P
KW = 4
DECAY = 0.9
MIN_LOG_GATE = -20.0
FLOOR = -80.0
BETA_FLOOR = -40.0
BASE = 8
UPPER = [8, 16, 32, 64]
LEVELS = [1, 2, 4] + UPPER
BANK_OF = {8: 4, 16: 6, 32: 0, 64: 2}


class Tensors:
    pass


class Steps:

    def __init__(self, names, rounds_ahead=0):
        self.names, self.done = names, 0
        self.index = {n: k + 1 for k, n in enumerate(names)}
        assert len(self.index) == len(names)
        self.credit = rounds_ahead * len(names)

    def at(self, name, i=0):
        return i * len(self.names) + self.index[name] + self.credit

    def before(self, name, i):
        return self.at(name, i) - len(self.names)

    def one(self, name):
        assert self.names[self.done % len(self.names)] == name, (name, self.done)
        self.done += 1
        return 1


def bc(ap, shape):
    return ap.to_broadcast(shape)


def setup_phase(nc, m, a):
    with ExitStack() as ctx:
        setup_tensors(nc, ctx, m)
        a.x, a.mods, a.weights = sources(m, a.ins)

        def steps(names):
            return Steps(names.split())

        x_in = ctx.enter_context(nc.semaphore("x_in"))
        mod_in = ctx.enter_context(nc.semaphore("mod_in"))
        weights_in = ctx.enter_context(nc.semaphore("weights_in"))
        pool_done = ctx.enter_context(nc.semaphore("setup_pool_done"))
        pool = steps("zero one select ident "
                     + " ".join(f"from{k} upto{k}" for k in range(1 + len(LEVELS)))
                     + " causal bd0 bd1 bd2 scan scan0 beta_w fills")
        vector_done = ctx.enter_context(nc.semaphore("setup_vector_done"))
        vec = steps("""
            eps c0 sum mean center var_sum norm c1 c2 c3
            ones_c g_neg g_max g_sign g_sign2 g_fin rows_c1 cols_c1
            h1 h hvar rms_in conv_w tap0 tap1 tap2 tap3 floor s1 s2 silu
            spike_beta masks first_neg flags states""" + " drive1 drive3 drive5 drive7 drive9 drive11 drive13 drive15")
        scalar_done = ctx.enter_context(nc.semaphore("setup_scalar_done"))
        act = steps("""c_exp sq1 ln1 r1 rows0 rows1 rows2 rows3 cols
            sq2 ln2 r2 hT0 hT1 hT2 hT3 s_exp""" + " drive0 drive2 drive4 drive6 drive8 drive10 drive12 drive14")
        tensor_done = ctx.enter_context(nc.semaphore("setup_tensor_done"))
        pe = steps("""rows0 rows1 rows2 rows3 cols hT0 hT1 hT2 hT3 """ + " ".join(f"drive{n}" for n in range(16)))

        x, xc, sq = m.x, m.arena[:, 0:2048], m.arena[:, 2048:4096]
        xc3, sq3 = (v.rearrange("p (n d) -> p n d", d=D) for v in (xc, sq))
        hr = m.arena[:, 4096:6144]
        hr3 = hr.rearrange("p (n d) -> p n d", d=D)
        st = m.stats
        block = ctx.enter_context(nc.Block())

        n_weights = len(a.weights)

        @block.sync
        def _(eng):
            eng.dma_start(m.x[:, :, :], a.x).then_inc(x_in, 16)
            for dst, src in a.weights[::2]:
                eng.dma_start(dst, src).then_inc(weights_in, 16)

        @block.gpsimd
        def _(eng):
            eng.memset(m.ident[:, :], 0.0).then_inc(pool_done, pool.one("zero"))
            eng.wait_ge(pool_done, pool.at("zero"))
            eng.memset(m.ones[:, :], 1.0).then_inc(pool_done, pool.one("one"))
            eng.wait_ge(pool_done, pool.at("one"))
            eng.memset(m.maskf[:, :], 1.0).then_inc(pool_done, pool.one("select"))
            eng.wait_ge(pool_done, pool.at("select"))
            eng.affine_select(out=m.ident[:, :], in_=m.ident[:, :], compare_op=ALU.not_equal, fill=1.0,
                                   base=0, pattern=[[-1, P]], channel_multiplier=1).then_inc(pool_done, pool.one("ident"))
            eng.wait_ge(pool_done, pool.at("ident"))
            own = m.maskf[:, 0:P].rearrange("p (b s) -> p b s", s=BASE)
            tables = [(own, BASE, BASE)]
            for n, s in enumerate(LEVELS):
                at = P + HD * n
                tables.append((m.maskf[:, at:at + HD].rearrange("p (b s) -> p b s", s=s), 2 * s, s))
            for k, (v, step, s) in enumerate(tables):
                nb = v.shape[1]
                eng.affine_select(out=v, in_=v, compare_op=ALU.is_ge, fill=0.0, base=0,
                                       pattern=[[-step, nb], [0, s]], channel_multiplier=1).then_inc(pool_done, pool.one(f"from{k}"))
                eng.wait_ge(pool_done, pool.at(f"from{k}"))
                eng.affine_select(out=v, in_=v, compare_op=ALU.is_ge, fill=0.0, base=s - 1,
                                       pattern=[[step, nb], [0, s]], channel_multiplier=-1).then_inc(pool_done, pool.one(f"upto{k}"))
                eng.wait_ge(pool_done, pool.at(f"upto{k}"))
            eng.affine_select(out=own, in_=own, compare_op=ALU.is_ge, fill=0.0, base=0,
                                   pattern=[[BASE, P // BASE], [1, BASE]], channel_multiplier=-1).then_inc(pool_done, pool.one("causal"))
            eng.wait_ge(pool_done, pool.at("causal"))
            eng.memset(m.bd[:, :], 0.0).then_inc(pool_done, pool.one("bd0"))
            eng.wait_ge(pool_done, pool.at("bd0"))
            eng.memset(m.bd[0:HD, 0:HD], 1.0).then_inc(pool_done, pool.one("bd1"))
            eng.wait_ge(pool_done, pool.at("bd1"))
            eng.memset(m.bd[HD:P, HD:P], 1.0).then_inc(pool_done, pool.one("bd2"))
            eng.wait_ge(pool_done, pool.at("bd2"))
            eng.memset(m.scan_keep[:, :, :], 1.0).then_inc(pool_done, pool.one("scan"))
            eng.wait_ge(pool_done, pool.at("scan"))
            eng.memset(m.scan_keep[:, :, 0:1], 0.0).then_inc(pool_done, pool.one("scan0"))
            eng.wait_ge(pool_done, pool.at("scan0"))
            eng.wait_ge(weights_in, 16 * n_weights)
            eng.tensor_copy(m.beta_w[:, :, :], bc(m.wbeta[:, :].unsqueeze(2), [P, H, HD])).then_inc(pool_done, pool.one("beta_w"))
            eng.wait_ge(pool_done, pool.at("beta_w"))
            eng.tensor_copy(m.beta_b[:, :, :], bc(m.bbeta[:, :].unsqueeze(2), [1, H, HD])).then_inc(pool_done, pool.one("fills"))
            eng.wait_ge(pool_done, pool.at("fills"))

        @block.scalar
        def _(eng):
            for dst, src in a.mods:
                eng.dma_start(dst, src).then_inc(mod_in, 16)
            for dst, src in a.weights[1::2]:
                eng.dma_start(dst, src).then_inc(weights_in, 16)
            eng.wait_ge(vector_done, vec.at("c0"))
            eng.activation(st[:, 0:2], m.c[:, :], ACT.Exp, scale=-1.0).then_inc(scalar_done, act.one("c_exp"))
            eng.wait_ge(vector_done, vec.at("center"))
            eng.activation(sq, xc, ACT.Square).then_inc(scalar_done, act.one("sq1"))
            eng.wait_ge(vector_done, vec.at("var_sum"))
            eng.wait_ge(vector_done, vec.at("eps"))
            eng.activation(st[:, 48:64], st[:, 48:64], ACT.Ln, scale=1.0 / D, bias=m.eps[:, 0:1]).then_inc(scalar_done, act.one("ln1"))
            eng.wait_ge(scalar_done, act.at("ln1"))
            eng.activation(st[:, 48:64], st[:, 48:64], ACT.Exp, scale=-0.5).then_inc(scalar_done, act.one("r1"))
            for l in range(2):
                for b in range(2):
                    n = 2 * l + b
                    eng.wait_ge(tensor_done, pe.at(f"rows{n}"))
                    eng.activation(m.mod_rows[:, l, 384 * b:384 * b + 384], m.ps[:, n, 0:384], ACT.Copy).then_inc(scalar_done, act.one(f"rows{n}"))
            eng.wait_ge(tensor_done, pe.at("cols"))
            eng.activation(m.mod_cols[:, :, :].rearrange("p l k -> p (l k)"), m.ps[:, 4, 0:12], ACT.Copy).then_inc(scalar_done, act.one("cols"))
            eng.wait_ge(vector_done, vec.at("h"))
            eng.activation(sq, m.h[:, :, :].rearrange("p n d -> p (n d)"), ACT.Square).then_inc(scalar_done, act.one("sq2"))
            eng.wait_ge(vector_done, vec.at("hvar"))
            eng.activation(st[:, 64:80], st[:, 64:80], ACT.Ln, scale=1.0 / D, bias=m.eps[:, 1:2]).then_inc(scalar_done, act.one("ln2"))
            eng.wait_ge(scalar_done, act.at("ln2"))
            eng.activation(st[:, 64:80], st[:, 64:80], ACT.Exp, scale=-0.5).then_inc(scalar_done, act.one("r2"))
            eng.wait_ge(vector_done, vec.at("c3"))
            for n in range(4):
                eng.wait_ge(tensor_done, pe.at(f"hT{n}"))
                eng.activation(m.hist[:, KW - 1 + 512 * n:KW - 1 + 512 * n + 512], m.ps[:, n, :], ACT.Copy).then_inc(scalar_done, act.one(f"hT{n}"))
            eng.wait_ge(vector_done, vec.at("floor"))
            eng.activation(sq, xc, ACT.Exp, scale=-1.0).then_inc(scalar_done, act.one("s_exp"))
            for n in range(0, 16, 2):
                eng.wait_ge(tensor_done, pe.at(f"drive{n}"))
                eng.activation(m.drive[:, n // 4, 512 * (n % 4):512 * (n % 4) + 512], m.ps[:, n % 8, :],
                                       ACT.Copy, scale=2.0).then_inc(scalar_done, act.one(f"drive{n}"))

        @block.tensor
        def _(eng):
            eng.wait_ge(vector_done, vec.at("ones_c"))
            for l in range(2):
                for b in range(2):
                    eng.matmul(m.ps[:, 2 * l + b, 0:384], m.c_wide[:, l, :], m.wmod[:, l, 384 * b:384 * b + 384],
                                      start=True, stop=True).then_inc(tensor_done, pe.one(f"rows{2 * l + b}"))
            for l in range(2):
                for k in range(6):
                    ins = eng.matmul(m.ps[:, 4, 6 * l + k:6 * l + k + 1], m.wmod[:, l, k * D:(k + 1) * D],
                                     st[:, 4 + l:5 + l], start=True, stop=True)
            ins.then_inc(tensor_done, pe.one("cols"))
            eng.wait_ge(pool_done, pool.at("ident"))
            eng.wait_ge(vector_done, vec.at("rms_in"))
            for n in range(4):
                eng.wait_ge(scalar_done, act.at(f"rows{n}"))
                for k in range(4):
                    ins = eng.transpose(m.ps[:, n, k * D:(k + 1) * D], hr3[:, 4 * n + k, :], m.ident[:, :])
                ins.then_inc(tensor_done, pe.one(f"hT{n}"))
            eng.wait_ge(vector_done, vec.at("silu"))
            eng.wait_ge(scalar_done, act.at("cols"))
            for n in range(16):
                if n < 4:
                    eng.wait_ge(scalar_done, act.at(f"hT{n}"))
                if n >= 8:
                    if n % 2 == 0:
                        eng.wait_ge(scalar_done, act.at(f"drive{n - 8}"))
                    else:
                        eng.wait_ge(vector_done, vec.at(f"drive{n - 8}"))
                eng.matmul(m.ps[:, n % 8, :], m.wspike[:, n // 4 * P:n // 4 * P + P],
                                  m.hh[:, 512 * (n % 4):512 * (n % 4) + 512], start=True, stop=True).then_inc(tensor_done, pe.one(f"drive{n}"))

        @block.vector
        def _(eng):
            eng.memset(m.eps[:, 0:1], 1e-5)
            eng.memset(m.eps[:, 1:2], 1e-6).then_inc(vector_done, vec.one("eps"))
            eng.wait_ge(mod_in, 16 * len(a.mods))
            eng.tensor_scalar(m.c[:, :], m.c[:, :], FLOOR, None, ALU.max).then_inc(vector_done, vec.one("c0"))
            eng.wait_ge(x_in, 16)
            eng.tensor_reduce(st[:, 16:32], x[:, :, :], AX, ALU.add).then_inc(vector_done, vec.one("sum"))
            eng.wait_ge(vector_done, vec.at("sum"))
            eng.tensor_scalar(st[:, 32:48], st[:, 16:32], -1.0 / D, None, ALU.mult).then_inc(vector_done, vec.one("mean"))
            eng.wait_ge(vector_done, vec.at("mean"))
            eng.tensor_tensor(xc3, x[:, :, :], bc(st[:, 32:48].unsqueeze(2), [P, NT, D]), ALU.add).then_inc(vector_done, vec.one("center"))
            eng.wait_ge(scalar_done, act.at("sq1"))
            eng.tensor_reduce(st[:, 48:64], sq3, AX, ALU.add).then_inc(vector_done, vec.one("var_sum"))
            eng.wait_ge(scalar_done, act.at("r1"))
            eng.tensor_tensor(xc3, xc3, bc(st[:, 48:64].unsqueeze(2), [P, NT, D]), ALU.mult).then_inc(vector_done, vec.one("norm"))
            eng.wait_ge(scalar_done, act.at("c_exp"))
            eng.tensor_scalar(st[:, 2:4], st[:, 0:2], 1.0, None, ALU.add).then_inc(vector_done, vec.one("c1"))
            eng.wait_ge(vector_done, vec.at("c1"))
            eng.reciprocal(st[:, 6:8], st[:, 2:4]).then_inc(vector_done, vec.one("c2"))
            eng.wait_ge(vector_done, vec.at("c2"))
            eng.wait_ge(mod_in, 16 * len(a.mods))
            eng.memset(m.hist[:, 0:KW - 1], 0.0)
            eng.tensor_tensor(st[:, 4:6], st[:, 6:8], m.c[:, :], ALU.mult).then_inc(vector_done, vec.one("c3"))
            eng.wait_ge(vector_done, vec.at("c3"))
            eng.tensor_copy(m.c_wide[:, :, :], bc(st[:, 4:6].unsqueeze(2), [P, 2, P])).then_inc(vector_done, vec.one("ones_c"))
            eng.wait_ge(scalar_done, act.at("rows3"))
            g = m.mod_rows[:, :, :].rearrange("p l (u k d) -> p (l u) k d", u=2, k=3)[:, :, 2, :]
            s1 = m.scratch[:, 0:512].rearrange("p (u d) -> p u d", u=4)
            eng.tensor_scalar(s1, g, -1.0, None, ALU.mult).then_inc(vector_done, vec.one("g_neg"))
            eng.wait_ge(vector_done, vec.at("g_neg"))
            eng.tensor_tensor(s1, s1, g, ALU.max).then_inc(vector_done, vec.one("g_max"))
            s2 = m.scratch[:, 512:1024].rearrange("p (u d) -> p u d", u=4)
            eng.tensor_scalar(s2, g, 0.0, 2.0, ALU.is_ge, ALU.mult).then_inc(vector_done, vec.one("g_sign"))
            eng.wait_ge(vector_done, vec.at("g_sign"))
            eng.tensor_scalar(s2, s2, -1.0, None, ALU.add).then_inc(vector_done, vec.one("g_sign2"))
            eng.wait_ge(vector_done, vec.at("g_sign2"))
            eng.scalar_tensor_tensor(g, s1, 0.25, s2, ALU.max, ALU.mult).then_inc(vector_done, vec.one("g_fin"))
            one_row = m.mod_rows[:, :, :].rearrange("p l (u k d) -> p (l u) k d", u=2, k=3)[:, :, 1, :]
            eng.tensor_scalar(one_row, one_row, 1.0, None, ALU.add).then_inc(vector_done, vec.one("rows_c1"))
            eng.wait_ge(scalar_done, act.at("cols"))
            one_col = m.mod_cols[:, :, :].rearrange("p l (u k) -> p (l u) k", u=2)[:, :, 1]
            eng.tensor_scalar(one_col, one_col, 1.0, None, ALU.add).then_inc(vector_done, vec.one("cols_c1"))
            eng.wait_ge(vector_done, vec.at("norm"))
            eng.wait_ge(vector_done, vec.at("rows_c1"))
            eng.tensor_tensor(m.h[:, :, :], xc3, bc(m.mod_rows[:, 0:1, D:2 * D], [P, NT, D]), ALU.mult).then_inc(vector_done, vec.one("h1"))
            eng.wait_ge(vector_done, vec.at("h1"))
            eng.tensor_tensor(m.h[:, :, :], m.h[:, :, :], bc(m.mod_rows[:, 0:1, 0:D], [P, NT, D]), ALU.add).then_inc(vector_done, vec.one("h"))
            eng.wait_ge(scalar_done, act.at("sq2"))
            eng.tensor_reduce(st[:, 64:80], sq3, AX, ALU.add).then_inc(vector_done, vec.one("hvar"))
            eng.wait_ge(scalar_done, act.at("r2"))
            eng.tensor_tensor(hr3, m.h[:, :, :], bc(st[:, 64:80].unsqueeze(2), [P, NT, D]), ALU.mult).then_inc(vector_done, vec.one("rms_in"))
            eng.wait_ge(weights_in, 16 * n_weights)
            eng.tensor_scalar(m.conv_w[:, :], m.conv_w[:, :], m.norm_in[:, 0:1], None, ALU.mult).then_inc(vector_done, vec.one("conv_w"))
            eng.wait_ge(vector_done, vec.at("conv_w"))
            eng.wait_ge(scalar_done, act.at("hT3"))
            eng.tensor_scalar(xc, m.hist[:, 0:T], m.conv_w[:, 0:1], m.conv_b[:, 0:1], ALU.mult, ALU.add).then_inc(vector_done, vec.one("tap0"))
            for k in range(1, KW):
                eng.wait_ge(vector_done, vec.at(f"tap{k - 1}"))
                eng.scalar_tensor_tensor(xc, m.hist[:, k:k + T], m.conv_w[:, k:k + 1], xc, ALU.mult, ALU.add).then_inc(vector_done, vec.one(f"tap{k}"))
            eng.wait_ge(vector_done, vec.at(f"tap{KW - 1}"))
            eng.tensor_scalar(xc, xc, FLOOR, None, ALU.max).then_inc(vector_done, vec.one("floor"))
            eng.wait_ge(scalar_done, act.at("s_exp"))
            eng.tensor_scalar(sq, sq, 1.0, None, ALU.add).then_inc(vector_done, vec.one("s1"))
            eng.wait_ge(vector_done, vec.at("s1"))
            eng.reciprocal(hr, sq).then_inc(vector_done, vec.one("s2"))
            eng.wait_ge(vector_done, vec.at("s2"))
            eng.tensor_tensor(m.hh[:, :], hr, xc, ALU.mult).then_inc(vector_done, vec.one("silu"))
            eng.wait_ge(pool_done, pool.at("fills"))
            eng.tensor_tensor(m.beta_s[:, :, :], bc(m.bd[:, :].unsqueeze(1), [P, NP, P]),
                                      bc(m.bspike[:, :].unsqueeze(2), [P, NP, P]), ALU.mult).then_inc(vector_done, vec.one("spike_beta"))
            eng.tensor_scalar(m.mask[:, :], m.maskf[:, :], 0.5, None, ALU.is_gt).then_inc(vector_done, vec.one("masks"))
            for n in range(len(LEVELS)):
                ins = eng.tensor_reduce(m.first_neg[:, n:n + 1], m.maskf[:, P + HD * n:P + HD * n + HD], AX, ALU.max, negate=True)
            ins.then_inc(vector_done, vec.one("first_neg"))
            eng.memset(m.diff[:, :, :], 0.0)
            eng.memset(m.wide[:, :], 0.0).then_inc(vector_done, vec.one("flags"))
            eng.memset(m.mem[:, :, 0:1], 0.0).then_inc(vector_done, vec.one("states"))
            for n in range(1, 16, 2):
                eng.wait_ge(tensor_done, pe.at(f"drive{n}"))
                eng.tensor_scalar(m.drive[:, n // 4, 512 * (n % 4):512 * (n % 4) + 512], m.ps[:, n % 8, :],
                                          2.0, None, ALU.mult).then_inc(vector_done, vec.one(f"drive{n}"))


def spike_phase(nc, m):
    SURE = 3
    with ExitStack() as ctx:
        step = ctx.enter_context(nc.semaphore("membrane_step"))
        block = ctx.enter_context(nc.Block())
        u, d = m.mem, m.drive[:, :, :].rearrange("p c (n t) -> p (c n) t", t=P)
        start = u[:, :, 0:1].rearrange("p (c n) o -> p c (n o)", c=NP)
        end = u[:, :, P:P + 1].rearrange("p (c n) o -> p c (n o)", c=NP)

        @block.vector
        def _(eng):
            def a_pass():
                eng.sem_clear(step)
                for t in range(P):
                    if t:
                        eng.wait_ge(step, 2 * t)
                    eng.scalar_tensor_tensor(m.kept[:, :], u[:, :, t], 1.0, u[:, :, t], ALU.is_gt, ALU.subtract).then_inc(step, 1)
                    eng.wait_ge(step, 2 * t + 1)
                    eng.scalar_tensor_tensor(u[:, :, t + 1], m.kept[:, :], -DECAY, d[:, :, t], ALU.mult, ALU.add).then_inc(step, 1)
                n = 2 * P
                eng.wait_ge(step, n)
                eng.tensor_tensor(m.diff[:, :, 0:NT - 1], start[:, :, 1:NT], end[:, :, 0:NT - 1], ALU.not_equal).then_inc(step, 1)
                eng.wait_ge(step, n + 1)
                eng.tensor_reduce(m.wide[:, 0:1], m.diff[:, :, :].rearrange("p c n -> p (c n)"), AX, ALU.max).then_inc(step, 1)
                eng.tensor_copy(start[:, :, 1:NT], end[:, :, 0:NT - 1]).then_inc(step, 1)
                eng.wait_ge(step, n + 3)
                eng.transpose(m.wide_t[:, 0:32], m.wide[:, 0:32]).then_inc(step, 1)
                eng.wait_ge(step, n + 4)
                eng.tensor_reduce(m.flag[:, 0:1], m.wide_t[:, 0:32], AX, ALU.max).then_inc(step, 1)
                eng.wait_ge(step, n + 5)

            def changed():
                value = eng.value_load(m.flag[0:1, 0:1])
                for q in range(1, 4):
                    value = value + eng.value_load(m.flag[32 * q:32 * q + 1, 0:1])
                return value

            with eng.Fori(0, SURE) as _:
                a_pass()
            with eng.If(changed() > 0):
                with eng.Fori(0, NT - SURE) as _:
                    with eng.If(changed() > 0):
                        a_pass()


def delta_phase(nc, m):
    with ExitStack() as ctx:
        delta_tensors(nc, ctx, m)

        HALVES = "ab"
        names = {
            "tensor_back": " ".join(f"base{n}" for n in range(4))
            + "".join(f" up{s}{x}" for s in UPPER for x in HALVES) + " tra trb"
            + "".join(f" X{s}a X{s}b" + f" XTa{s} XTb{s}" for s in LEVELS[1:])
            + " seen kend solved out update",
            "scalar_back": "tra trb" + "".join(f" X{s}a X{s}b" for s in LEVELS[1:]) + " kend solved out",
            "vector_back": " ".join(f"base{n}" for n in range(4)) + " up8a up8b tt"
            + "".join(f" up{s}{x}" for s in UPPER[1:] for x in HALVES)
            + "".join(f" TXa{s} XTa{s} TXb{s} XTb{s}" if s < 64 else f" XTa{s} XTb{s}" for s in LEVELS[1:])
            + " rest keep update",
            "tensor_front": "k q au drive_a ksum qsum beta count v",
            "scalar_front": "hh k q au_e zb_e zb_ln beta_e n_ln n_rt n_ln2 n_rec lift_up lift_p lift_n lift_all last v",
            "vector_front": "spikes au0 au1 au2 au z zfloor guard b0 active log_a G mid"
            + "".join(f" lo{s} hi{s}" for s in UPPER) + " toend unit b3 beta_k kq_base"
            + "".join(f" kq{s}" for s in UPPER) + " kq_all k_end",
            "pool_front": "square push km_base" + "".join(f" km{s}" for s in UPPER),
        }
        pe, act, vec = (Steps(names[e + "_back"].split(), 1) for e in ("tensor", "scalar", "vector"))
        fpe, fact, fvec, fpool = (Steps(names[e + "_front"].split(), 1) for e in ("tensor", "scalar", "vector", "pool"))
        tensor_front = ctx.enter_context(nc.semaphore("tensor_front"))
        scalar_front = ctx.enter_context(nc.semaphore("scalar_front"))
        vector_front = ctx.enter_context(nc.semaphore("vector_front"))
        pool_front = ctx.enter_context(nc.semaphore("pool_front"))
        tensor_back = ctx.enter_context(nc.semaphore("tensor_back"))
        scalar_back = ctx.enter_context(nc.semaphore("scalar_back"))
        vector_back = ctx.enter_context(nc.semaphore("vector_back"))

        kq = m.kq
        kqf = kq[:, :, :].rearrange("p a c -> p (a c)")
        EX = m.arena[:, 0:3072].rearrange("p (n c) -> p n c", c=512)
        up_lift = {s: EX[:, n] for n, s in enumerate(UPPER)}
        end_lift, mid = EX[:, 4], EX[:, 5]
        base_p, base_n, all_lift = (m.arena[:, 3072 + 512 * n:3584 + 512 * n] for n in range(3))
        square = m.arena[:, 4608:5632]
        g3 = m.G[:, :, :]
        gf = m.G[:, :, :].rearrange("p c t -> p (c t)")
        bt = {s: m.drive[:, :, :].rearrange("p c t -> p (c t)")[:, 1024 * n:1024 * n + 1024].rearrange("p (h t) -> p h t", t=P)
              for n, s in enumerate(LEVELS)}

        def halves(ap, s):
            return ap.rearrange("p (b two s) -> p b two s", two=2, s=s)

        def head_halves(ap, s, hs, which):
            return ap[:, hs, :].rearrange("p h (b two s) -> p h b two s", two=2, s=s)[:, :, :, which, :]

        def mask_of(s, n, table=m.mask):
            c = P + HD * LEVELS.index(s)
            v = table[:, c:c + HD].rearrange("p (b s) -> p b s", s=s).unsqueeze(1)
            return bc(v, [P, n, HD // s, s])

        def base_heads(n):
            return range(4 * (n // 2) + n % 2, 4 * (n // 2) + 4, 2)

        def tok(i):
            return bass.ds(i * P, P)

        block = ctx.enter_context(nc.Block())
        zb = m.zb
        zbf = zb[:, :, :].rearrange("p a c -> p (a c)")

        @block.gpsimd
        def _(eng):
            eng.sem_inc(pool_front, fpool.credit)

            def front(n):
                eng.wait_ge(scalar_front, fact.at("q", n))
                eng.wait_ge(tensor_front, fpe.before("qsum", n))
                eng.tensor_tensor(square, kqf, kqf, ALU.mult).then_inc(pool_front, fpool.one("square"))
                eng.wait_ge(vector_front, fvec.at("spikes", n))
                eng.tensor_tensor(m.push[:, :, :], m.spk[:, :, :], bc(m.aspike[:, :].unsqueeze(2), [P, NP, P]), ALU.mult).then_inc(pool_front, fpool.one("push"))
                eng.wait_ge(vector_front, fvec.at("beta_k", n))
                eng.wait_ge(scalar_front, fact.at("lift_n", n))
                eng.wait_ge(tensor_back, pe.before("base3", n))
                eng.tensor_tensor(m.km[:, :], m.beta_k[:, :], base_n, ALU.mult).then_inc(pool_front, fpool.one("km_base"))
                for s in UPPER:
                    eng.wait_ge(vector_front, fvec.at(f"kq{s}", n))
                    eng.tensor_tensor(up_lift[s], m.beta_k[:, :], up_lift[s], ALU.mult).then_inc(pool_front, fpool.one(f"km{s}"))

            eng.wait_ge(m.chain_v, 1)
            eng.memset(m.drive[:, :, :], 0.0).then_inc(m.chain_v, 1)
            eng.wait_ge(m.chain_v, 2)
            front(0)
            with eng.Fori(0, NT - 1) as i:
                front(i + 1)

        @block.scalar
        def _(eng):
            nc.scalar.preload_act_table_set("natural_log_exp_and_others")
            eng.sem_inc(scalar_front, fact.credit)
            eng.sem_inc(scalar_back, act.credit)

            def front_tokens(n):
                eng.wait_ge(tensor_front, fpe.before("v", n))
                eng.activation(m.hh_tile[:, :], m.hh[:, tok(n)], ACT.Copy).then_inc(scalar_front, fact.one("hh"))

            def front_kq(n):
                eng.wait_ge(tensor_front, fpe.at("k", n))
                eng.wait_ge(vector_front, fvec.before("kq_all", n))
                eng.wait_ge(pool_front, fpool.before("square", n))
                eng.activation(kq[:, 0, :], m.ps[:, 4, :], ACT.Copy).then_inc(scalar_front, fact.one("k"))
                eng.wait_ge(tensor_front, fpe.at("q", n))
                eng.activation(kq[:, 1, :], m.ps[:, 5, :], ACT.Copy).then_inc(scalar_front, fact.one("q"))

            def front_au(n):
                eng.wait_ge(vector_front, fvec.at("au0", n))
                eng.activation(m.au_e[:, :], m.au_x[:, :], ACT.Exp, scale=-1.0).then_inc(scalar_front, fact.one("au_e"))

            def front_gates(n):
                eng.wait_ge(vector_front, fvec.at("b0", n))
                eng.activation(zbf, zbf, ACT.Exp, scale=-1.0).then_inc(scalar_front, fact.one("zb_e"))
                eng.wait_ge(scalar_front, fact.at("zb_e", n))
                eng.activation(zbf, zbf, ACT.Ln, bias=1.0).then_inc(scalar_front, fact.one("zb_ln"))

            def front_beta(n):
                eng.wait_ge(scalar_front, fact.at("zb_ln", n))
                eng.wait_ge(vector_front, fvec.before("beta_k", n))
                eng.activation(m.beta[:, :], zb[:, 1, :], ACT.Exp, scale=-1.0).then_inc(scalar_front, fact.one("beta_e"))

            def front_norm1(n):
                eng.wait_ge(vector_front, fvec.at("guard", n))
                eng.activation(m.norm[:, :], m.norm[:, :], ACT.Ln).then_inc(scalar_front, fact.one("n_ln"))

            def front_norm2(n):
                eng.wait_ge(scalar_front, fact.at("n_ln", n))
                eng.activation(m.norm[:, :], m.norm[:, :], ACT.Exp, scale=0.5).then_inc(scalar_front, fact.one("n_rt"))

            def front_norm3(n):
                eng.wait_ge(scalar_front, fact.at("n_rt", n))
                eng.activation(m.norm[:, :], m.norm[:, :], ACT.Ln, bias=m.eps[:, 1:2]).then_inc(scalar_front, fact.one("n_ln2"))
                eng.wait_ge(scalar_front, fact.at("n_ln2", n))
                eng.activation(m.norm[:, :], m.norm[:, :], ACT.Exp, scale=-1.0).then_inc(scalar_front, fact.one("n_rec"))

            def front_lift(n):
                eng.wait_ge(vector_front, fvec.at("toend", n))
                eng.activation(EX[:, 0:5, :], EX[:, 0:5, :], ACT.Exp).then_inc(scalar_front, fact.one("lift_up"))

            def front_lift2(n):
                eng.activation(base_p, mid, ACT.Exp).then_inc(scalar_front, fact.one("lift_p"))
                eng.wait_ge(pool_front, fpool.before("km_base", n))
                eng.activation(base_n, mid, ACT.Exp, scale=-1.0).then_inc(scalar_front, fact.one("lift_n"))
                eng.activation(all_lift, gf, ACT.Exp).then_inc(scalar_front, fact.one("lift_all"))

            def front_late(n):
                eng.wait_ge(vector_back, vec.before("keep", n))
                eng.activation(m.last[:, :].unsqueeze(2), g3[:, :, P - 1:P], ACT.Exp).then_inc(scalar_front, fact.one("last"))
                eng.wait_ge(tensor_front, fpe.at("v", n))
                eng.wait_ge(vector_back, vec.before("rest", n))
                eng.activation(m.v[:, :], m.ps[:, 3, :], ACT.Copy).then_inc(scalar_front, fact.one("v"))

            def transposed(i):
                for n, x in enumerate(HALVES):
                    eng.wait_ge(tensor_back, pe.at(f"tr{x}", i))
                    eng.activation(m.tm[:, 4 * n:4 * n + 4, :], m.ps[:, 4 + n, :].rearrange("p (h t) -> p h t", t=P), ACT.Copy).then_inc(scalar_back, act.one(f"tr{x}"))

            def join(i, s):
                for n, x in enumerate(HALVES):
                    hs = slice(4 * n, 4 * n + 4)
                    eng.wait_ge(tensor_back, pe.at(f"X{s}{x}", i))
                    src = m.ps[:, 4 + n, 0:256].rearrange("p (h b s) -> p h b s", h=4, s=s)
                    dst = head_halves(m.xf, s, hs, 0)
                    if HD // s == 1:
                        src, dst = src[:, :, 0, :], dst[:, :, 0, :]
                    eng.activation(dst, src, ACT.Copy).then_inc(scalar_back, act.one(f"X{s}{x}"))

            def state(i):
                eng.wait_ge(tensor_back, pe.at("kend", i))
                eng.activation(m.k_end_rows[:, :], m.ps[:, 4, :], ACT.Copy).then_inc(scalar_back, act.one("kend"))
                eng.wait_ge(tensor_back, pe.at("solved", i))
                eng.activation(m.u_rows[:, :], m.ps[:, 5, :], ACT.Copy).then_inc(scalar_back, act.one("solved"))
                eng.wait_ge(tensor_back, pe.at("out", i))
                y = m.mem[:, :, 0:P].rearrange("p (c n) t -> p c n t", c=NP)[:, :, bass.ds(i, 1), :]
                eng.activation(y[:, :, :, 0:HD], m.ps[:, 6, 0:256].rearrange("p (c v) -> p c v", c=NP).unsqueeze(2), ACT.Copy)
                eng.activation(y[:, :, :, HD:P], m.ps[:, 7, 0:256].rearrange("p (c v) -> p c v", c=NP).unsqueeze(2), ACT.Copy).then_inc(scalar_back, act.one("out"))

            front_tokens(0)
            front_kq(0)
            front_au(0)
            front_gates(0)
            front_beta(0)
            front_norm1(0)
            front_norm2(0)
            front_norm3(0)
            front_lift(0)
            front_lift2(0)
            front_late(0)
            with eng.Fori(0, NT - 1) as i:
                front_tokens(i + 1)
                front_kq(i + 1)
                front_au(i + 1)
                transposed(i)
                join(i, 2)
                join(i, 4)
                join(i, 8)
                front_gates(i + 1)
                join(i, 16)
                front_beta(i + 1)
                front_norm1(i + 1)
                join(i, 32)
                front_norm2(i + 1)
                join(i, 64)
                front_norm3(i + 1)
                front_lift(i + 1)
                front_lift2(i + 1)
                state(i)
                front_late(i + 1)
            transposed(NT - 1)
            for s in LEVELS[1:]:
                join(NT - 1, s)
            state(NT - 1)

        @block.tensor
        def _(eng):
            eng.sem_inc(tensor_front, fpe.credit)
            eng.sem_inc(tensor_back, pe.credit)

            def head(h):
                return slice(HD * (h % 2), HD * (h % 2) + HD), slice(P * (h // 2), P * (h // 2) + P)

            def project(bank, w, rhs, rows=P):
                for c in range(NP):
                    ins = eng.matmul(m.ps[:, bank, c * P:c * P + P], w[:, c * P:c * P + P], rhs, start=True, stop=True)
                return ins

            def front_project(n):
                project(4, m.wk, m.hh[:, tok(n)]).then_inc(tensor_front, fpe.one("k"))
                project(5, m.wq, m.hh[:, tok(n)]).then_inc(tensor_front, fpe.one("q"))
                eng.matmul(m.ps[0:R, 6, 0:P], m.wau[:, :], m.hh[:, tok(n)], start=True, stop=True).then_inc(tensor_front, fpe.one("au"))

            def front_sums(n):
                eng.wait_ge(vector_front, fvec.at("au", n))
                eng.wait_ge(vector_back, vec.before("up64b", n))
                project(0, m.wad, m.au[:, :]).then_inc(tensor_front, fpe.one("drive_a"))
                eng.wait_ge(pool_front, fpool.at("square", n))
                eng.matmul(m.ps[:, 2, :], m.bd[:, :], square[:, 0:512], start=True, stop=True).then_inc(tensor_front, fpe.one("ksum"))
                eng.matmul(m.ps[:, 3, :], m.bd[:, :], square[:, 512:1024], start=True, stop=True).then_inc(tensor_front, fpe.one("qsum"))
                for c in range(NP):
                    o = m.ps[:, 1, c * P:c * P + P]
                    eng.matmul(o, m.beta_w[:, :, :].rearrange("p h k -> p (h k)")[:, c * P:c * P + P], m.hh[:, tok(n)], start=True, stop=False)
                    eng.matmul(o, m.beta_s[:, c, :], m.spk[:, c, :], start=False, stop=False)
                    ins = eng.matmul(o, m.beta_b[:, :, :].rearrange("p h k -> p (h k)")[:, c * P:c * P + P], m.ones[0:1, :], start=False, stop=True)
                ins.then_inc(tensor_front, fpe.one("beta"))

            def front_count(n):
                eng.wait_ge(vector_front, fvec.at("z", n))
                eng.matmul(m.ps[:, 0, :], m.bd[:, :], m.spk[:, :, :].rearrange("p c t -> p (c t)"), start=True, stop=True).then_inc(tensor_front, fpe.one("count"))

            def front_late(n):
                eng.wait_ge(vector_back, vec.before("rest", n))
                eng.wait_ge(scalar_front, fact.at("hh", n))
                eng.wait_ge(vector_front, fvec.at("guard", n))
                eng.matmul(m.ps[:, 3, :], m.hh_tile[:, :], m.wv[:, :], start=True, stop=True).then_inc(tensor_front, fpe.one("v"))

            def blocks(i, ahead):
                eng.wait_ge(vector_front, fvec.at("kq_base", i))
                eng.wait_ge(pool_front, fpool.at("km_base", i))
                eng.wait_ge(scalar_front, fact.at("v", i))
                eng.wait_ge(vector_back, vec.before("update", i))
                for n in range(4):
                    for j, h in enumerate(base_heads(n)):
                        ks, cs = head(h)
                        ins = eng.matmul(m.ps[:, n, 256 * j:256 * j + 256], m.km[ks, cs], m.kq_base[ks, :, cs], start=True, stop=True)
                    ins.then_inc(tensor_back, pe.one(f"base{n}"))
                for s in UPPER:
                    eng.wait_ge(vector_front, fvec.at(f"kq{s}", i))
                    eng.wait_ge(pool_front, fpool.at(f"km{s}", i))
                    at = BANK_OF[s]
                    if s == 8:
                        eng.wait_ge(scalar_back, act.before("out", i))
                        if ahead:
                            eng.wait_ge(scalar_front, fact.at("q", i + 1))
                    if s == 16 and ahead:
                        eng.wait_ge(vector_front, fvec.at("au0", i + 1))
                    for n, x in enumerate(HALVES):
                        if s == 32:
                            eng.wait_ge(vector_back, vec.at(f"base{n}", i))
                        if s == 64:
                            eng.wait_ge(vector_back, vec.at(f"base{2 + n}", i))
                        for h in range(n, H, 2):
                            ks, cs = head(h)
                            half = slice(HD * (h // 2), HD * (h // 2) + HD)
                            ins = eng.matmul(m.ps[:, at + n, P * (h // 2):P * (h // 2) + P], up_lift[s][ks, cs], m.kq_up[s][ks, :, half], start=True, stop=True)
                        ins.then_inc(tensor_back, pe.one(f"up{s}{x}"))
                eng.wait_ge(vector_back, vec.at("tt", i))
                for n, x in enumerate(HALVES):
                    for h in range(4 * n, 4 * n + 4):
                        ins = eng.transpose(m.ps[:, 4 + n, P * (h % 4):P * (h % 4) + P], m.tt[:, h, :], m.ident[:, :])
                    ins.then_inc(tensor_back, pe.one(f"tr{x}"))

            def join(i, s):
                def cols(t, which):
                    return t.rearrange("p (b two s) -> p b two s", two=2, s=s)[:, :, which, :]

                for n, x in enumerate(HALVES):
                    if s == 2:
                        eng.wait_ge(scalar_back, act.at(f"tr{x}", i))
                        eng.wait_ge(vector_back, vec.at("up64b", i))
                    else:
                        eng.wait_ge(vector_back, vec.at(f"TX{x}{s // 2}", i))
                    for h in range(4 * n, 4 * n + 4):
                        ins = eng.matmul(m.ps[:, 4 + n, HD * (h % 4):HD * (h % 4) + HD], bt[s][:, h, :], cols(m.tm[:, h, :], 0), start=True, stop=True)
                    ins.then_inc(tensor_back, pe.one(f"X{s}{x}"))
                for n, x in enumerate(HALVES):
                    eng.wait_ge(scalar_back, act.at(f"X{s}{x}", i))
                    if s > 2:
                        eng.wait_ge(vector_back, vec.at(f"XT{x}{s // 2}", i))
                    if s < 64:
                        for h in range(4 * n, 4 * n + 4):
                            eng.matmul(m.ps[:, 6 + n, HD * (h % 4):HD * (h % 4) + HD], m.tt[:, h, :], cols(m.xf[:, h, :], 0), start=True, stop=True)
                    for h in range(4 * n, 4 * n + 4):
                        ins = eng.matmul(m.ps[:, 6 + n, 256 + HD * (h % 4):256 + HD * (h % 4) + HD], m.xf[:, h, :], cols(m.tt[:, h, :], 1), start=True, stop=True)
                    ins.then_inc(tensor_back, pe.one(f"XT{x}{s}"))

            def state1(i):
                eng.wait_ge(vector_front, fvec.at("k_end", i))
                for h in range(H):
                    ks, cs = head(h)
                    ins = eng.matmul(m.ps[:, 2 + h % 2, HD * (h // 2):HD * (h // 2) + HD], m.kq_all[ks, 0, cs], m.state[ks, h // 2, :], start=True, stop=True)
                ins.then_inc(tensor_back, pe.one("seen"))
                for c in range(NP):
                    ins = eng.transpose(m.ps[:, 4, c * P:c * P + P], m.k_end[:, c * P:c * P + P], m.ident[:, :])
                ins.then_inc(tensor_back, pe.one("kend"))

            def solve(i):
                eng.wait_ge(vector_back, vec.at("rest", i))
                for h in range(H):
                    ins = eng.matmul(m.ps[:, 5, HD * h:HD * h + HD], m.tt[:, h, :], m.rest[:, HD * h:HD * h + HD], start=True, stop=True)
                ins.then_inc(tensor_back, pe.one("solved"))

            def state2(i):
                eng.wait_ge(scalar_back, act.at("solved", i))
                for h in range(H):
                    ks, cs = head(h)
                    o = m.ps[:, 6 + h % 2, HD * (h // 2):HD * (h // 2) + HD]
                    eng.matmul(o, m.kq_all[ks, 1, cs], m.state[ks, h // 2, :], start=True, stop=False)
                    ins = eng.matmul(o, m.a_qk[:, h, :], m.u_rows[:, HD * h:HD * h + HD], start=False, stop=True)
                ins.then_inc(tensor_back, pe.one("out"))
                for h in range(H):
                    e = HD * (h % 2)
                    ins = eng.matmul(m.ps[e:e + HD, 0, HD * (h // 2):HD * (h // 2) + HD], m.k_end_rows[:, HD * h:HD * h + HD],
                                     m.u_rows[:, HD * h:HD * h + HD], start=True, stop=True)
                ins.then_inc(tensor_back, pe.one("update"))

            front_project(0)
            front_sums(0)
            front_count(0)
            front_late(0)
            with eng.Fori(0, NT - 1) as i:
                eng.wait_ge(scalar_back, act.before("out", i))
                front_project(i + 1)
                blocks(i, True)
                join(i, 2)
                front_sums(i + 1)
                join(i, 4)
                front_count(i + 1)
                join(i, 8)
                join(i, 16)
                join(i, 32)
                eng.wait_ge(vector_front, fvec.at("active", i + 1))
                join(i, 64)
                state1(i)
                solve(i)
                front_late(i + 1)
                state2(i)
            blocks(NT - 1, False)
            for s in LEVELS[1:]:
                join(NT - 1, s)
            state1(NT - 1)
            solve(NT - 1)
            state2(NT - 1)

        @block.vector
        def _(eng):
            eng.sem_inc(vector_front, fvec.credit)
            eng.sem_inc(vector_back, vec.credit)
            eng.memset(m.state[:, :, :], 0.0)
            eng.memset(m.xf[:, :, :], 0.0)
            eng.memset(m.a_qk[:, :, :], 0.0)
            eng.memset(m.au[R:R + 1, :], 1.0).then_inc(m.chain_v, 1)
            eng.wait_ge(m.chain_v, 1)

            def front_spikes(n):
                u = m.mem[:, :, 1:P + 1].rearrange("p (c n) t -> p c n t", c=NP)[:, :, bass.ds(n, 1), :]
                eng.wait_ge(tensor_front, fpe.before("count", n))
                eng.wait_ge(pool_front, fpool.before("push", n))
                eng.tensor_scalar(m.spk[:, :, :].unsqueeze(2), u, 1.0, None, ALU.is_gt).then_inc(vector_front, fvec.one("spikes"))
                eng.wait_ge(tensor_front, fpe.at("au", n))
                eng.tensor_scalar(m.au_x[:, :], m.ps[0:R, 6, 0:P], m.bau[:, 0:1], FLOOR, ALU.add, ALU.max).then_inc(vector_front, fvec.one("au0"))

            def front_au(n):
                eng.wait_ge(scalar_front, fact.at("au_e", n))
                eng.tensor_scalar(m.au_e[:, :], m.au_e[:, :], 1.0, None, ALU.add).then_inc(vector_front, fvec.one("au1"))
                eng.wait_ge(vector_front, fvec.at("au1", n))
                eng.reciprocal(m.au_r[:, :], m.au_e[:, :]).then_inc(vector_front, fvec.one("au2"))
                eng.wait_ge(vector_front, fvec.at("au2", n))
                eng.tensor_tensor(m.au[0:R, :], m.au_x[:, :], m.au_r[:, :], ALU.mult).then_inc(vector_front, fvec.one("au"))

            def front_sums(n):
                eng.wait_ge(tensor_front, fpe.at("qsum", n))
                eng.tensor_scalar(m.norm[:, :], m.ps[:, 2:4, :].rearrange("p b c -> p (b c)"), 1e-19, None, ALU.max).then_inc(vector_front, fvec.one("guard"))
                eng.wait_ge(tensor_front, fpe.at("beta", n))
                eng.tensor_scalar(zb[:, 1, :], m.ps[:, 1, :], BETA_FLOOR, None, ALU.max).then_inc(vector_front, fvec.one("b0"))

            def front_active(n):
                eng.wait_ge(tensor_front, fpe.at("count", n))
                eng.tensor_scalar(m.active[:, :], m.ps[:, 0, :], 0.5, None, ALU.is_gt).then_inc(vector_front, fvec.one("active"))

            def front_z(n):
                eng.wait_ge(tensor_front, fpe.at("drive_a", n))
                eng.wait_ge(pool_front, fpool.at("push", n))
                eng.tensor_tensor(zb[:, 0, :], m.ps[:, 0, :], m.push[:, :, :].rearrange("p c t -> p (c t)"), ALU.add).then_inc(vector_front, fvec.one("z"))
                eng.wait_ge(vector_front, fvec.at("z", n))
                eng.tensor_scalar(zb[:, 0, :], zb[:, 0, :], MIN_LOG_GATE, None, ALU.max).then_inc(vector_front, fvec.one("zfloor"))

            def front_exponents(n):
                eng.wait_ge(scalar_front, fact.at("zb_ln", n))
                eng.wait_ge(vector_front, fvec.at("active", n))
                eng.scalar_tensor_tensor(zb[:, 0, :], zb[:, 0, :], -1.0, m.active[:, :], ALU.mult, ALU.mult).then_inc(vector_front, fvec.one("log_a"))
                eng.wait_ge(scalar_front, fact.before("lift_all", n))
                eng.wait_ge(vector_front, fvec.at("log_a", n))
                eng.tensor_tensor_scan(gf, m.scan_keep[:, :, :].rearrange("p c t -> p (c t)"), zb[:, 0, :], 0.0, ALU.mult, ALU.add).then_inc(vector_front, fvec.one("G"))
                eng.wait_ge(vector_front, fvec.at("G", n))
                gb = gf.rearrange("p (b s) -> p b s", s=BASE)
                eng.tensor_tensor(mid.rearrange("p (b s) -> p b s", s=BASE), gb, bc(gb[:, :, BASE // 2 - 1:BASE // 2], [P, 512 // BASE, BASE]), ALU.subtract).then_inc(vector_front, fvec.one("mid"))

            def front_exponents2(n):
                eng.wait_ge(tensor_back, pe.before("up64b", n))
                for s in UPPER:
                    gs, xs = halves(gf, s), halves(up_lift[s], s)
                    split = bc(gs[:, :, 0, s - 1:s], [P, 256 // s, s])
                    eng.tensor_tensor(xs[:, :, 0, :], split, gs[:, :, 0, :], ALU.subtract).then_inc(vector_front, fvec.one(f"lo{s}"))
                    eng.tensor_tensor(xs[:, :, 1, :], gs[:, :, 1, :], split, ALU.subtract).then_inc(vector_front, fvec.one(f"hi{s}"))
                eng.tensor_tensor(end_lift.rearrange("p (c t) -> p c t", t=P), bc(g3[:, :, P - 1:P], [P, NP, P]), g3, ALU.subtract).then_inc(vector_front, fvec.one("toend"))

            def front_unit(n):
                eng.wait_ge(scalar_front, fact.at("n_rec", n))
                eng.tensor_tensor(kqf, kqf, m.norm[:, :], ALU.mult).then_inc(vector_front, fvec.one("unit"))
                eng.wait_ge(scalar_front, fact.at("beta_e", n))
                eng.tensor_tensor(m.beta[:, :], m.beta[:, :], m.active[:, :], ALU.mult).then_inc(vector_front, fvec.one("b3"))
                eng.wait_ge(vector_front, fvec.at("b3", n))
                eng.wait_ge(pool_front, fpool.before("km64", n))
                eng.tensor_tensor(m.beta_k[:, :], kq[:, 0, :], m.beta[:, :], ALU.mult).then_inc(vector_front, fvec.one("beta_k"))
                eng.wait_ge(scalar_front, fact.at("lift_p", n))
                eng.wait_ge(tensor_back, pe.before("base3", n))
                eng.tensor_tensor(m.kq_base[:, :, :], kq[:, :, :], bc(base_p.unsqueeze(1), [P, 2, 512]), ALU.mult).then_inc(vector_front, fvec.one("kq_base"))

            def front_upper(n):
                for s in UPPER:
                    for a in range(2):
                        ins = eng.tensor_tensor(m.kq_up[s][:, a, :].rearrange("p (b s) -> p b s", s=s), halves(kq[:, a, :], s)[:, :, 1, :],
                                                halves(up_lift[s], s)[:, :, 1, :], ALU.mult)
                    ins.then_inc(vector_front, fvec.one(f"kq{s}"))

            def front_late(n):
                eng.wait_ge(scalar_front, fact.at("lift_all", n))
                eng.wait_ge(tensor_back, pe.before("out", n))
                eng.wait_ge(vector_front, fvec.at("beta_k", n))
                eng.tensor_tensor(m.kq_all[:, :, :], kq[:, :, :], bc(all_lift.unsqueeze(1), [P, 2, 512]), ALU.mult).then_inc(vector_front, fvec.one("kq_all"))
                eng.tensor_tensor(m.k_end[:, :], m.beta_k[:, :], end_lift, ALU.mult).then_inc(vector_front, fvec.one("k_end"))

            def blocks(i):
                for n in range(4):
                    eng.wait_ge(tensor_back, pe.at(f"base{n}", i))
                    eng.memset(m.wait_word[:, n:n + 1], 0.0)
                    ps = m.ps[:, n, :].rearrange("p (h a t) -> p h a t", h=2, a=2)
                    hs = slice(4 * (n // 2) + n % 2, 4 * (n // 2) + 4, 2)
                    for s in LEVELS[:3]:
                        eng.copy_predicated(head_halves(bt[s], s, hs, 1), mask_of(s, 2),
                                            ps[:, :, 0, :].rearrange("p h (b two s) -> p h b two s", two=2, s=s)[:, :, :, 1, :])
                    eng.copy_predicated(m.a_qk[:, hs, :], bc(m.mask[:, 0:P].unsqueeze(1), [P, 2, P]), ps[:, :, 1, :]).then_inc(vector_back, vec.one(f"base{n}"))
                for s in UPPER:
                    at = BANK_OF[s]
                    for n, x in enumerate(HALVES):
                        eng.wait_ge(tensor_back, pe.at(f"up{s}{x}", i))
                        ps = m.ps[:, at + n, :].rearrange("p (h a b s) -> p h a b s", h=4, a=2, s=s)
                        hs = slice(n, H, 2)
                        if s == 8:
                            eng.wait_ge(vector_back, vec.at("base3", i))
                        else:
                            eng.wait_ge(vector_back, vec.at(f"up{s // 2}{x}", i))
                        if s == 64:
                            q = slice(0, HD)
                            eng.tensor_copy(bt[s][q, hs, HD:P], ps[q, :, 0, 0, :])
                            ins = eng.tensor_copy(m.a_qk[q, hs, HD:P], ps[q, :, 1, 0, :])
                        else:
                            eng.tensor_tensor(head_halves(bt[s], s, hs, 1), ps[:, :, 0, :, :], mask_of(s, 4, m.maskf), ALU.mult)
                            ins = eng.copy_predicated(head_halves(m.a_qk, s, hs, 1), mask_of(s, 4), ps[:, :, 1, :, :])
                        ins.then_inc(vector_back, vec.one(f"up{s}{x}"))
                    if s == 8:
                        eng.scalar_tensor_tensor(m.tt[:, :, :], bt[1][:, :, :], -1.0, bc(m.ident[:, :].unsqueeze(1), [P, H, P]), ALU.mult, ALU.add).then_inc(vector_back, vec.one("tt"))

            def join(i, s):
                for n, x in enumerate(HALVES):
                    hs = slice(4 * n, 4 * n + 4)
                    eng.wait_ge(tensor_back, pe.at(f"XT{x}{s}", i))
                    if s < 64:
                        v = halves(m.tm[:, hs, :].rearrange("p h t -> p (h t)"), s)[:, :, 0, :]
                        if s > 2:
                            eng.wait_ge(vector_back, vec.at(f"TX{x}{s // 2}", i))
                        eng.tensor_tensor(v, v, m.ps[:, 6 + n, 0:256].rearrange("p (b s) -> p b s", s=s), ALU.subtract).then_inc(vector_back, vec.one(f"TX{x}{s}"))
                    v = halves(m.tt[:, hs, :].rearrange("p h t -> p (h t)"), s)[:, :, 1, :]
                    if s > 2:
                        eng.wait_ge(vector_back, vec.at(f"XT{x}{s // 2}", i))
                    else:
                        eng.wait_ge(vector_back, vec.at("tt", i))
                    eng.scalar_tensor_tensor(v, m.ps[:, 6 + n, 256:512].rearrange("p (b s) -> p b s", s=s), m.first_neg[:, LEVELS.index(s):LEVELS.index(s) + 1], v, ALU.mult, ALU.add).then_inc(vector_back, vec.one(f"XT{x}{s}"))

            def rest(i):
                eng.wait_ge(tensor_back, pe.at("seen", i))
                eng.wait_ge(scalar_front, fact.at("v", i))
                for e in range(2):
                    parity = [t.rearrange("p (c e v) -> p c e v", c=NP, e=2)[:, :, e, :] for t in (m.rest, m.v[:, :])]
                    ins = eng.tensor_tensor(parity[0], parity[1], m.ps[:, 2 + e, 0:256].rearrange("p (c v) -> p c v", c=NP), ALU.subtract)
                ins.then_inc(vector_back, vec.one("rest"))

            def state(i):
                eng.wait_ge(tensor_back, pe.at("out", i))
                eng.tensor_tensor(m.state[:, :, :], m.state[:, :, :], bc(m.last[:, :].unsqueeze(2), [P, NP, HD]), ALU.mult).then_inc(vector_back, vec.one("keep"))
                eng.wait_ge(tensor_back, pe.at("update", i))
                eng.wait_ge(vector_back, vec.at("keep", i))
                eng.tensor_tensor(m.state[:, :, :], m.state[:, :, :], m.ps[:, 0, 0:256].rearrange("p (c v) -> p c v", c=NP), ALU.add).then_inc(vector_back, vec.one("update"))

            front_spikes(0)
            front_au(0)
            front_z(0)
            front_sums(0)
            front_active(0)
            front_exponents(0)
            front_exponents2(0)
            front_unit(0)
            front_upper(0)
            front_late(0)
            eng.wait_ge(m.chain_v, 2)
            with eng.Fori(0, NT - 1) as i:
                front_spikes(i + 1)
                blocks(i)
                front_au(i + 1)
                join(i, 2)
                front_z(i + 1)
                join(i, 4)
                front_sums(i + 1)
                join(i, 8)
                front_active(i + 1)
                join(i, 16)
                front_exponents(i + 1)
                join(i, 32)
                front_exponents2(i + 1)
                join(i, 64)
                rest(i)
                front_unit(i + 1)
                front_upper(i + 1)
                state(i)
                front_late(i + 1)
            blocks(NT - 1)
            for s in LEVELS[1:]:
                join(NT - 1, s)
            rest(NT - 1)
            state(NT - 1)


def allocate(nc, ctx, m):
    def sb(name, shape, dt=F32):
        return ctx.enter_context(nc.sbuf_tensor(name, shape, dt))

    m.ps = ctx.enter_context(nc.psum_tensor("ps", [P, 8, 512], F32))
    m.chain_v = ctx.enter_context(nc.semaphore("blocks_cleared"))
    m.x = sb("x", [P, NT, D])
    m.h = sb("h", [P, NT, D])
    m.hh = sb("hh", [P, T])
    m.drive = sb("drive", [P, NP, T])
    m.mem = sb("mem", [P, NP * NT, P + 1])
    m.stats = sb("stats", [P, 96])
    m.c = sb("c", [P, 2]);
    m.mod_rows = sb("mod_rows", [P, 2, 6 * D]); m.mod_cols = sb("mod_cols", [P, 2, 6]); m.eps = sb("eps", [P, 2])
    m.conv_w = sb("conv_w", [P, KW]); m.conv_b = sb("conv_b", [P, 1]); m.norm_in = sb("norm_in", [P, 1])
    m.wq = sb("wq", [P, 512]); m.wk = sb("wk", [P, 512]); m.wv = sb("wv", [P, 512]);
    m.wau = sb("wau", [P, R]); m.bau = sb("bau", [R, 1]); m.wad = sb("wad", [R + 1, 512])
    m.aspike = sb("aspike", [P, NP]); m.bspike = sb("bspike", [P, NP]); m.wbeta = sb("wbeta", [P, H]); m.bbeta = sb("bbeta", [1, H])
    m.beta_w = sb("beta_w", [P, H, HD]); m.beta_b = sb("beta_b", [1, H, HD]); m.beta_s = sb("beta_s", [P, NP, P])
    m.ident = sb("ident", [P, P]); m.ones = sb("ones", [P, P]); m.bd = sb("bd", [P, P])
    n = P + HD * len(LEVELS)
    m.maskf = sb("maskf", [P, n]); m.mask = sb("mask", [P, n], U8); m.first_neg = sb("first_neg", [P, len(LEVELS)])
    m.scan_keep = sb("scan_keep", [P, NP, P])
    m.kept = sb("kept", [P, NP * NT]); m.diff = sb("diff", [P, NP, NT]); m.wide = sb("wide", [P, 32]); m.wide_t = sb("wide_t", [P, 32]); m.flag = sb("flag", [P, 32], I32)


def setup_tensors(nc, ctx, m):
    def sb(name, shape, dt=F32):
        return ctx.enter_context(nc.sbuf_tensor("setup_" + name, shape, dt))

    m.arena = sb("arena", [P, 6144])
    m.hist = sb("hist", [P, KW - 1 + T])
    m.c_wide = sb("c_wide", [P, 2, P])
    m.wmod = sb("wmod", [P, 2, 6 * D])
    m.scratch = sb("scratch", [P, 1024])
    m.wspike = sb("wspike", [P, 512])


def delta_tensors(nc, ctx, m):
    def sb(name, shape, dt=F32):
        return ctx.enter_context(nc.sbuf_tensor("delta_" + name, shape, dt))

    m.arena = sb("arena", [P, 5632])
    m.state = sb("state", [P, NP, HD]); m.wait_word = sb("wait_word", [P, 4]); m.last = sb("last", [P, NP])
    m.hh_tile = sb("hh_tile", [P, P]); m.kq = sb("kq", [P, 2, 512]); m.v = sb("v", [P, 512]); m.norm = sb("norm", [P, 1024])
    m.au_e = sb("au_e", [R, P]); m.au_x = sb("au_x", [R, P]); m.au_r = sb("au_r", [R, P]); m.au = sb("au", [R + 1, P])
    m.spk = sb("spk", [P, NP, P]); m.push = sb("push", [P, NP, P]); m.active = sb("active", [P, 512]); m.zb = sb("zb", [P, 2, 512]); m.G = sb("G", [P, NP, P])
    m.beta = sb("beta", [P, 512]); m.beta_k = sb("beta_k", [P, 512])
    m.km = sb("km", [P, 512]); m.kq_base = sb("kq_base", [P, 2, 512]); m.kq_all = sb("kq_all", [P, 2, 512]); m.k_end = sb("k_end", [P, 512])
    m.kq_up = {s: sb(f"kq_up{s}", [P, 2, 256]) for s in UPPER}
    m.a_qk = sb("a_qk", [P, H, P]); m.tt = sb("tt", [P, H, P]); m.tm = sb("tm", [P, H, P]); m.xf = sb("xf", [P, H, P])
    spare = m.drive[:, :, :].rearrange("p c t -> p (c t)")[:, len(LEVELS) * H * P:]
    m.k_end_rows, m.rest = spare[:, 0:512], spare[:, 512:1024]
    m.u_rows = sb("u_rows", [P, 512])


def sources(m, ins):
    def col(v, n):
        return v.rearrange("(c p) -> p c", p=n)

    g = {k[8:]: v for k, v in ins.items() if k.startswith("L0_attn_")}
    x = g["x"].rearrange("a (n p) d -> p (a n) d", p=P)
    mods = [(m.wmod[:, l, :], ins[f"L{l}_wmod"]) for l in range(2)] + \
           [(m.c[:, l:l + 1], ins[f"L{l}_c"].rearrange("a p -> p a")) for l in range(2)]
    weights = [
        (m.conv_w[:, :], g["conv_w"].rearrange("p a k -> p (a k)")), (m.conv_b[:, :], col(g["conv_b"], P)),
        (m.norm_in[:, :], col(g["norm_in_w"], P)), (m.wspike[:, :], g["Wspike"]),
        (m.wk[:, :], g["Wk"]), (m.wq[:, :], g["Wq"]), (m.wv[:, :], g["Wv"]),
        (m.wau[:, :], g["Wau"]), (m.bau[:, :], col(g["bau"], R)), (m.wad[0:R, :], g["Wad"]),
        (m.wad[R:R + 1, :], g["bad"].rearrange("(a n) -> a n", a=1)),
        (m.aspike[:, :], g["alpha_spike"]),
        (m.bspike[:, :], g["beta_spike"]),
        (m.wbeta[:, :], g["Wbeta"]), (m.bbeta[:, :], g["bbeta"].rearrange("(a n) -> a n", a=1)),
    ]
    return x, mods, weights


GROUP = 4
GT = GROUP * P
NH1, D1, WIN = 16, 8, 32
NW = P // WIN
NG = 4
QS = float(D1) ** -0.5
NEG = -1e30


def post_tensors(nc, ctx, m):
    def sb(name, shape, dt=F32):
        return ctx.enter_context(nc.sbuf_tensor("post_" + name, shape, dt))

    m.wo = sb("wo", [P, NP, D]); m.head_norm = sb("head_norm", [P, NP]); m.wu1 = sb("wu1", [P, R]); m.bu1 = sb("bu1", [R, 1])
    m.wu2 = sb("wu2", [R + 1, D]); m.ff_norm = sb("ff_norm", [P, 1]); m.wff1 = sb("wff1", [P, FF]); m.wff3 = sb("wff3", [P, FF]); m.wff2 = sb("wff2", [P, NF, D])
    m.w1 = sb("w1", [P, FF]); m.b1 = sb("b1", [P, NF]); m.w2 = sb("w2", [P, NF, D]); m.b2 = sb("b2", [1, D])
    m.wq1 = sb("wq1", [P, D]); m.wk1 = sb("wk1", [P, D]); m.wv1 = sb("wv1", [P, D]); m.wo1 = sb("wo1", [P, D])
    m.gamma = sb("gamma", [P, 1]); m.beta1 = sb("beta1", [P, 1])
    m.fc1_q = sb("fc1_q", [P, FF], I32); m.fc1 = sb("fc1", [P, FF]); m.fc1_s = sb("fc1_s", [1, FF]); m.fc1_b = sb("fc1_b", [P, NF])
    m.fc2_q = sb("fc2_q", [P, NF, D], I32); m.fc2 = sb("fc2", [P, NF, D]); m.fc2_s = sb("fc2_s", [1, FF]); m.fc2_b = sb("fc2_b", [1, D])
    m.st = sb("st", [P, 160])
    free = m.drive[:, :, :]
    m.work, m.work2 = free[:, 0, :], free[:, 1, :]
    m.yt = free[:, 2, :].rearrange("p (c t) -> p c t", t=GT)
    m.hid = free[:, 3, :].rearrange("p (c t) -> p c t", t=GT)
    m.xc = sb("xc", [P, GROUP, D]); m.y1 = sb("y1", [P, GROUP, D]); m.h_in = sb("h_in", [P, GROUP, D]); m.xs = sb("xs", [P, GROUP, D]); m.gate = sb("gate", [P, GT]); m.hT = sb("hT", [P, GT]); m.gu = sb("gu", [R + 1, GT]); m.gu_e = sb("gu_e", [R, GT]); m.gu_x = sb("gu_x", [R, GT])
    m.hid_e = sb("hid_e", [P, 2, GT])
    m.hc = sb("hc", [P, WIN + GT]); m.qc = sb("qc", [P, GT]); m.kc = sb("kc", [P, WIN + GT]); m.v2 = sb("v2", [P, GT // 64, D])
    m.head_of = sb("head_of", [P, NH1]); m.head_scaled = sb("head_scaled", [P, NH1]); m.band = sb("band", [P, NW, 2 * WIN])
    m.sc = sb("sc", [P, 2, 16, 64]); m.pt = sb("pt", [P, 8, P]); m.ao = sb("ao", [P, GT]); m.mx = sb("mx", [P, 16]); m.sm = sb("sm", [P, 16])


def post_sources(m, ins):
    def col(v):
        return v.rearrange("(c p) -> p c", p=P)

    def row(v):
        return v.rearrange("(a n) -> a n", a=1)

    g = {k[8:]: v for k, v in ins.items() if k.startswith("L0_attn_")}
    f = {k[7:]: v for k, v in ins.items() if k.startswith("L0_ffn_")}
    l = {k[3:]: v for k, v in ins.items() if k.startswith("L1_")}
    return [
        (m.wo[:, :, :], g["Wo"].rearrange("(c p) d -> p c d", p=P)), (m.head_norm[:, :], g["head_norm_w"]),
        (m.wu1[:, :], g["Wu1"]), (m.bu1[:, :], g["bu1"].rearrange("(p a) -> p a", a=1)),
        (m.wu2[0:R, :], g["Wu2"]), (m.wu2[R:R + 1, :], row(g["bu2"])),
        (m.ff_norm[:, :], col(g["ff_norm_w"])), (m.wff1[:, :], g["Wff1"]), (m.wff3[:, :], g["Wff3"]),
        (m.wff2[:, :, :], g["Wff2"].rearrange("(c p) d -> p c d", p=P)),
        (m.w1[:, :], f["w1"]), (m.b1[:, :], f["b1"]), (m.w2[:, :, :], f["w2"].rearrange("(c p) d -> p c d", p=P)),
        (m.b2[:, :], row(f["b2"])),
        (m.wq1[:, :], l["attn_wq"]), (m.wk1[:, :], l["attn_wk"]), (m.wv1[:, :], l["attn_wv"]), (m.wo1[:, :], l["attn_wo"]),
        (m.gamma[:, :], col(l["ffn_ln_gamma"])), (m.beta1[:, :], col(l["ffn_ln_beta"])),
        (m.fc1_q[:, :], l["ffn_fc1_q"]), (m.fc1_s[:, :], l["ffn_fc1_scales"]), (m.fc1_b[:, :], l["ffn_fc1_bias"]),
        (m.fc2_q[:, :, :], l["ffn_fc2_q"].rearrange("(c p) d -> p c d", p=P)),
        (m.fc2_s[:, :], l["ffn_fc2_scales"].rearrange("(a c) d -> a (c d)", a=1)), (m.fc2_b[:, :], row(l["ffn_fc2_bias"])),
    ]


def post_phase(nc, m, ins, out):
    with ExitStack() as ctx:
        post_tensors(nc, ctx, m)
        loads = post_sources(m, ins)

        def steps(names, ahead=0):
            return Steps(names.split(), rounds_ahead=ahead)

        loaded = ctx.enter_context(nc.semaphore("post_weights_in"))
        stored = ctx.enter_context(nc.semaphore("stored"))

        def each(fmt, n):
            return " ".join(fmt.format(k) for k in range(n))

        def norm_vec(p):
            return f" {p}_sum {p}_mean {p}_cen {p}_var {p}_nrm"

        def norm_act(p):
            return f" {p}_sq {p}_ln {p}_r"

        pre_pool_done = ctx.enter_context(nc.semaphore("post_pool_setup_done"))
        pre_pool = steps("head band0 head_from head_upto band_lo band_hi")
        pre_vector_done = ctx.enter_context(nc.semaphore("post_vector_setup_done"))
        pre_vec = steps("scaled fc1_f fc2_f fc1_m fc2_m fc1_w fc2_w first")
        pre_tensor_done = ctx.enter_context(nc.semaphore("post_tensor_setup_done"))
        pre_pe = steps("scales1 scales2")
        vector_done = ctx.enter_context(nc.semaphore("post_vector_done"))
        vec = steps("x_in h_in y_var yn g0 gu s0 gated y1 zvar z " + each("a{0}", 4)
                    + " y2 y2g x1" + norm_vec("n1") + " x2m x2" + norm_vec("n2")
                    + " " + "sc0 mx0 band sub0 sum0 rec0 prob0 "
                    + " ".join(f"sc{n} mx{n} sub{n} sum{n} rec{n} prob{n} pick{n - 1} fold{n - 1}" for n in range(1, GROUP))
                    + f" pick{GROUP - 1} fold{GROUP - 1}"
                    + " hist x3m x3" + norm_vec("n3") + " h3m h3" + norm_vec("n4") + " "
                    + "zh zg x4", 1)
        scalar_done = ctx.enter_context(nc.semaphore("post_scalar_done"))
        act = steps("hT y_sq y_ln y_r g_e g_ln g_sig yt0 yt1 yt2 yt3 s_e s_ln s_sig z_sq z_ln z_r zT " + each("a{0}_e", 4)
                    + norm_act("n1") + " n1T " + each("gelu{0}", 4) + norm_act("n2")
                    + " n2T qc kc v2a v2b " + each("exp{0} pt{0}", GROUP)
                    + norm_act("n3") + norm_act("n4") + " n4T " + each("b{0}_e", 4), 1)
        tensor_done = ctx.enter_context(nc.semaphore("post_tensor_done"))
        pe = steps("hT g1 yT0 yT1 yT2 yT3 gate proj zT " + each("a{0}", 4) + " ff2 n1T "
                   + each("c{0}", 4) + " w2 n2T q k va vb " + "sc0 "
                   + " ".join(f"sc{n} pt{n - 1} pv{n - 1}" for n in range(1, GROUP)) + f" pt{GROUP - 1} pv{GROUP - 1}"
                   + " wo n4T " + each("b{0}", 4) + " fc2", 1)
        pool_done = ctx.enter_context(nc.semaphore("post_pool_done"))
        pool = steps(each("qm{0}", GROUP), 1)
        st = m.st
        block = ctx.enter_context(nc.Block())
        flat = "p n d -> p (n d)"

        @block.sync
        def _(eng):
            for dst, src in loads:
                eng.dma_start(dst, src).then_inc(loaded, 16)
            o = out.rearrange("a (n p) d -> p (a n) d", p=P)
            with eng.Fori(0, NT // GROUP) as i:
                eng.wait_ge(vector_done, vec.at("x4", i))
                eng.dma_start(o[:, bass.ds(i * GROUP, GROUP), :], m.x[:, bass.ds(i * GROUP, GROUP), :]).then_inc(stored, 16)
            eng.wait_ge(stored, 16 * (NT // GROUP))

        @block.gpsimd
        def _(eng):
            eng.memset(m.head_of[:, :], 1.0).then_inc(pre_pool_done, pre_pool.one("head"))
            eng.wait_ge(pre_pool_done, pre_pool.at("head"))
            eng.memset(m.band[:, :, :], 0.0).then_inc(pre_pool_done, pre_pool.one("band0"))
            eng.wait_ge(pre_pool_done, pre_pool.at("band0"))
            eng.affine_select(out=m.head_of[:, :], in_=m.head_of[:, :], compare_op=ALU.is_ge, fill=0.0, base=0,
                                   pattern=[[-D1, NH1]], channel_multiplier=1).then_inc(pre_pool_done, pre_pool.one("head_from"))
            eng.wait_ge(pre_pool_done, pre_pool.at("head_from"))
            eng.affine_select(out=m.head_of[:, :], in_=m.head_of[:, :], compare_op=ALU.is_ge, fill=0.0, base=D1 - 1,
                                   pattern=[[D1, NH1]], channel_multiplier=-1).then_inc(pre_pool_done, pre_pool.one("head_upto"))
            eng.wait_ge(pre_pool_done, pre_pool.at("head_upto"))
            for a in range(4):
                v = m.band[WIN * a:WIN * a + WIN, :, :]
                ins_ = eng.affine_select(out=v, in_=v, compare_op=ALU.is_gt, fill=NEG, base=0,
                                         pattern=[[0, NW], [1, 2 * WIN]], channel_multiplier=-1)
            ins_.then_inc(pre_pool_done, pre_pool.one("band_lo"))
            eng.wait_ge(pre_pool_done, pre_pool.at("band_lo"))
            for a in range(4):
                v = m.band[WIN * a:WIN * a + WIN, :, :]
                ins_ = eng.affine_select(out=v, in_=v, compare_op=ALU.is_ge, fill=NEG, base=WIN,
                                         pattern=[[0, NW], [-1, 2 * WIN]], channel_multiplier=1)
            ins_.then_inc(pre_pool_done, pre_pool.one("band_hi"))
            eng.wait_ge(pre_pool_done, pre_pool.at("band_hi"))
            eng.wait_ge(pre_vector_done, pre_vec.at("first"))
            eng.sem_inc(pool_done, pool.credit)
            with eng.Fori(0, NT // GROUP) as i:
                for n in range(GROUP):
                    if n:
                        eng.wait_ge(tensor_done, pe.at(f"sc{n - 1}", i))
                    else:
                        eng.wait_ge(scalar_done, act.at("qc", i))
                    q = m.qc[:, P * n:P * n + P].rearrange("p (j q) -> p j q", q=WIN).unsqueeze(2)
                    eng.tensor_tensor(m.work2[:, :].rearrange("p (j h q) -> p j h q", h=NH1, q=WIN), bc(q, [P, NW, NH1, WIN]),
                                               bc(m.head_scaled[:, :].unsqueeze(1).unsqueeze(3), [P, NW, NH1, WIN]), ALU.mult).then_inc(pool_done, pool.one(f"qm{n}"))

        def group(t, i):
            return t[:, bass.ds(i * GROUP, GROUP), :]

        def y_group(i):
            return m.mem[:, :, 0:P].rearrange("p (c n) t -> p c n t", c=NP)[:, :, bass.ds(i * GROUP, GROUP), :]

        @block.scalar
        def _(eng):
            eng.sem_inc(scalar_done, act.credit)

            def norm(p, c, i, eps, width=D):
                eng.wait_ge(scalar_done, act.at(f"{p}_sq", i))
                eng.wait_ge(vector_done, vec.at({"y": "y_var", "z": "zvar"}.get(p, f"{p}_var"), i))
                eng.activation(c, c, ACT.Ln, scale=1.0 / width, bias=m.eps[:, eps:eps + 1]).then_inc(scalar_done, act.one(f"{p}_ln"))
                eng.wait_ge(scalar_done, act.at(f"{p}_ln", i))
                eng.activation(c, c, ACT.Exp, scale=-0.5).then_inc(scalar_done, act.one(f"{p}_r"))

            w512 = m.work[:, 0:GT]
            with eng.Fori(0, NT // GROUP) as i:
                nc.scalar.preload_act_table_set("natural_log_exp_and_others")
                eng.wait_ge(tensor_done, pe.at("hT", i))
                eng.activation(m.hT[:, :], m.ps[:, 4, :], ACT.Copy).then_inc(scalar_done, act.one("hT"))
                eng.activation(m.work[:, :].rearrange("p (c n t) -> p c n t", c=NP, n=GROUP), y_group(i), ACT.Square).then_inc(scalar_done, act.one("y_sq"))
                norm("y", st[:, 0:32], i, 1, HD)
                eng.wait_ge(vector_done, vec.at("g0", i))
                eng.activation(m.gu_e[:, :], m.gu_x[:, :], ACT.Exp, scale=-1.0).then_inc(scalar_done, act.one("g_e"))
                eng.wait_ge(scalar_done, act.at("g_e", i))
                eng.activation(m.gu_e[:, :], m.gu_e[:, :], ACT.Ln, bias=1.0).then_inc(scalar_done, act.one("g_ln"))
                eng.wait_ge(scalar_done, act.at("g_ln", i))
                eng.activation(m.gu_e[:, :], m.gu_e[:, :], ACT.Exp, scale=-1.0).then_inc(scalar_done, act.one("g_sig"))
                for c in range(NP):
                    eng.wait_ge(tensor_done, pe.at(f"yT{c}", i))
                    eng.activation(m.yt[:, c, :], m.ps[:, c, :], ACT.Copy, scale=m.head_norm[:, c:c + 1]).then_inc(scalar_done, act.one(f"yt{c}"))
                eng.wait_ge(vector_done, vec.at("s0", i))
                eng.activation(m.gate[:, :], m.gate[:, :], ACT.Exp, scale=-1.0).then_inc(scalar_done, act.one("s_e"))
                eng.wait_ge(scalar_done, act.at("s_e", i))
                eng.activation(m.gate[:, :], m.gate[:, :], ACT.Ln, bias=1.0).then_inc(scalar_done, act.one("s_ln"))
                eng.wait_ge(scalar_done, act.at("s_ln", i))
                eng.activation(m.gate[:, :], m.gate[:, :], ACT.Exp, scale=-1.0).then_inc(scalar_done, act.one("s_sig"))
                eng.wait_ge(vector_done, vec.at("y1", i))
                eng.activation(w512, m.y1[:, :, :].rearrange(flat), ACT.Square).then_inc(scalar_done, act.one("z_sq"))
                norm("z", st[:, 32:36], i, 1)
                eng.wait_ge(tensor_done, pe.at("zT", i))
                eng.activation(m.hT[:, :], m.ps[:, 4, :], ACT.Copy, scale=m.ff_norm[:, 0:1]).then_inc(scalar_done, act.one("zT"))
                for f in range(NF):
                    eng.wait_ge(tensor_done, pe.at(f"a{f}", i))
                    if f > 1:
                        eng.wait_ge(vector_done, vec.at(f"a{f - 2}", i))
                    eng.activation(m.hid_e[:, f % 2, :], m.ps[:, 2 * (f % 2), :], ACT.Silu).then_inc(scalar_done, act.one(f"a{f}_e"))

                nc.scalar.preload_act_table_set("natural_log_exp_and_others")

                def square(p):
                    eng.wait_ge(vector_done, vec.at(f"{p}_cen", i))
                    eng.activation(w512, m.xc[:, :, :].rearrange(flat), ACT.Square).then_inc(scalar_done, act.one(f"{p}_sq"))

                square("n1")
                norm("n1", st[:, 48:52], i, 0)
                eng.wait_ge(tensor_done, pe.at("n1T", i))
                eng.activation(m.hT[:, :], m.ps[:, 5, :], ACT.Identity, scale=m.mod_cols[:, 0, 4:5], bias=m.mod_cols[:, 0, 3:4]).then_inc(scalar_done, act.one("n1T"))
                for f in range(NF):
                    eng.wait_ge(tensor_done, pe.at(f"c{f}", i))
                    eng.activation(m.hid[:, f, :], m.ps[:, f, :], ACT.Gelu, bias=m.b1[:, f:f + 1]).then_inc(scalar_done, act.one(f"gelu{f}"))
                nc.scalar.preload_act_table_set("natural_log_exp_and_others")
                square("n2")
                norm("n2", st[:, 56:60], i, 0)
                eng.wait_ge(tensor_done, pe.at("n2T", i))
                eng.activation(m.hc[:, WIN:WIN + GT], m.ps[:, 6, :], ACT.Identity, scale=m.mod_cols[:, 1, 1:2], bias=m.mod_cols[:, 1, 0:1]).then_inc(scalar_done, act.one("n2T"))
                eng.wait_ge(tensor_done, pe.at("q", i))
                eng.activation(m.qc[:, :], m.ps[:, 0, :], ACT.Copy).then_inc(scalar_done, act.one("qc"))
                eng.wait_ge(tensor_done, pe.at("k", i))
                eng.activation(m.kc[:, WIN:WIN + GT], m.ps[:, 1, :], ACT.Copy).then_inc(scalar_done, act.one("kc"))
                for b, x in enumerate("ab"):
                    eng.wait_ge(tensor_done, pe.at(f"v{x}", i))
                    eng.activation(m.v2[:, 4 * b:4 * b + 4, :], m.ps[:, 2 + b, :].rearrange("p (w d) -> p w d", d=D), ACT.Copy).then_inc(scalar_done, act.one(f"v2{x}"))
                for n in range(GROUP):
                    eng.wait_ge(vector_done, vec.at(f"sub{n}", i))
                    eng.activation(m.sc[:, n % 2], m.sc[:, n % 2], ACT.Exp).then_inc(scalar_done, act.one(f"exp{n}"))
                    eng.wait_ge(tensor_done, pe.at(f"pt{n}", i))
                    eng.activation(m.pt[:, :, :].rearrange("p g t -> p (g t)"), m.ps[:, 2:4, :].rearrange("p b t -> p (b t)"), ACT.Copy).then_inc(scalar_done, act.one(f"pt{n}"))
                square("n3")
                norm("n3", st[:, 64:68], i, 0)
                square("n4")
                norm("n4", st[:, 72:76], i, 0)
                eng.wait_ge(tensor_done, pe.at("n4T", i))
                eng.activation(m.hT[:, :], m.ps[:, 5, :], ACT.Identity, scale=m.gamma[:, 0:1], bias=m.beta1[:, 0:1]).then_inc(scalar_done, act.one("n4T"))
                for f in range(NF):
                    eng.wait_ge(tensor_done, pe.at(f"b{f}", i))
                    eng.activation(m.hid[:, f, :], m.ps[:, f, :], ACT.Silu, bias=m.fc1_b[:, f:f + 1]).then_inc(scalar_done, act.one(f"b{f}_e"))

        @block.tensor
        def _(eng):
            eng.wait_ge(loaded, 16 * len(loads))
            eng.matmul(m.ps[:, 0, :], m.ones[0:1, :], m.fc1_s[:, :], start=True, stop=True).then_inc(pre_tensor_done, pre_pe.one("scales1"))
            eng.matmul(m.ps[:, 1, :], m.ones[0:1, :], m.fc2_s[:, :], start=True, stop=True).then_inc(pre_tensor_done, pre_pe.one("scales2"))
            eng.wait_ge(pre_vector_done, pre_vec.at("first"))
            eng.sem_inc(tensor_done, pe.credit)

            def rows_to_columns(bank, src3, name):
                for n in range(GROUP):
                    ins_ = eng.transpose(m.ps[:, bank, P * n:P * n + P], src3[:, n, :], m.ident[:, :])
                ins_.then_inc(tensor_done, pe.one(name))

            def hidden(bank, w, src, name):
                eng.matmul(m.ps[:, bank, :], w, src, start=True, stop=True).then_inc(tensor_done, pe.one(name))

            def back_to_rows(bank, src, w, name, bias=None):
                for n in range(GROUP):
                    o = m.ps[:, bank, P * n:P * n + P]
                    for f in range(NF):
                        ins_ = eng.matmul(o, src[:, f, P * n:P * n + P], w[:, f, :], start=(f == 0), stop=(f == NF - 1 and bias is None))
                    if bias is not None:
                        ins_ = eng.matmul(o, m.ones[0:1, :], bias, start=False, stop=True)
                ins_.then_inc(tensor_done, pe.one(name))

            with eng.Fori(0, NT // GROUP) as i:
                eng.wait_ge(vector_done, vec.at("h_in", i))
                rows_to_columns(4, m.h_in, "hT")
                eng.wait_ge(scalar_done, act.at("hT", i))
                eng.matmul(m.ps[0:R, 5, :], m.wu1[:, :], m.hT[:, :], start=True, stop=True).then_inc(tensor_done, pe.one("g1"))
                eng.wait_ge(vector_done, vec.at("yn", i))
                for c in range(NP):
                    rows_to_columns(c, m.work2[:, :].rearrange("p (c n t) -> p c n t", c=NP, n=GROUP)[:, c, :, :], f"yT{c}")
                eng.wait_ge(vector_done, vec.at("gu", i))
                for n in range(GROUP):
                    ins_ = eng.matmul(m.ps[:, 6, P * n:P * n + P], m.gu[:, P * n:P * n + P], m.wu2[:, :], start=True, stop=True)
                ins_.then_inc(tensor_done, pe.one("gate"))
                eng.wait_ge(scalar_done, act.at("yt3", i))
                back_to_rows(7, m.yt, m.wo, "proj")
                eng.wait_ge(vector_done, vec.at("z", i))
                rows_to_columns(4, m.xc, "zT")
                eng.wait_ge(scalar_done, act.at("zT", i))
                for f in range(NF):
                    if f >= 2:
                        eng.wait_ge(vector_done, vec.at(f"a{f - 2}", i))
                    eng.matmul(m.ps[:, 2 * (f % 2), :], m.wff1[:, P * f:P * f + P], m.hT[:, :], start=True, stop=True)
                    hidden(2 * (f % 2) + 1, m.wff3[:, P * f:P * f + P], m.hT[:, :], f"a{f}")
                eng.wait_ge(vector_done, vec.at("a3", i))
                back_to_rows(4, m.hid, m.wff2, "ff2")
                eng.wait_ge(vector_done, vec.at("n1_nrm", i))
                rows_to_columns(5, m.xc, "n1T")
                eng.wait_ge(scalar_done, act.at("n1T", i))
                for f in range(NF):
                    hidden(f, m.w1[:, P * f:P * f + P], m.hT[:, :], f"c{f}")
                eng.wait_ge(scalar_done, act.at("gelu3", i))
                back_to_rows(4, m.hid, m.w2, "w2", m.b2[:, :])
                eng.wait_ge(vector_done, vec.at("n2_nrm", i))
                rows_to_columns(6, m.xc, "n2T")
                eng.wait_ge(scalar_done, act.at("n2T", i))
                hidden(0, m.wq1[:, :], m.hc[:, WIN:WIN + GT], "q")
                hidden(1, m.wk1[:, :], m.hc[:, WIN:WIN + GT], "k")
                for b, x in enumerate("ab"):
                    for w in range(8):
                        win = 8 * b + w
                        e = 64 * (w % 2)
                        ins_ = eng.matmul(m.ps[e:e + 64, 2 + b, P * (w // 2):P * (w // 2) + P], m.hc[:, WIN * win:WIN * win + 64], m.wv1[:, :], start=True, stop=True)
                    ins_.then_inc(tensor_done, pe.one(f"v{x}"))
                eng.wait_ge(scalar_done, act.at("v2b", i))

                def scores(n):
                    eng.wait_ge(pool_done, pool.at(f"qm{n}", i))
                    if n:
                        eng.wait_ge(vector_done, vec.at(f"sc{n - 1}", i))
                    for j in range(NW):
                        for g in range(NG):
                            k0 = P * n + WIN * j
                            ins_ = eng.matmul(m.ps[:, j // 2, P * g + 64 * (j % 2):P * g + 64 * (j % 2) + 64],
                                              m.work2[:, 512 * j + P * g:512 * j + P * g + P], m.kc[:, k0:k0 + 64], start=True, stop=True)
                    ins_.then_inc(tensor_done, pe.one(f"sc{n}"))

                scores(0)
                for n in range(GROUP):
                    if n < GROUP - 1:
                        scores(n + 1)
                    eng.wait_ge(vector_done, vec.at(f"prob{n}", i))
                    s4 = m.sc[:, n % 2].rearrange("p (a g j) k -> p a g (j k)", a=2, j=2)
                    for a in range(2):
                        for g in range(NG):
                            ins_ = eng.transpose(m.ps[:, 2 + a, P * g:P * g + P], s4[:, a, g, :], m.ident[:, :])
                    ins_.then_inc(tensor_done, pe.one(f"pt{n}"))
                    eng.wait_ge(scalar_done, act.at(f"pt{n}", i))
                    if n:
                        eng.wait_ge(vector_done, vec.at(f"pick{n - 1}", i))
                    for j in range(NW):
                        e = 64 * (j % 2)
                        ins_ = eng.matmul(m.ps[:, 4 + j, :], m.v2[e:e + 64, 2 * n + j // 2, :],
                                          m.pt[e:e + 64, 4 * (j // 2):4 * (j // 2) + 4, :].rearrange("p g t -> p (g t)"), start=True, stop=True)
                    ins_.then_inc(tensor_done, pe.one(f"pv{n}"))
                eng.wait_ge(vector_done, vec.at(f"fold{GROUP - 1}", i))
                for n in range(GROUP):
                    ins_ = eng.matmul(m.ps[:, 4, P * n:P * n + P], m.ao[:, P * n:P * n + P], m.wo1[:, :], start=True, stop=True)
                ins_.then_inc(tensor_done, pe.one("wo"))
                eng.wait_ge(vector_done, vec.at("n4_nrm", i))
                rows_to_columns(5, m.xc, "n4T")
                eng.wait_ge(scalar_done, act.at("n4T", i))
                for f in range(NF):
                    hidden(f, m.fc1[:, P * f:P * f + P], m.hT[:, :], f"b{f}")
                eng.wait_ge(scalar_done, act.at("b3_e", i))
                back_to_rows(4, m.hid, m.fc2, "fc2", m.fc2_b[:, :])

        @block.vector
        def _(eng):
            eng.wait_ge(loaded, 16 * len(loads))
            eng.wait_ge(pre_pool_done, pre_pool.at("band_hi"))
            eng.tensor_scalar(m.head_scaled[:, :], m.head_of[:, :], QS, None, ALU.mult).then_inc(pre_vector_done, pre_vec.one("scaled"))
            fc2, fc2q = (t[:, :, :].rearrange("p c d -> p (c d)") for t in (m.fc2, m.fc2_q))
            eng.tensor_copy(m.fc1[:, :], m.fc1_q[:, :]).then_inc(pre_vector_done, pre_vec.one("fc1_f"))
            eng.tensor_copy(fc2, fc2q).then_inc(pre_vector_done, pre_vec.one("fc2_f"))
            eng.wait_ge(pre_vector_done, pre_vec.at("fc2_f"))
            eng.tensor_scalar(m.fc1[:, :], m.fc1[:, :], -128.0, None, ALU.add).then_inc(pre_vector_done, pre_vec.one("fc1_m"))
            eng.tensor_scalar(fc2, fc2, -128.0, None, ALU.add).then_inc(pre_vector_done, pre_vec.one("fc2_m"))
            eng.wait_ge(pre_vector_done, pre_vec.at("fc2_m"))
            eng.wait_ge(pre_tensor_done, pre_pe.at("scales2"))
            eng.tensor_tensor(m.fc1[:, :], m.fc1[:, :], m.ps[:, 0, :], ALU.mult).then_inc(pre_vector_done, pre_vec.one("fc1_w"))
            eng.tensor_tensor(fc2, fc2, m.ps[:, 1, :], ALU.mult).then_inc(pre_vector_done, pre_vec.one("fc2_w"))
            eng.memset(m.gu[R:R + 1, :], 1.0)
            eng.memset(m.hc[:, 0:WIN], 0.0)
            eng.memset(m.kc[:, 0:WIN], 0.0)
            eng.memset(m.band[:, 0, 0:WIN], NEG).then_inc(pre_vector_done, pre_vec.one("first"))
            eng.wait_ge(pre_vector_done, pre_vec.at("first"))
            eng.sem_inc(vector_done, vec.credit)
            w3 = m.work[:, 0:GT].rearrange("p (n d) -> p n d", d=D)

            with eng.Fori(0, NT // GROUP) as i:
                xs = m.xs[:, :, :]

                def bank3(b):
                    return m.ps[:, b, :].rearrange("p (n d) -> p n d", d=D)

                def mod_row(l, k):
                    return bc(m.mod_rows[:, l:l + 1, D * k:D * k + D], [P, GROUP, D])

                def norm(p, src, c):
                    mean, r = st[:, c + 4:c + 8], st[:, c:c + 4]
                    eng.tensor_reduce(mean, src, AX, ALU.add).then_inc(vector_done, vec.one(f"{p}_sum"))
                    eng.wait_ge(vector_done, vec.at(f"{p}_sum", i))
                    eng.tensor_scalar(mean, mean, -1.0 / D, None, ALU.mult).then_inc(vector_done, vec.one(f"{p}_mean"))
                    eng.wait_ge(vector_done, vec.at(f"{p}_mean", i))
                    eng.tensor_tensor(m.xc[:, :, :], src, bc(mean.unsqueeze(2), [P, GROUP, D]), ALU.add).then_inc(vector_done, vec.one(f"{p}_cen"))
                    eng.wait_ge(scalar_done, act.at(f"{p}_sq", i))
                    eng.tensor_reduce(r, w3, AX, ALU.add).then_inc(vector_done, vec.one(f"{p}_var"))
                    eng.wait_ge(scalar_done, act.at(f"{p}_r", i))
                    eng.tensor_tensor(m.xc[:, :, :], m.xc[:, :, :], bc(r.unsqueeze(2), [P, GROUP, D]), ALU.mult).then_inc(vector_done, vec.one(f"{p}_nrm"))

                eng.wait_ge(vector_done, vec.before("x4", i))
                eng.tensor_copy(xs, group(m.x, i)).then_inc(vector_done, vec.one("x_in"))
                eng.tensor_copy(m.h_in[:, :, :], group(m.h, i)).then_inc(vector_done, vec.one("h_in"))
                eng.wait_ge(scalar_done, act.at("y_sq", i))
                eng.tensor_reduce(st[:, 0:32], m.work[:, :].rearrange("p (g v) -> p g v", v=HD), AX, ALU.add).then_inc(vector_done, vec.one("y_var"))
                eng.wait_ge(scalar_done, act.at("y_r", i))
                for c in range(NP):
                    yc = m.mem[:, :, 0:P].rearrange("p (c n) t -> p c n t", c=NP)[:, c, bass.ds(i * GROUP, GROUP), :]
                    ins_ = eng.tensor_tensor(m.work2[:, 512 * c:512 * c + 512].rearrange("p (n e v) -> p n e v", n=GROUP, e=2),
                                             yc.rearrange("p n (e v) -> p n e v", e=2),
                                             bc(st[:, 8 * c:8 * c + 8].rearrange("p (n e) -> p n e", e=2).unsqueeze(3), [P, GROUP, 2, HD]), ALU.mult)
                ins_.then_inc(vector_done, vec.one("yn"))
                eng.wait_ge(tensor_done, pe.at("g1", i))
                eng.tensor_scalar(m.gu_x[:, :], m.ps[0:R, 5, :], m.bu1[:, 0:1], FLOOR, ALU.add, ALU.max).then_inc(vector_done, vec.one("g0"))
                eng.wait_ge(scalar_done, act.at("g_sig", i))
                eng.tensor_tensor(m.gu[0:R, :], m.gu_x[:, :], m.gu_e[:, :], ALU.mult).then_inc(vector_done, vec.one("gu"))
                eng.wait_ge(tensor_done, pe.at("gate", i))
                eng.tensor_scalar(m.gate[:, :], m.ps[:, 6, :], FLOOR, None, ALU.max).then_inc(vector_done, vec.one("s0"))
                eng.wait_ge(scalar_done, act.at("s_sig", i))
                eng.wait_ge(tensor_done, pe.at("proj", i))
                eng.tensor_tensor(m.gate[:, :], m.gate[:, :], m.ps[:, 7, :], ALU.mult).then_inc(vector_done, vec.one("gated"))
                eng.wait_ge(vector_done, vec.at("gated", i))
                eng.tensor_tensor(m.y1[:, :, :], m.gate[:, :].rearrange("p (n d) -> p n d", d=D), m.h_in[:, :, :], ALU.add).then_inc(vector_done, vec.one("y1"))
                eng.wait_ge(scalar_done, act.at("z_sq", i))
                eng.tensor_reduce(st[:, 32:36], w3, AX, ALU.add).then_inc(vector_done, vec.one("zvar"))
                eng.wait_ge(scalar_done, act.at("z_r", i))
                eng.tensor_tensor(m.xc[:, :, :], m.y1[:, :, :], bc(st[:, 32:36].unsqueeze(2), [P, GROUP, D]), ALU.mult).then_inc(vector_done, vec.one("z"))
                for f in range(NF):
                    eng.wait_ge(scalar_done, act.at(f"a{f}_e", i))
                    eng.tensor_tensor(m.hid[:, f, :], m.hid_e[:, f % 2, :], m.ps[:, 2 * (f % 2) + 1, :], ALU.mult).then_inc(vector_done, vec.one(f"a{f}"))
                eng.wait_ge(tensor_done, pe.at("ff2", i))
                eng.tensor_tensor(m.y1[:, :, :], m.y1[:, :, :], bank3(4), ALU.add).then_inc(vector_done, vec.one("y2"))
                eng.wait_ge(vector_done, vec.at("y2", i))
                eng.tensor_tensor(m.y1[:, :, :], m.y1[:, :, :], mod_row(0, 2), ALU.mult).then_inc(vector_done, vec.one("y2g"))
                eng.wait_ge(vector_done, vec.at("y2g", i))
                eng.tensor_tensor(xs, xs, m.y1[:, :, :], ALU.add).then_inc(vector_done, vec.one("x1"))
                eng.wait_ge(vector_done, vec.at("x1", i))
                norm("n1", xs, 48)
                eng.wait_ge(tensor_done, pe.at("w2", i))
                eng.tensor_tensor(m.y1[:, :, :], bank3(4), mod_row(0, 5), ALU.mult).then_inc(vector_done, vec.one("x2m"))
                eng.wait_ge(vector_done, vec.at("x2m", i))
                eng.tensor_tensor(xs, xs, m.y1[:, :, :], ALU.add).then_inc(vector_done, vec.one("x2"))
                eng.wait_ge(vector_done, vec.at("x2", i))
                norm("n2", xs, 56)

                def weights(n):
                    sc = m.sc[:, n % 2]
                    eng.wait_ge(tensor_done, pe.at(f"sc{n}", i))
                    if n == 1:
                        eng.wait_ge(vector_done, vec.at("band", i))
                    band = bc(m.band[:, :, :].rearrange("p (a j) k -> p a (j k)", a=2).unsqueeze(2), [P, 2, NG, 4 * WIN])
                    eng.tensor_tensor(sc.rearrange("p (a g j) k -> p a g (j k)", a=2, j=2),
                                      m.ps[:, 0:2, :].rearrange("p a (g k) -> p a g k", g=NG), band, ALU.add).then_inc(vector_done, vec.one(f"sc{n}"))
                    eng.wait_ge(vector_done, vec.at(f"sc{n}", i))
                    eng.tensor_reduce(m.mx[:, :], sc, AX, ALU.max).then_inc(vector_done, vec.one(f"mx{n}"))
                    if n == 0:
                        eng.tensor_copy(m.band[:, 0, :], m.band[:, 1, :]).then_inc(vector_done, vec.one("band"))
                    eng.wait_ge(vector_done, vec.at(f"mx{n}", i))
                    eng.tensor_tensor(sc, sc, bc(m.mx[:, :].unsqueeze(2), [P, 16, 64]), ALU.subtract).then_inc(vector_done, vec.one(f"sub{n}"))
                    eng.wait_ge(scalar_done, act.at(f"exp{n}", i))
                    eng.tensor_reduce(m.sm[:, :], sc, AX, ALU.add).then_inc(vector_done, vec.one(f"sum{n}"))
                    eng.wait_ge(vector_done, vec.at(f"sum{n}", i))
                    eng.reciprocal(m.sm[:, :], m.sm[:, :]).then_inc(vector_done, vec.one(f"rec{n}"))
                    eng.wait_ge(vector_done, vec.at(f"rec{n}", i))
                    eng.tensor_tensor(sc, sc, bc(m.sm[:, :].unsqueeze(2), [P, 16, 64]), ALU.mult).then_inc(vector_done, vec.one(f"prob{n}"))

                def fold(n):
                    eng.wait_ge(tensor_done, pe.at(f"pv{n}", i))
                    own = bc(m.head_of[:, :].unsqueeze(1).unsqueeze(3), [P, NW, NH1, WIN])
                    w4 = m.work[:, :].rearrange("p (j h q) -> p j h q", h=NH1, q=WIN)
                    eng.tensor_tensor(w4, m.ps[:, 4:8, :].rearrange("p j (h q) -> p j h q", q=WIN), own, ALU.mult).then_inc(vector_done, vec.one(f"pick{n}"))
                    eng.wait_ge(vector_done, vec.at(f"pick{n}", i))
                    eng.tensor_reduce(m.ao[:, P * n:P * n + P].rearrange("p (j q) -> p j q", q=WIN),
                                      m.work[:, :].rearrange("p (j h q) -> p j q h", h=NH1, q=WIN), AX, ALU.add).then_inc(vector_done, vec.one(f"fold{n}"))

                weights(0)
                for n in range(1, GROUP):
                    weights(n)
                    fold(n - 1)
                eng.wait_ge(vector_done, vec.at(f"fold{GROUP - 2}", i))
                fold(GROUP - 1)
                eng.tensor_copy(m.hc[:, 0:WIN], m.hc[:, GT:GT + WIN])
                eng.tensor_copy(m.kc[:, 0:WIN], m.kc[:, GT:GT + WIN]).then_inc(vector_done, vec.one("hist"))
                eng.wait_ge(tensor_done, pe.at("wo", i))
                eng.tensor_tensor(m.y1[:, :, :], bank3(4), mod_row(1, 2), ALU.mult).then_inc(vector_done, vec.one("x3m"))
                eng.wait_ge(vector_done, vec.at("x3m", i))
                eng.tensor_tensor(xs, xs, m.y1[:, :, :], ALU.add).then_inc(vector_done, vec.one("x3"))
                eng.wait_ge(vector_done, vec.at("x3", i))
                norm("n3", xs, 64)
                eng.wait_ge(vector_done, vec.at("n3_nrm", i))
                eng.tensor_tensor(m.y1[:, :, :], m.xc[:, :, :], mod_row(1, 4), ALU.mult).then_inc(vector_done, vec.one("h3m"))
                eng.wait_ge(vector_done, vec.at("h3m", i))
                eng.tensor_tensor(m.y1[:, :, :], m.y1[:, :, :], mod_row(1, 3), ALU.add).then_inc(vector_done, vec.one("h3"))
                eng.wait_ge(vector_done, vec.at("h3", i))
                norm("n4", m.y1[:, :, :], 72)
                eng.wait_ge(tensor_done, pe.at("fc2", i))
                eng.scalar_tensor_tensor(m.y1[:, :, :].rearrange(flat), m.ps[:, 4, :], 0.5, m.y1[:, :, :].rearrange(flat), ALU.mult, ALU.add).then_inc(vector_done, vec.one("zh"))
                eng.wait_ge(vector_done, vec.at("zh", i))
                eng.tensor_tensor(m.y1[:, :, :], m.y1[:, :, :], mod_row(1, 5), ALU.mult).then_inc(vector_done, vec.one("zg"))
                eng.wait_ge(vector_done, vec.at("zg", i))
                eng.tensor_tensor(group(m.x, i), xs, m.y1[:, :, :], ALU.add).then_inc(vector_done, vec.one("x4"))


def program(nc, ins, out):
    with ExitStack() as ctx:
        m, a = Tensors(), Tensors()
        allocate(nc, ctx, m)
        a.ins = ins
        setup_phase(nc, m, a)
        spike_phase(nc, m)
        delta_phase(nc, m)
        post_phase(nc, m, ins, out)


_COLUMNS = {"L0_attn_alpha_spike", "L0_attn_beta_spike", "L0_attn_head_norm_w", "L0_ffn_b1", "L1_ffn_fc1_bias"}
_TRANSPOSED = {"L1_attn_wq", "L1_attn_wk", "L1_attn_wv", "L1_attn_wo"}


def kernel(**inputs):
    import numpy as np
    import concourse.bacc as bacc
    from concourse import mybir as mb
    from concourse.bass_utils import run_bass_kernel_spmd as run

    nc = bacc.Bacc("TRN2", target_bir_lowering=False, num_devices=1)
    arrays, ins = {}, {}
    for name in inputs:
        v = np.asarray(inputs[name])
        if name in _COLUMNS:
            v = v.reshape(-1, 128).T
        elif name in _TRANSPOSED:
            v = v.T
        v = np.ascontiguousarray(v)
        arrays[f"in_{name}"] = v
        ins[name] = nc.dram_tensor(f"in_{name}", v.shape, mb.dt.from_np(v.dtype), kind="ExternalInput").ap()
    out = nc.dram_tensor("out", (1, 2048, 128), mb.dt.float32, kind="ExternalOutput").ap()
    program(nc, ins, out)
    r = run(nc, [arrays], core_ids=[0])
    return r.results[0]["out"]
```
